# Optimizing a Trainium2 kernel written in Bass

```python
import numpy as np
import jax
import jax.numpy as jnp

def _softmax(x, axis=-1):
    return jax.nn.softmax(x, axis=axis)

def _gelu(x):
    return jax.nn.gelu(x, approximate=True)

def _silu(x):
    return jax.nn.silu(x)

def _sigmoid(x):
    return jax.nn.sigmoid(x)

def _layernorm(x, axis=-1, eps=1e-05):
    m = jnp.mean(x, axis=axis, keepdims=True)
    v = jnp.var(x, axis=axis, keepdims=True)
    return (x - m) / jnp.sqrt(v + eps)

def _scatter_add(tgt, idx, src, axis=0):
    return tgt.at[idx].add(src)

def _segment_sum(src, seg, n):
    return jax.ops.segment_sum(src, seg, n)
kernel_name = 'mk_gnn_preln_d2_gnn_r32_25fcbc'

def setup_inputs(seed: int=0):
    np.random.seed(seed)
    _w = jnp.asarray

    def _rec_inputs():
        import jax
        import jax.numpy as jnp
        _gk = jax.random.key(seed)
        x = 0.0001963 + 1 * jax.random.normal(jax.random.fold_in(_gk, 1), (3125, 256), jnp.float32)
        _s = jax.random.randint(jax.random.fold_in(_gk, 2), (25000,), 0, 3125, jnp.int32)
        _d = jax.random.randint(jax.random.fold_in(_gk, 3), (25000,), 0, 3125, jnp.int32)
        _loop = jnp.arange(3125, dtype=jnp.int32)
        src = jnp.concatenate([_s, _d, _loop])
        dst = jnp.concatenate([_d, _s, _loop])
        _o = jnp.argsort(dst, stable=True)
        src = src[_o]
        dst = dst[_o]
        return (x, src, dst)
    x, src, dst = _rec_inputs()

    def _L0_gnn_setup():
        import jax, jax.numpy as jnp
        import numpy as np
        N_NODES = 3125
        N_EDGES = 10000
        DIM = 256

        def _graph_conv(src, dst, h, W, b):
            ones = jnp.ones((src.shape[0],), dtype=h.dtype)
            out_deg = jnp.clip(jax.ops.segment_sum(ones, src, num_segments=N_NODES), 1.0)
            in_deg = jnp.clip(jax.ops.segment_sum(ones, dst, num_segments=N_NODES), 1.0)
            h = h * (out_deg ** (-0.5))[:, None]
            agg = jax.ops.segment_sum(h[src], dst, num_segments=N_NODES)
            agg = agg * (in_deg ** (-0.5))[:, None]
            return agg @ W + b
        key = jax.random.key(seed)
        ks = jax.random.split(key, 7)
        src = jax.random.randint(ks[0], (N_EDGES,), 0, N_NODES, dtype=jnp.int32)
        dst = jax.random.randint(ks[1], (N_EDGES,), 0, N_NODES, dtype=jnp.int32)
        node_feature = jax.random.normal(ks[2], (N_NODES, DIM), dtype=jnp.float32)
        s = 1.0 / np.sqrt(DIM)
        W1 = jax.random.normal(ks[3], (DIM, DIM), dtype=jnp.float32) * s
        b1 = jnp.zeros((DIM,), dtype=jnp.float32)
        W2 = jax.random.normal(ks[4], (DIM, DIM), dtype=jnp.float32) * s
        b2 = jnp.zeros((DIM,), dtype=jnp.float32)
        return {'src': src, 'dst': dst, 'node_feature': node_feature, 'W1': W1, 'b1': b1, 'W2': W2, 'b2': b2}
    _L0_gnn_all = _L0_gnn_setup()
    _L0_gnn_in = {k: v for k, v in _L0_gnn_all.items() if k in ('W1', 'b1', 'W2', 'b2')}
    del _L0_gnn_all

    def _L1_gnn_setup():
        import jax, jax.numpy as jnp
        import numpy as np
        N = 50000
        E = 15625
        CH = 256
        H1, C1 = (4, 64)
        H2, C2 = (8, 32)
        CONCAT = H1 * C1 + H2 * C2

        def _layer_norm(x, gamma, beta, eps=1e-05):
            mu = jnp.mean(x, axis=-1, keepdims=True)
            var = jnp.var(x, axis=-1, keepdims=True)
            return (x - mu) * jax.lax.rsqrt(var + eps) * gamma + beta

        def _gat_conv(x, src, dst, W, a_src, a_dst, bias, heads, out_ch, n_nodes):
            h = (x @ W).reshape(n_nodes, heads, out_ch)
            alpha_s = jnp.einsum('nhc,hc->nh', h, a_src)
            alpha_d = jnp.einsum('nhc,hc->nh', h, a_dst)
            e = jax.nn.leaky_relu(alpha_s[src] + alpha_d[dst], negative_slope=0.2)
            m = jax.ops.segment_max(e, dst, num_segments=n_nodes)
            ex = jnp.exp(e - m[dst])
            denom = jax.ops.segment_sum(ex, dst, num_segments=n_nodes)
            a = ex / (denom[dst] + 1e-16)
            msg = h[src] * a[:, :, None]
            out = jax.ops.segment_sum(msg, dst, num_segments=n_nodes)
            return out.reshape(n_nodes, heads * out_ch) + bias
        key = jax.random.key(seed)
        ks = jax.random.split(key, 16)
        s = 0.05
        x = jax.random.normal(ks[0], (N, CH), dtype=jnp.float32)
        edge_index = jax.random.randint(ks[1], (2, E), 0, N, dtype=jnp.int64)
        return {'x': x, 'edge_index': edge_index, 'gamma': jnp.ones((CH,), jnp.float32), 'beta': jnp.zeros((CH,), jnp.float32), 'W1': jax.random.normal(ks[2], (CH, H1 * C1), jnp.float32) * s, 'a_src1': jax.random.normal(ks[3], (H1, C1), jnp.float32) * s, 'a_dst1': jax.random.normal(ks[4], (H1, C1), jnp.float32) * s, 'b1': jnp.zeros((H1 * C1,), jnp.float32), 'W2': jax.random.normal(ks[5], (CH, H2 * C2), jnp.float32) * s, 'a_src2': jax.random.normal(ks[6], (H2, C2), jnp.float32) * s, 'a_dst2': jax.random.normal(ks[7], (H2, C2), jnp.float32) * s, 'b2': jnp.zeros((H2 * C2,), jnp.float32), 'Wu': jax.random.normal(ks[8], (CONCAT, CH), jnp.float32) * s, 'bu': jnp.zeros((CH,), jnp.float32)}
    _L1_gnn_all = _L1_gnn_setup()
    _L1_gnn_in = {k: v for k, v in _L1_gnn_all.items() if k in ('gamma', 'beta', 'W1', 'a_src1', 'a_dst1', 'b1', 'W2', 'a_src2', 'a_dst2', 'b2', 'Wu', 'bu')}
    del _L1_gnn_all
    return {'x': x, 'src': src, 'dst': dst, 'L0_gnn_W1': _L0_gnn_in['W1'], 'L0_gnn_b1': _L0_gnn_in['b1'], 'L0_gnn_W2': _L0_gnn_in['W2'], 'L0_gnn_b2': _L0_gnn_in['b2'], 'L1_gnn_gamma': _L1_gnn_in['gamma'], 'L1_gnn_beta': _L1_gnn_in['beta'], 'L1_gnn_W1': _L1_gnn_in['W1'], 'L1_gnn_a_src1': _L1_gnn_in['a_src1'], 'L1_gnn_a_dst1': _L1_gnn_in['a_dst1'], 'L1_gnn_b1': _L1_gnn_in['b1'], 'L1_gnn_W2': _L1_gnn_in['W2'], 'L1_gnn_a_src2': _L1_gnn_in['a_src2'], 'L1_gnn_a_dst2': _L1_gnn_in['a_dst2'], 'L1_gnn_b2': _L1_gnn_in['b2'], 'L1_gnn_Wu': _L1_gnn_in['Wu'], 'L1_gnn_bu': _L1_gnn_in['bu']}

def reference(x, src, dst, L0_gnn_W1, L0_gnn_b1, L0_gnn_W2, L0_gnn_b2, L1_gnn_gamma, L1_gnn_beta, L1_gnn_W1, L1_gnn_a_src1, L1_gnn_a_dst1, L1_gnn_b1, L1_gnn_W2, L1_gnn_a_src2, L1_gnn_a_dst2, L1_gnn_b2, L1_gnn_Wu, L1_gnn_bu):
    import jax
    import jax.numpy as jnp

    def _L0_gnn_ref(src, dst, node_feature, W1, b1, W2, b2):
        import jax, jax.numpy as jnp
        import numpy as np
        N_NODES = 3125
        N_EDGES = 10000
        DIM = 256

        def _graph_conv(src, dst, h, W, b):
            ones = jnp.ones((src.shape[0],), dtype=h.dtype)
            out_deg = jnp.clip(jax.ops.segment_sum(ones, src, num_segments=N_NODES), 1.0)
            in_deg = jnp.clip(jax.ops.segment_sum(ones, dst, num_segments=N_NODES), 1.0)
            h = h * (out_deg ** (-0.5))[:, None]
            agg = jax.ops.segment_sum(h[src], dst, num_segments=N_NODES)
            agg = agg * (in_deg ** (-0.5))[:, None]
            return agg @ W + b
        h = _graph_conv(src, dst, node_feature, W1, b1)
        h = _graph_conv(src, dst, jax.nn.relu(h), W2, b2)
        return jax.nn.relu(h)

    def _L1_gnn_ref(x, edge_index, gamma, beta, W1, a_src1, a_dst1, b1, W2, a_src2, a_dst2, b2, Wu, bu):
        import jax, jax.numpy as jnp
        import numpy as np
        N = 50000
        E = 15625
        CH = 256
        H1, C1 = (4, 64)
        H2, C2 = (8, 32)
        CONCAT = H1 * C1 + H2 * C2

        def _layer_norm(x, gamma, beta, eps=1e-05):
            mu = jnp.mean(x, axis=-1, keepdims=True)
            var = jnp.var(x, axis=-1, keepdims=True)
            return (x - mu) * jax.lax.rsqrt(var + eps) * gamma + beta

        def _gat_conv(x, src, dst, W, a_src, a_dst, bias, heads, out_ch, n_nodes):
            h = (x @ W).reshape(n_nodes, heads, out_ch)
            alpha_s = jnp.einsum('nhc,hc->nh', h, a_src)
            alpha_d = jnp.einsum('nhc,hc->nh', h, a_dst)
            e = jax.nn.leaky_relu(alpha_s[src] + alpha_d[dst], negative_slope=0.2)
            m = jax.ops.segment_max(e, dst, num_segments=n_nodes)
            ex = jnp.exp(e - m[dst])
            denom = jax.ops.segment_sum(ex, dst, num_segments=n_nodes)
            a = ex / (denom[dst] + 1e-16)
            msg = h[src] * a[:, :, None]
            out = jax.ops.segment_sum(msg, dst, num_segments=n_nodes)
            return out.reshape(n_nodes, heads * out_ch) + bias
        n = x.shape[0]
        loop = jnp.arange(n, dtype=edge_index.dtype)
        src = jnp.concatenate([edge_index[0], loop])
        dst = jnp.concatenate([edge_index[1], loop])
        residual = x
        x_norm = _layer_norm(x, gamma, beta)
        out1 = _gat_conv(x_norm, src, dst, W1, a_src1, a_dst1, b1, H1, C1, n)
        out2 = _gat_conv(x_norm, src, dst, W2, a_src2, a_dst2, b2, H2, C2, n)
        x_cat = jax.nn.elu(jnp.concatenate([out1, out2], axis=-1))
        unified = x_cat @ Wu + bu
        return residual + unified
    edge_index = jnp.stack([src, dst])
    h = jnp.maximum(_layernorm(x, axis=-1), 0.0)
    x = x + _L0_gnn_ref(src, dst, h, L0_gnn_W1, L0_gnn_b1, L0_gnn_W2, L0_gnn_b2)
    h = jnp.maximum(_layernorm(x, axis=-1), 0.0)
    x = x + _L1_gnn_ref(h, edge_index, L1_gnn_gamma, L1_gnn_beta, L1_gnn_W1, L1_gnn_a_src1, L1_gnn_a_dst1, L1_gnn_b1, L1_gnn_W2, L1_gnn_a_src2, L1_gnn_a_dst2, L1_gnn_b2, L1_gnn_Wu, L1_gnn_bu)
    return x

_drawn_inputs = setup_inputs


def setup_inputs(seed=0):
    import zlib

    import numpy as np

    out = dict(_drawn_inputs(seed))
    spreads = {'L0_gnn_b1': (0.0, 0.1),
     'L0_gnn_b2': (0.0, 0.1),
     'L1_gnn_gamma': (1.0, 0.2),
     'L1_gnn_beta': (0.0, 0.1),
     'L1_gnn_b1': (0.0, 0.1),
     'L1_gnn_b2': (0.0, 0.1),
     'L1_gnn_bu': (0.0, 0.1)}
    factors = {'L1_gnn_a_src1': 2.817,
     'L1_gnn_a_dst1': 7.07,
     'L1_gnn_a_src2': 3.093,
     'L1_gnn_a_dst2': 8.0}
    for name, (base, spread) in spreads.items():
        noise = np.random.default_rng([zlib.crc32(name.encode()), seed]).standard_normal(out[name].shape)
        drawn = base * np.exp(spread * noise) if base else spread * noise
        out[name] = jnp.asarray(drawn.astype(out[name].dtype))
    for name, factor in factors.items():
        out[name] = (out[name] * factor).astype(out[name].dtype)
    return out
```

```python
import concourse.bass as bass
from concourse import mybir
from contextlib import ExitStack

F32 = mybir.dt.float32
BF16 = mybir.dt.bfloat16
I32 = mybir.dt.int32
ALU = mybir.AluOpType
ACT = mybir.ActivationFunctionType
AX = mybir.AxisListType

N = 3125
E = 53125
D = 256
BP = 125
BLOCKS = N // BP
P = 128
TILES = 18
HALF = TILES // 2
CAP = P * TILES
UNROLL = 5
SLOTS = 5
AHEAD = 4
PARTS = 9
MAXCH = -(-(BLOCKS + E // CAP) // UNROLL) * UNROLL
NCH = MAXCH + AHEAD
EC = E // BP
H1, C1, H2, C2 = 4, 64, 8, 32
HW = 32
HEADS = 2 * D // HW
ROW3 = 2 * D + HEADS
SIDE = HEADS + D
WC = 2 * D + 2 * HEADS
EPS = 1e-5
BIG = 1e30
ROUND = 1.5 * 2 ** 23


class Chain:

    def __init__(self, eng, sem, base=0):
        self.eng, self.sem, self.base, self.n = eng, sem, base, 0

    def step(self, ins):
        self.n += 1
        ins.then_inc(self.sem, 1)
        self.eng.wait_ge(self.sem, self.base + self.n)


def gnn(nc, x, src, dst, gw1, gb1, gw2, gb2, gamma, beta, aw1, as1, ad1, ab1, aw2, as2, ad2, ab2,
        wu, bu, out):
    ctx = ExitStack()
    with ctx:
        def sb(name, shape, dt=F32):
            return ctx.enter_context(nc.sbuf_tensor(name, shape, dt))

        def sem(name):
            return ctx.enter_context(nc.semaphore(name))

        def dram(name, shape, dt=F32):
            return nc.dram_tensor(name, shape, dt, kind="Internal").ap()

        src_lin = dram("src_lin", [E + CAP], I32)
        dst_lin = dram("dst_lin", [E + CAP + 2], I32)
        plan_d = dram("plan_d", [NCH, 2])
        sout_d = dram("sout_d", [BLOCKS, BP])
        table = [dram("table1", [N, D]), dram("table2", [N, D]), dram("table3", [N, ROW3])]
        side_d = dram("side", [N, SIDE])

        ident = sb("ident", [P, P])
        ones = sb("ones", [P, P])
        iota_v = sb("iota_v", [P, BP])
        ring = sb("ring", [P, SLOTS, HALF * ROW3])
        hot = sb("hot", [P, SLOTS, HALF, BP])
        idx = sb("idx", [P, UNROLL, TILES], I32)
        dwin = sb("dwin", [P, UNROLL, TILES + 2], I32)
        cb = sb("cb", [P, UNROLL, 2])
        sout_c = sb("sout_c", [P, UNROLL])
        wg = sb("wg", [P, 2, 2, D])
        bg = sb("bg", [P, 2, D])
        wcat = sb("wcat", [P, 2, WC])
        wu_s = sb("wu_s", [P, 4, D])
        gam = sb("gam", [P, D])
        bet = sb("bet", [P, D])
        bu_s = sb("bu_s", [P, D])
        ab = sb("ab", [P, 2 * D])
        dwf = sb("dwf", [P, TILES + 2])
        pb = [ctx.enter_context(nc.psum_tensor(f"bank{i}", [P, 512], F32)) for i in range(8)]

        s_const = sem("s_const")
        s_ld = sem("s_ld")
        s_x = sem("s_x")
        s_w = sem("s_w")
        s_pad = sem("s_pad")
        s_dve = sem("s_dve")
        s_h1 = sem("s_h1")
        s_hm = sem("s_hm")
        s_cnt = sem("s_cnt")
        s_sc = sem("s_sc")
        s_sq = sem("s_sq")
        s_rt = sem("s_rt")
        s_t1 = sem("s_t1")
        s_plan = sem("s_plan")
        s_pd = sem("s_pd")
        s_go = [sem(f"s_go{i}") for i in range(3)]
        s_st1 = sem("s_st1")
        s_gate = sem("s_gate")

        NOWHERE = 1 << 20
        plan_i = sb("plan_i", [1, 2, NCH], I32)
        niter_i = sb("niter_i", [1, 2], I32)

        class Phase:
            def __init__(self, i):
                self.i = i
                self.rec = [sem(f"rec{i}_{u}") for u in range(UNROLL)]
                self.rows = [sem(f"rows{i}_{s}") for s in range(SLOTS)]
                self.hot = sem(f"hot{i}")
                self.used = sem(f"used{i}")
                self.acc = sem(f"acc{i}")
                self.z = sem(f"z{i}")
                self.t = sem(f"t{i}")
                self.fin = sem(f"fin{i}")
                self.st = sem(f"st{i}")
                self.free = sem(f"free{i}")
                self.dve = sem(f"dve{i}")
                self.hc = sem(f"hc{i}")
                self.dg = sem(f"dg{i}")
                self.sq = sem(f"sq{i}")
                self.rt = sem(f"rt{i}")

        ph = [Phase(i) for i in range(3)]
        NREC = [4, 4, 5]

        phase_a = ExitStack()
        def sa(name, shape, dt=F32):
            return phase_a.enter_context(nc.sbuf_tensor(name, shape, dt))
        with phase_a:
            src_i = sa("src_i", [BP, EC], I32)
            dst_i = sa("dst_i", [BP, EC], I32)
            src_f = sa("src_f", [BP, EC])
            low_f = sa("low_f", [BP, EC])
            low_b = sa("low_b", [BP, EC], BF16)
            high_b = sa("high_b", [BP, EC], BF16)
            dst_f = sa("dst_f", [BP, EC])
            junk = sa("junk", [BP, EC])
            x_all = ring[0:BP, :, :].rearrange("p s n -> p (s n)")[:, 0:BLOCKS * D].rearrange(
                "p (b d) -> p b d", d=D)
            PC = EC // 25
            iota_r = sa("iota_r", [BP, BP, PC], BF16)
            oh_lo = sa("oh_lo", [BP, 2, BP, PC], BF16)
            oh_hi = sa("oh_hi", [BP, 2, BLOCKS, PC], BF16)
            stats = sa("stats", [BP, BLOCKS, 6])
            mv = sa("mv", [BP, BLOCKS, 2])
            rstd = sa("rstd", [BP, BLOCKS])
            sout = sa("sout", [BP, BLOCKS])
            sc1 = sa("sc1", [BP, BLOCKS])
            nb1 = sa("nb1", [BP, BLOCKS])
            cnt = sa("cnt", [BP, BLOCKS])
            pad_i = sa("pad_i", [1, 2, CAP + 2], I32)
            row = sa("row", [1, 8, BLOCKS + 1])
            grid = sa("grid", [1, NCH * BLOCKS])
            iotas = sa("iotas", [1, NCH * BLOCKS])
            pl = sa("pl", [1, 4, NCH])
            plan_f = sa("plan_f", [1, NCH, 2])
            arow = sa("arow", [P, 2, 2 * D])
            prod = hot[:].rearrange("p s j v -> p (s j v)")[:, 0:4 * D].rearrange("p (s n) -> p s n", s=2)

            with nc.Block() as block:
                @block.sync
                def _(sp):
                    sp.dma_start(src_i[:], src.rearrange("(p c) -> p c", p=BP)).then_inc(s_ld, 16)
                    sp.dma_start(dst_i[:], dst.rearrange("(p c) -> p c", p=BP)).then_inc(s_ld, 16)
                    sp.dma_start(x_all, x.rearrange("(b p) d -> p b d", p=BP)).then_inc(s_x, 16)
                    sp.dma_start(src_lin[0:E].rearrange("(p c) -> p c", p=BP),
                                 src.rearrange("(p c) -> p c", p=BP)).then_inc(s_pad, 16)
                    sp.dma_start(dst_lin[1:1 + E].rearrange("(p c) -> p c", p=BP),
                                 dst.rearrange("(p c) -> p c", p=BP)).then_inc(s_pad, 16)
                    sp.wait_ge(s_const, 1)
                    sp.dma_start(src_lin[E:E + CAP].unsqueeze(0), pad_i[:, 0, 0:CAP]).then_inc(s_pad, 16)
                    sp.dma_start(dst_lin[1 + E:E + CAP + 2].unsqueeze(0),
                                 pad_i[:, 1, 0:CAP + 1]).then_inc(s_pad, 16)
                    sp.dma_start(dst_lin[0:1].unsqueeze(0), pad_i[:, 1, 0:1]).then_inc(s_pad, 16)
                    for w, l in ((gw1, 0), (gw2, 1)):
                        sp.dma_start(wg[:, l], w.rearrange("(c p) n -> p c n", p=P)).then_inc(s_w, 16)
                    sp.dma_start(wcat[:, :, 0:D], aw1.rearrange("(c p) n -> p c n", p=P)).then_inc(s_w, 16)
                    sp.dma_start(wcat[:, :, D:2 * D], aw2.rearrange("(c p) n -> p c n", p=P)).then_inc(s_w, 16)
                    sp.dma_start(wu_s[:], wu.rearrange("(c p) n -> p c n", p=P)).then_inc(s_w, 16)
                    for to, of in ((bg[:, 0], gb1), (bg[:, 1], gb2), (gam[:], gamma), (bet[:], beta),
                                   (bu_s[:], bu), (ab[:, 0:D], ab1), (ab[:, D:2 * D], ab2),
                                   (arow[:, 0, 0:D], as1.rearrange("h c -> (h c)")),
                                   (arow[:, 0, D:2 * D], as2.rearrange("h c -> (h c)")),
                                   (arow[:, 1, 0:D], ad1.rearrange("h c -> (h c)")),
                                   (arow[:, 1, D:2 * D], ad2.rearrange("h c -> (h c)"))):
                        sp.dma_start(to, of.partition_broadcast(P)).then_inc(s_w, 16)
                    sp.wait_ge(s_plan, 1)
                    sp.dma_start(plan_d.unsqueeze(0), plan_f[:]).then_inc(s_pd, 16)
                    sp.wait_ge(s_sc, 1)
                    with nc.allow_non_contiguous_dma(reason="a scale per node, once"):
                        sp.dma_start(sout_d.rearrange("b p -> p b"), sout[:]).then_inc(s_pd, 16)
                    for b in range(BLOCKS):
                        sp.wait_ge(s_t1, b + 1)
                        sp.dma_start(table[0][b * BP:(b + 1) * BP, :], x_all[:, b, :]).then_inc(s_st1, 16)
                    sp.wait_ge(s_st1, 16 * BLOCKS)
                    sp.wait_ge(s_pd, 32)
                    sp.wait_ge(s_pad, 16 * 5)
                    sp.sem_inc(s_go[0], 1)

                @block.gpsimd
                def _(pool):
                    pool.memset(pad_i[:, 0, :], 0)
                    pool.memset(pad_i[:, 1, :], NOWHERE).then_inc(s_const, 1)
                    pool.iota(iota_r[:], [[1, BP], [0, PC]], base=0, channel_multiplier=0,
                              allow_small_or_imprecise_dtypes=True).then_inc(s_const, 1)
                    pool.iota(iotas[:], [[1, NCH * BLOCKS]], base=0, channel_multiplier=0,
                              allow_small_or_imprecise_dtypes=True)
                    pool.iota(iota_v[:], [[1, BP]], base=0, channel_multiplier=0,
                              allow_small_or_imprecise_dtypes=True)
                    pool.memset(ones[:], 1.0)
                    pool.memset(ident[:], 0.0).then_inc(s_const, 1)
                    pool.wait_ge(s_const, 3)
                    pool.affine_select(ident[:], ident[:], pattern=[[-1, P]], compare_op=ALU.not_equal,
                                       fill=1.0, base=0, channel_multiplier=1).then_inc(s_const, 1)

                @block.vector
                def _(dve):
                    ch = Chain(dve, s_dve)
                    dve.wait_ge(s_ld, 32)
                    ch.step(dve.tensor_copy(src_f[:], src_i[:]))
                    ch.step(dve.tensor_scalar(low_f[:], src_f[:], -float(BP // 2), 1.0 / BP, ALU.add, ALU.mult))
                    ch.step(dve.tensor_scalar(low_f[:], low_f[:], ROUND, None, ALU.add))
                    ch.step(dve.tensor_scalar(low_f[:], low_f[:], -ROUND, None, ALU.add))
                    ch.step(dve.tensor_copy(high_b[:], low_f[:]))
                    ch.step(dve.scalar_tensor_tensor(low_b[:], low_f[:], -float(BP), src_f[:], ALU.mult, ALU.add))
                    dve.wait_ge(s_const, 4)
                    for c in range(25):
                        cs = slice(c * PC, (c + 1) * PC)
                        if c >= 2:
                            dve.wait_ge(s_hm, c - 1)
                        dve.tensor_tensor(oh_lo[:, c % 2], iota_r[:],
                                          low_b[:, cs].unsqueeze(1).to_broadcast([BP, BP, PC]),
                                          ALU.is_equal)
                        dve.tensor_tensor(oh_hi[:, c % 2], iota_r[:, 0:BLOCKS],
                                          high_b[:, cs].unsqueeze(1).to_broadcast([BP, BLOCKS, PC]),
                                          ALU.is_equal).then_inc(s_h1, 1)
                    dve.wait_ge(s_x, 16)
                    for b in range(BLOCKS):
                        last = dve.bn_stats(stats[:, b], x_all[:, b])
                    ch.step(last)
                    for b in range(BLOCKS):
                        last = dve.bn_aggr(mv[:, b], stats[:, b])
                    ch.step(last)
                    dve.tensor_scalar(rstd[:], mv[:, :, 1], EPS, None, ALU.add).then_inc(s_sq, 1)
                    dve.wait_ge(s_hm, 25)
                    dve.tensor_scalar(sout[:], pb[0][0:BP, 0:BLOCKS], 1.0, None, ALU.max).then_inc(s_sq, 1)
                    dve.wait_ge(s_rt, 2)
                    ch.step(dve.reciprocal(rstd[:], rstd[:]))
                    ch.step(dve.reciprocal(sout[:], sout[:]))
                    ch.step(dve.tensor_tensor(sc1[:], rstd[:], sout[:], ALU.mult))
                    dve.scalar_tensor_tensor(nb1[:], mv[:, :, 0], -1.0, sc1[:], ALU.mult,
                                             ALU.mult).then_inc(s_sc, 1)
                    ch.step(dve.tensor_copy(dst_f[:], dst_i[:]))
                    for b in range(1, BLOCKS):
                        ch.step(dve.scalar_tensor_tensor(junk[:], dst_f[:], float(b * BP),
                                                         ones[0:BP, 0:1].to_broadcast([BP, EC]), ALU.is_lt,
                                                         ALU.mult, accum_out=cnt[:, b - 1:b]))
                    dve.sem_inc(s_cnt, 1)
                    dve.wait_ge(s_cnt, 2)
                    st, ln, nch, cum, off = (row[:, i, :] for i in range(5))
                    onerow = row[:, 5, 0:BLOCKS]
                    dve.wait_ge(s_const, 4)
                    dve.memset(onerow, 1.0)
                    dve.memset(st[:, 0:1], 0.0)
                    dve.memset(st[:, BLOCKS:BLOCKS + 1], float(E))
                    ch.step(dve.tensor_copy(st[:, 1:BLOCKS], pb[1][0:1, 0:BLOCKS - 1]))
                    ch.step(dve.tensor_tensor(ln[:, 0:BLOCKS], st[:, 1:BLOCKS + 1], st[:, 0:BLOCKS],
                                              ALU.subtract))
                    M = E // CAP
                    caps = grid[:, 0:M]
                    ch.step(dve.tensor_scalar(caps, iotas[:, 1:1 + M], float(CAP), None, ALU.mult))
                    g2 = grid[:, M:M + BLOCKS * M].rearrange("p (b m) -> p b m", m=M)
                    ch.step(dve.tensor_tensor(g2, ln[:, 0:BLOCKS].unsqueeze(2).to_broadcast([1, BLOCKS, M]),
                                              caps.unsqueeze(1).to_broadcast([1, BLOCKS, M]), ALU.is_gt))
                    ch.step(dve.tensor_reduce(nch[:, 0:BLOCKS], g2, AX.X, ALU.add))
                    ch.step(dve.tensor_scalar(nch[:, 0:BLOCKS], nch[:, 0:BLOCKS], 1.0, None, ALU.add))
                    ch.step(dve.tensor_tensor_scan(cum[:, 0:BLOCKS], onerow, nch[:, 0:BLOCKS], 0.0,
                                                   ALU.mult, ALU.add))
                    gk = grid[:, 0:NCH * (BLOCKS - 1)].rearrange("p (k b) -> p k b", k=NCH)
                    kk = iotas[:, 0:NCH]
                    ch.step(dve.tensor_tensor(gk, kk.unsqueeze(2).to_broadcast([1, NCH, BLOCKS - 1]),
                                              cum[:, 0:BLOCKS - 1].unsqueeze(1).to_broadcast([1, NCH, BLOCKS - 1]),
                                              ALU.is_ge))
                    blk = pl[:, 0, :]
                    ch.step(dve.tensor_reduce(blk, gk, AX.X, ALU.add))
                    ch.step(dve.tensor_tensor(off[:, 0:BLOCKS], nch[:, 0:BLOCKS], cum[:, 0:BLOCKS], ALU.subtract))
                    ch.step(dve.scalar_tensor_tensor(off[:, 0:BLOCKS], off[:, 0:BLOCKS], float(CAP),
                                                     st[:, 0:BLOCKS], ALU.mult, ALU.add))
                    gb = grid[:, 0:NCH * BLOCKS].rearrange("p (k b) -> p k b", k=NCH)
                    ch.step(dve.tensor_tensor(gb, blk.unsqueeze(2).to_broadcast([1, NCH, BLOCKS]),
                                              iotas[:, 0:BLOCKS].unsqueeze(1).to_broadcast([1, NCH, BLOCKS]),
                                              ALU.is_equal))
                    ch.step(dve.tensor_tensor(gb, gb, off[:, 0:BLOCKS].unsqueeze(1).to_broadcast([1, NCH, BLOCKS]),
                                              ALU.mult))
                    base = pl[:, 1, :]
                    ch.step(dve.tensor_reduce(base, gb, AX.X, ALU.add))
                    ch.step(dve.scalar_tensor_tensor(base, kk, float(CAP), base, ALU.mult, ALU.add))
                    ch.step(dve.tensor_scalar(base, base, float(E), None, ALU.min))
                    goes, first = plan_f[:, :, 0], plan_f[:, :, 1]
                    ch.step(dve.memset(goes, 0.0))
                    ch.step(dve.tensor_tensor(goes[:, 1:NCH], blk[:, 1:NCH], blk[:, 0:NCH - 1], ALU.is_equal))
                    ch.step(dve.tensor_scalar(first, blk, float(BP), None, ALU.mult))
                    ch.step(dve.tensor_copy(plan_i[:, 0, :], base))
                    ch.step(dve.tensor_copy(plan_i[:, 1, :], first))
                    T = MAXCH // UNROLL
                    g5 = pl[:, 2, 0:T]
                    ch.step(dve.tensor_scalar(g5, iotas[:, 0:T], float(UNROLL), cum[:, BLOCKS - 1:BLOCKS],
                                              ALU.mult, ALU.is_lt))
                    ch.step(dve.tensor_reduce(pl[:, 3, 0:1], g5, AX.X, ALU.add))
                    ch.step(dve.tensor_scalar(pl[:, 3, 1:2], pl[:, 3, 0:1], -1.0, None, ALU.add))
                    dve.tensor_copy(niter_i[:], pl[:, 3, 0:2]).then_inc(s_plan, 1)
                    dve.wait_ge(s_w, 16 * 16)
                    for c in range(2):
                        for s in range(2):
                            ch.step(dve.tensor_tensor(prod[:, s], wcat[:, c, 0:2 * D], arow[:, s], ALU.mult))
                            lo = 2 * D + s * HEADS
                            for twin in range(2):
                                dve.tensor_reduce(wcat[:, c, lo + twin:lo + 2 * H1:2],
                                                  prod[:, s, 0:D].rearrange("p (h k) -> p h k", k=C1),
                                                  AX.X, ALU.add)
                            ch.step(dve.tensor_reduce(wcat[:, c, lo + 2 * H1:lo + HEADS],
                                                      prod[:, s, D:2 * D].rearrange("p (h k) -> p h k", k=C2),
                                                      AX.X, ALU.add))

                @block.scalar
                def _(act):
                    for n, v in enumerate((rstd, sout)):
                        act.wait_ge(s_sq, n + 1)
                        act.activation(v[:], v[:], ACT.Sqrt).then_inc(s_rt, 1)
                    act.wait_ge(s_sc, 1)
                    for b in range(BLOCKS):
                        act.activation(x_all[:, b], x_all[:, b], ACT.Relu, bias=nb1[:, b:b + 1],
                                       scale=sc1[:, b:b + 1]).then_inc(s_t1, 1)

                @block.tensor
                def _(pe):
                    for c in range(25):
                        pe.wait_ge(s_h1, c + 1)
                        for j in range(PC):
                            last = pe.matmul(pb[0][0:BP, 0:BLOCKS], oh_lo[:, c % 2, :, j], oh_hi[:, c % 2, :, j],
                                             start=(c == 0 and j == 0), stop=(c == 24 and j == PC - 1))
                        last.then_inc(s_hm, 1)
                    pe.wait_ge(s_const, 4)
                    pe.wait_ge(s_cnt, 1)
                    pe.matmul(pb[1][0:1, 0:BLOCKS - 1], ones[0:BP, 0:1], cnt[:, 0:BLOCKS - 1],
                              start=True, stop=True).then_inc(s_cnt, 1)

        def load_record(sp, f, k, u, own):
            base = sp.value_load(plan_i[0:1, 0, bass.ds(k, 1)], min_val=0, max_val=E)
            node = sp.value_load(plan_i[0:1, 1, bass.ds(k, 1)], min_val=0, max_val=N - BP)
            sp.dma_start(idx[:, u], bass.AP(src_lin.tensor, base, [[TILES, P], [1, TILES]])).then_inc(f.rec[u], 16)
            sp.dma_start(dwin[:, u], bass.AP(dst_lin.tensor, base, [[TILES, P], [1, TILES + 2]])).then_inc(f.rec[u], 16)
            sp.dma_start(cb[:, u], bass.AP(plan_d.tensor, k * 2, [[0, P], [1, 2]])).then_inc(f.rec[u], 16)
            own(sp, f, node, u)

        def sp_phase(sp, f, own, store, nst):
            n = sp.value_load(niter_i[0:1, 0:1], min_val=UNROLL, max_val=MAXCH // UNROLL)
            for k in range(AHEAD):
                load_record(sp, f, k, k, own)
            sp.sem_inc(f.free, 1)
            with sp.Fori(0, n) as it:
                for u in range(UNROLL):
                    k = it * UNROLL + u
                    load_record(sp, f, k + AHEAD, (u + AHEAD) % UNROLL, own)
                    node = sp.value_load(plan_i[0:1, 1, bass.ds(k, 1)], min_val=0, max_val=N - BP)
                    sp.wait_ge(f.fin, k + 1)
                    store(sp, f, node)
                    sp.wait_ge(f.st, (k + 1) * 16 * nst)
                    sp.sem_inc(f.free, 1)
            for u in range(AHEAD):
                sp.wait_ge(f.rec[u], (n + 1) * 16 * NREC[f.i])
            if f.i < 2:
                sp.sem_inc(s_go[f.i + 1], 1)
            else:
                sp.sem_inc(s_gate, 1)

        def pool_phase(pool, f):
            width = D if f.i < 2 else ROW3
            n = pool.value_load(niter_i[0:1, 0:1], min_val=UNROLL, max_val=MAXCH // UNROLL)
            pool.wait_ge(s_go[f.i], 1)
            with pool.Fori(0, n) as it:
                for u in range(UNROLL):
                    pool.wait_ge(f.rec[u], (it + 1) * 16 * NREC[f.i])
                    for g in range(2):
                        q = 2 * u + g
                        pool.wait_ge(f.used, it * (2 * UNROLL) + q + 1)
                        pool.sem_inc(s_gate, 1)
                        for j in range(HALF):
                            t = g * HALF + j
                            pool.indirect_dma_start(
                                ring[:, q % SLOTS, j * width:(j + 1) * width], None, table[f.i],
                                bass.IndirectOffsetOnAxis(idx[:, u, t:t + 1], 0)).then_inc(f.rows[q % SLOTS], 16)

        def rows_wait(eng, f, it, q):
            eng.wait_ge(f.rows[q % SLOTS], (it * 2 + (q // SLOTS + 1)) * 16 * HALF)

        def make_hot(dve, f, it, u):
            for g in range(2):
                q = 2 * u + g
                dve.wait_ge(f.used, it * (2 * UNROLL) + q + 1)
                dve.tensor_tensor(hot[:, q % SLOTS], iota_v[:].unsqueeze(1).to_broadcast([P, HALF, BP]),
                                  dwf[:, 1 + g * HALF:1 + (g + 1) * HALF].unsqueeze(2).to_broadcast([P, HALF, BP]),
                                  ALU.is_equal).then_inc(f.hot, 1)

        phase_b = ExitStack()
        def sbb(name, shape, dt=F32):
            return phase_b.enter_context(nc.sbuf_tensor(name, shape, dt))
        with phase_b:
            xrow = sbb("xrow", [P, UNROLL, D])
            aggT = sbb("aggT", [P, 2, BP])
            deg = sbb("deg", [P, 1])
            s_in = sbb("s_in", [P, 1])
            part = sbb("part", [P, 2, BP])
            zt = sbb("zt", [P, D])
            row12 = sbb("row12", [P, D])
            x2 = sbb("x2", [P, D])
            h2 = sbb("h2", [P, D])
            xn = sbb("xn", [P, D])
            xnT = sbb("xnT", [P, 2, BP])
            row3 = sbb("row3", [P, ROW3])
            rowS = sbb("rowS", [P, SIDE])
            bst = sbb("bst", [P, 6])
            bmv = sbb("bmv", [P, 2])
            brs = sbb("brs", [P, 2])
            s_h2 = sem("s_h2")
            s_xn = sem("s_xn")
            s_xt = sem("s_xt")
            s_xc = sem("s_xc")
            s_H = sem("s_H")
            s_rs = sem("s_rs")

            LINKS = [5, 19]
            ROOTS = [1, 3]

            def inv_root(dve, ch, f, count, v, ins):
                ins.then_inc(f.sq, 1)
                dve.wait_ge(f.rt, count)
                ch.step(dve.reciprocal(v, v))

            def root(act, f, count, v):
                act.wait_ge(f.sq, count)
                act.activation(v, v, ACT.Sqrt).then_inc(f.rt, 1)

            def gcn_hot(dve, ch, f, it, u):
                dve.wait_ge(f.rec[u], (it + 1) * 16 * NREC[f.i])
                ch.step(dve.tensor_scalar(dwf[:], dwin[:, u], cb[:, u, 1:2], None, ALU.subtract))
                make_hot(dve, f, it, u)

            def gcn_counts(dve, f, it, u):
                dve.wait_ge(f.hot, it * (2 * UNROLL) + 2 * u + 2)
                for g in range(2):
                    last = dve.tensor_reduce(part[:, g], hot[:, (2 * u + g) % SLOTS].rearrange("p j v -> p v j"),
                                             AX.X, ALU.add)
                last.then_inc(f.hc, 1)

            def gcn_vector(dve, f, it, u):
                k = it * UNROLL + u
                ch = Chain(dve, f.dve, 1 + k * LINKS[f.i])
                ahead = (it + (u + 1) // UNROLL, (u + 1) % UNROLL)
                gcn_hot(dve, ch, f, *ahead)
                goes = cb[:, u, 0:1]
                dve.wait_ge(f.used, k * 2 + 2 + SLOTS)
                for h in range(2):
                    last = dve.scalar_tensor_tensor(aggT[:, h], aggT[:, h], goes, pb[h][:, 0:BP],
                                                    ALU.mult, ALU.add)
                last.then_inc(f.acc, 1)
                dve.wait_ge(f.dg, k + 1)
                ch.step(dve.scalar_tensor_tensor(deg[0:BP], deg[0:BP], goes[0:BP], pb[2][0:BP, 0:1],
                                                 ALU.mult, ALU.add))
                inv_root(dve, ch, f, k * ROOTS[f.i] + 1, s_in[0:BP],
                         dve.tensor_scalar(s_in[0:BP], deg[0:BP], 1.0, None, ALU.max))
                gcn_counts(dve, f, *ahead)
                dve.wait_ge(f.z, k + 1)
                dve.wait_ge(f.free, k + 1)
                if f.i == 0:
                    ch.step(dve.scalar_tensor_tensor(zt[0:BP], pb[3][0:BP, 0:D], s_in[0:BP], bg[0:BP, 0],
                                                     ALU.mult, ALU.add))
                    ch.step(dve.tensor_scalar(row12[0:BP], zt[0:BP], 0.0, sout_c[0:BP, u:u + 1],
                                              ALU.max, ALU.mult))
                    dve.sem_inc(f.fin, 1)
                    assert ch.n == LINKS[0], ch.n
                    return
                ch.step(dve.scalar_tensor_tensor(zt[0:BP], pb[3][0:BP, 0:D], s_in[0:BP], bg[0:BP, 1],
                                                 ALU.mult, ALU.add))
                ch.step(dve.scalar_tensor_tensor(x2[0:BP], zt[0:BP], 0.0, xrow[0:BP, u], ALU.max, ALU.add))
                ch.step(dve.bn_stats(bst[0:BP], x2[0:BP]))
                dve.sem_inc(s_gate, 1)
                ch.step(dve.bn_aggr(bmv[0:BP], bst[0:BP]))
                inv_root(dve, ch, f, k * ROOTS[f.i] + 2, brs[0:BP, 0:1],
                         dve.tensor_scalar(brs[0:BP, 0:1], bmv[0:BP, 1:2], EPS, None, ALU.add))
                ch.step(dve.scalar_tensor_tensor(brs[0:BP, 1:2], bmv[0:BP, 0:1], -1.0, brs[0:BP, 0:1],
                                                 ALU.mult, ALU.mult))
                ch.step(dve.tensor_scalar(zt[0:BP], x2[0:BP], brs[0:BP, 0:1], brs[0:BP, 1:2], ALU.mult, ALU.add))
                ch.step(dve.tensor_scalar(h2[0:BP], zt[0:BP], 0.0, None, ALU.max))
                ch.step(dve.tensor_tensor(x2[0:BP], x2[0:BP], h2[0:BP], ALU.add))
                ch.step(dve.bn_stats(bst[0:BP], h2[0:BP]))
                dve.sem_inc(s_gate, 1)
                ch.step(dve.bn_aggr(bmv[0:BP], bst[0:BP]))
                inv_root(dve, ch, f, k * ROOTS[f.i] + 3, brs[0:BP, 0:1],
                         dve.tensor_scalar(brs[0:BP, 0:1], bmv[0:BP, 1:2], EPS, None, ALU.add))
                ch.step(dve.tensor_scalar(xn[0:BP], h2[0:BP], bmv[0:BP, 0:1], brs[0:BP, 0:1],
                                          ALU.subtract, ALU.mult))
                ch.step(dve.tensor_tensor(xn[0:BP], xn[0:BP], gam[0:BP], ALU.mult))
                ch.step(dve.tensor_tensor(xn[0:BP], xn[0:BP], bet[0:BP], ALU.add))
                dve.sem_inc(s_xn, 1)
                ch.step(dve.tensor_tensor(rowS[0:BP, HEADS:SIDE], x2[0:BP], bu_s[0:BP], ALU.add))
                dve.sem_inc(s_rs, 1)
                assert ch.n == LINKS[1], ch.n

            def gcn_project(pe, k):
                pe.wait_ge(s_xn, k + 1)
                for h in range(2):
                    last = pe.transpose(pb[4][:, h * P:h * P + BP], xn[0:BP, h * P:(h + 1) * P],
                                        ident[0:BP, 0:BP])
                last.then_inc(s_xt, 1)
                pe.wait_ge(s_xc, k + 1)
                for h in range(2):
                    pe.matmul(pb[5][0:BP, :], xnT[:, h], wcat[:, h, 0:2 * D], start=(h == 0), stop=(h == 1))
                for h in range(2):
                    last = pe.matmul(pb[6][0:BP, 0:2 * HEADS], xnT[:, h], wcat[:, h, 2 * D:WC],
                                     start=(h == 0), stop=(h == 1))
                last.then_inc(s_H, 1)

            def gcn_tensor(pe, f, it, u, first=False):
                k = it * UNROLL + u
                for g in range(2):
                    q = 2 * u + g
                    pe.wait_ge(f.hot, it * (2 * UNROLL) + q + 1)
                    rows_wait(pe, f, it, q)
                    for j in range(HALF):
                        a, z = (g == 0 and j == 0), (g == 1 and j == HALF - 1)
                        for h in range(2):
                            lo = j * D + h * P
                            last = pe.matmul(pb[h][:, 0:BP], ring[:, q % SLOTS, lo:lo + P],
                                             hot[:, q % SLOTS, j, :], start=a, stop=z)
                    last.then_inc(f.used, 1)
                    if f.i == 1 and g == 0 and not first:
                        gcn_project(pe, k - 1)
                pe.wait_ge(f.hc, k + 1)
                for g in range(2):
                    last = pe.matmul(pb[2][0:BP, 0:1], part[:, g], ones[:, 0:1], start=(g == 0), stop=(g == 1))
                last.then_inc(f.dg, 1)
                pe.wait_ge(f.acc, k + 1)
                for h in range(2):
                    last = pe.matmul(pb[3][0:BP, 0:D], aggT[:, h], wg[:, f.i, h], start=(h == 0), stop=(h == 1))
                last.then_inc(f.z, 1)

            def gcn2_scalar(act, f, it, u):
                k = it * UNROLL + u
                root(act, f, k * ROOTS[1] + 1, s_in[0:BP])
                root(act, f, k * ROOTS[1] + 2, brs[0:BP, 0:1])
                root(act, f, k * ROOTS[1] + 3, brs[0:BP, 0:1])
                act.wait_ge(s_xt, k + 1)
                act.copy(xnT[:], pb[4][:, 0:2 * P].rearrange("p (h n) -> p h n", h=2)[:, :, 0:BP]).then_inc(s_xc, 1)
                act.wait_ge(s_H, k + 1)
                act.wait_ge(f.free, k + 1)
                act.copy(row3[0:BP, 0:2 * D], pb[5][0:BP, :])
                act.copy(row3[0:BP, 2 * D:ROW3], pb[6][0:BP, 0:HEADS])
                act.copy(rowS[0:BP, 0:HEADS], pb[6][0:BP, HEADS:2 * HEADS]).then_inc(f.t, 1)
                act.wait_ge(f.t, k + 1)
                act.wait_ge(s_rs, k + 1)
                act.sem_inc(f.fin, 1)

            def own1(sp, f, node, u):
                sp.dma_start(sout_c[0:BP, u:u + 1],
                             bass.AP(sout_d.tensor, node, [[1, BP], [1, 1]])).then_inc(f.rec[u], 16)

            def own2(sp, f, node, u):
                sp.dma_start(xrow[0:BP, u], x[bass.ds(node, BP), :]).then_inc(f.rec[u], 16)

            def store1(sp, f, node):
                sp.dma_start(table[1][bass.ds(node, BP), :], row12[0:BP]).then_inc(f.st, 16)

            def store2(sp, f, node):
                sp.dma_start(table[2][bass.ds(node, BP), :], row3[0:BP]).then_inc(f.st, 16)
                sp.dma_start(side_d[bass.ds(node, BP), :], rowS[0:BP]).then_inc(f.st, 16)

            with nc.Block() as block:
                @block.sync
                def _(sp):
                    sp_phase(sp, ph[0], own1, store1, 1)
                    sp_phase(sp, ph[1], own2, store2, 2)

                @block.gpsimd
                def _(pool):
                    pool_phase(pool, ph[0])
                    pool_phase(pool, ph[1])

                @block.vector
                def _(dve):
                    n = dve.value_load(niter_i[0:1, 0:1], min_val=UNROLL, max_val=MAXCH // UNROLL)
                    dve.memset(aggT[:], 0.0)
                    dve.memset(deg[:], 0.0)
                    dve.wait_ge(s_go[0], 1)
                    for f in ph[0:2]:
                        if f.i == 1:
                            dve.wait_ge(ph[0].hot, n * (2 * UNROLL) + 2)
                            dve.wait_ge(ph[0].hc, n * UNROLL + 1)
                        gcn_hot(dve, Chain(dve, f.dve), f, 0, 0)
                        gcn_counts(dve, f, 0, 0)
                        with dve.Fori(0, n) as it:
                            for u in range(UNROLL):
                                gcn_vector(dve, f, it, u)

                @block.tensor
                def _(pe):
                    n = pe.value_load(niter_i[0:1, 0:1], min_val=UNROLL, max_val=MAXCH // UNROLL)
                    for f in ph[0:2]:
                        pe.sem_inc(f.used, SLOTS)
                        for u in range(UNROLL):
                            gcn_tensor(pe, f, 0, u, first=(u == 0))
                        with pe.Fori(1, n) as it:
                            for u in range(UNROLL):
                                gcn_tensor(pe, f, it, u)
                    gcn_project(pe, n * UNROLL - 1)

                @block.scalar
                def _(act):
                    n = act.value_load(niter_i[0:1, 0:1], min_val=UNROLL, max_val=MAXCH // UNROLL)
                    with act.Fori(0, n) as it:
                        for u in range(UNROLL):
                            root(act, ph[0], it * UNROLL + u + 1, s_in[0:BP])
                    with act.Fori(0, n) as it:
                        for u in range(UNROLL):
                            gcn2_scalar(act, ph[1], it, u)

        phase_c = ExitStack()
        def sc(name, shape, dt=F32):
            return phase_c.enter_context(nc.sbuf_tensor(name, shape, dt))
        with phase_c:
            f = ph[2]
            hotb = sc("hotb", [P, SLOTS, HALF, BP], BF16)
            hotT = sc("hotT", [BP, TILES, P], BF16)
            iden_b = sc("iden_b", [P, P], BF16)
            dwa = sc("dwa", [P, TILES + 2])
            same = sc("same", [P, TILES + 1])
            fr = sc("fr", [P, TILES])
            frp = sc("frp", [P, TILES])
            lastf = sc("lastf", [P, TILES])
            endc = sc("endc", [P, TILES])
            notp0 = sc("notp0", [P, 1])
            cc = sc("cc", [P, 2])
            pen = sc("pen", [P, HEADS, TILES])
            ash = sc("ash", [P, HEADS, TILES])
            pre = sc("pre", [P, HEADS, TILES])
            cpk = sc("cpk", [P, 3, HEADS])
            cpT = sc("cpT", [HEADS, 3, P])
            car = sc("car", [HEADS, P])
            cin = sc("cin", [HEADS, P])
            fl = sc("fl", [P, TILES, HEADS + 1])
            flb = sc("flb", [P, 3, TILES, HEADS + 1], BF16)
            tmp = sc("tmp", [P, TILES * (HEADS + 1)])
            mx = sc("mx", [P, HEADS])
            hp = sc("hp", [P, 2])
            lk = sc("lk", [P, 3, HEADS])
            dif = sc("dif", [P, 2, HEADS])
            rr = sc("rr", [P, 2 * HEADS])
            rb = sc("rb", [P, 3, 2 * HEADS], BF16)
            et = sc("et", [P, TILES, HEADS])
            ex = sc("ex", [P, TILES, HEADS])
            exb = sc("exb", [P, UNROLL, 3, TILES, HEADS], BF16)
            ab5 = sc("ab5", [P, UNROLL, 2, HEADS])
            den = sc("den", [P, HEADS])
            dsum = sc("dsum", [P, HEADS])
            rd = sc("rd", [P, HEADS])
            acc = sc("acc", [P, 2 * D])
            xo = sc("xo", [P, 2 * D])
            neg = sc("neg", [P, 2 * D])
            xcT = sc("xcT", [P, 4, BP])
            res = sc("res", [P, D])
            self_h = sc("self_h", [P, UNROLL, ROW3])
            side_c = sc("side_c", [P, UNROLL, SIDE])
            minus1 = sc("minus1", [P, 1])
            pb4b = pb[4][:, :].bitcast(BF16)
            s_ng = sem("s_ng")
            s_dc = sem("s_dc")
            s_nf = sem("s_nf")
            NUMB = [0, 1, 0, 1, 2]
            s_c3 = sem("s_c3")
            s_hb = sem("s_hb")
            s_ot = sem("s_ot")
            s_oc = sem("s_oc")
            s_cp = sem("s_cp")
            s_tp = sem("s_tp")
            s_tc = sem("s_tc")
            s_ci = sem("s_ci")
            s_tb = sem("s_tb")
            s_fl = sem("s_fl")
            s_mx = sem("s_mx")
            s_r3 = sem("s_r3")
            s_bc = sem("s_bc")
            s_df = sem("s_df")
            s_ab = sem("s_ab")
            s_et = sem("s_et")
            s_ex = sem("s_ex")
            s_xb = sem("s_xb")
            s_ms = sem("s_ms")
            s_xr = sem("s_xr")
            s_el = sem("s_el")
            s_xc = sem("s_xc2")
            s_xt = sem("s_xt2")
            s_xs = sem("s_xs")
            s_u = sem("s_u")

            def wide(ap):
                return ap.rearrange("p (h c) -> p h c", h=HEADS)

            def over(ap, n=HW):
                return ap.unsqueeze(2).to_broadcast([ap.shape[0], HEADS, n])

            def split3(dve, ch, v, parts, t):
                ch.step(dve.tensor_copy(parts[0], v))
                ch.step(dve.tensor_tensor(t, v, parts[0], ALU.subtract))
                ch.step(dve.tensor_copy(parts[1], t))
                return dve.tensor_tensor(parts[2], t, parts[1], ALU.subtract)

            def edge_flags(dve, ch, it, u):
                dve.wait_ge(f.rec[u], (it + 1) * 16 * NREC[2])
                ch.step(dve.tensor_scalar(dwa[:], dwin[:, u], cb[:, u, 1:2], None, ALU.subtract))
                for g in range(2):
                    q = 2 * u + g
                    dve.wait_ge(f.used, it * (2 * UNROLL) + q + 1)
                    dve.tensor_tensor(hotb[:, q % SLOTS], iota_v[:].unsqueeze(1).to_broadcast([P, HALF, BP]),
                                      dwa[:, 1 + g * HALF:1 + (g + 1) * HALF].unsqueeze(2).to_broadcast(
                                          [P, HALF, BP]), ALU.is_equal).then_inc(s_hb, 1)
                ch.step(dve.tensor_tensor(same[:], dwa[:, 0:TILES + 1], dwa[:, 1:TILES + 2], ALU.is_equal))
                ch.step(dve.tensor_scalar(fr[:], dwa[:, 1:TILES + 1], dwa[:, 1:2], None, ALU.is_equal))
                ch.step(dve.tensor_tensor(cc[:, 1:2], same[:, 0:1], notp0[:], ALU.mult))
                ch.step(dve.tensor_tensor(cc[:, 0:1], cc[:, 1:2], fr[:, TILES - 1:TILES], ALU.mult))
                dve.tensor_scalar(cpk[:, 1:3], cc[:].unsqueeze(2).to_broadcast([P, 2, HEADS]), -1.0, BIG,
                                  ALU.add, ALU.mult)
                dve.tensor_scalar(pen[:, :, 1:TILES],
                                  same[:, 1:TILES].unsqueeze(1).to_broadcast([P, HEADS, TILES - 1]), -1.0, BIG,
                                  ALU.add, ALU.mult)
                dve.tensor_scalar(frp[:], fr[:], -1.0, BIG, ALU.add, ALU.mult)
                ch.step(dve.tensor_scalar(lastf[:], same[:, 1:TILES + 1], -1.0, 1.0, ALU.mult, ALU.add))
                ch.step(dve.tensor_tensor(lastf[:], lastf[:], endc[:], ALU.max))

            def run_maxima(dve, ch, it, u):
                for g in range(2):
                    q = 2 * u + g
                    rows_wait(dve, f, it, q)
                    last = dve.tensor_copy(ash[:, :, g * HALF:(g + 1) * HALF],
                                           ring[:, q % SLOTS].rearrange("p (j n) -> p n j", j=HALF)[:, 2 * D:ROW3])
                ch.step(last)
                ch.step(dve.tensor_tensor_scan(pre[:].rearrange("p h j -> p (h j)"),
                                               pen[:].rearrange("p h j -> p (h j)"),
                                               ash[:].rearrange("p h j -> p (h j)"), -BIG, ALU.add, ALU.max))
                dve.tensor_copy(cpk[:, 0], pre[:, :, TILES - 1]).then_inc(s_cp, 1)

            def carry(dve, ch, k):
                dve.wait_ge(s_tc, k + 1)
                ch.step(dve.tensor_tensor_scan(car[:], cpT[:, 1], cpT[:, 0], -BIG, ALU.add, ALU.max))
                dve.tensor_tensor(cin[:, 1:P], car[:, 0:P - 1], cpT[:, 2, 1:P], ALU.add).then_inc(s_ci, 1)

            def whole_runs(dve, ch, k):
                dve.wait_ge(s_tb, k + 1)
                t = tmp[:, 0:HEADS * TILES].rearrange("p (h j) -> p h j", h=HEADS)
                ch.step(dve.tensor_tensor(t, frp[:].unsqueeze(1).to_broadcast([P, HEADS, TILES]),
                                          over(pb[5][:, 384:384 + HEADS], TILES), ALU.add))
                ch.step(dve.tensor_tensor(pre[:], pre[:], t, ALU.max))
                dve.tensor_copy(fl[:, :, HEADS], lastf[:])
                ch.step(dve.tensor_tensor(fl[:, :, 0:HEADS].rearrange("p j h -> p h j"), pre[:],
                                          lastf[:].unsqueeze(1).to_broadcast([P, HEADS, TILES]), ALU.mult))
                split3(dve, ch, fl[:].rearrange("p j h -> p (j h)"),
                       [flb[:, i].rearrange("p j h -> p (j h)") for i in range(3)], tmp[:]).then_inc(s_fl, 1)

            def leaky(dve, ch, v):
                ch.step(dve.scalar_tensor_tensor(v, v, 0.2, v, ALU.mult, ALU.max))

            def node_maxima(dve, ch, k, u):
                b = slice(0, BP)
                dve.wait_ge(s_mx, k + 1)
                as_self, ad = self_h[b, u, 2 * D:ROW3], side_c[b, u, 0:HEADS]
                ch.step(dve.tensor_scalar(hp[b, 0:1], pb[5][b, 400 + HEADS:401 + HEADS], -1.0, BIG,
                                          ALU.add, ALU.mult))
                ch.step(dve.tensor_scalar(hp[b, 1:2], cb[b, u, 0:1], -1.0, BIG, ALU.add, ALU.mult))
                dve.tensor_tensor(lk[b, 0], mx[b], ad, ALU.add)
                ch.step(dve.scalar_tensor_tensor(lk[b, 1], pb[5][b, 400:400 + HEADS], hp[b, 0:1], as_self,
                                                 ALU.add, ALU.max))
                ch.step(dve.scalar_tensor_tensor(mx[b], mx[b], hp[b, 1:2], lk[b, 1], ALU.add, ALU.max))
                dve.tensor_tensor(lk[b, 1], mx[b], ad, ALU.add)
                ch.step(dve.tensor_tensor(lk[b, 2], as_self, ad, ALU.add))
                leaky(dve, ch, lk[b])
                dve.tensor_copy(rr[b, 0:HEADS], ad)
                ch.step(dve.tensor_copy(rr[b, HEADS:2 * HEADS], lk[b, 1]))
                dve.tensor_tensor(dif[b, 0], lk[b, 0], lk[b, 1], ALU.subtract)
                ch.step(dve.tensor_tensor(dif[b, 1], lk[b, 2], lk[b, 1], ALU.subtract))
                dve.tensor_scalar(dif[b], dif[b], 0.0, None, ALU.min).then_inc(s_df, 1)
                split3(dve, ch, rr[b], [rb[b, i] for i in range(3)], tmp[b, 0:2 * HEADS]).then_inc(s_r3, 1)

            def edge_weights(dve, ch, k):
                dve.wait_ge(s_bc, k + 1)
                for g in range(2):
                    js = slice(g * HALF, (g + 1) * HALF)
                    b6 = pb[BCB[g]][:, 0:HALF * 2 * HEADS].rearrange("p (j n) -> p j n", j=HALF)
                    last = dve.tensor_tensor(et[:, js], ash[:, :, js].rearrange("p h j -> p j h"),
                                             b6[:, :, 0:HEADS], ALU.add)
                ch.step(last)
                leaky(dve, ch, et[:].rearrange("p j h -> p (j h)"))
                for g in range(2):
                    js = slice(g * HALF, (g + 1) * HALF)
                    b6 = pb[BCB[g]][:, 0:HALF * 2 * HEADS].rearrange("p (j n) -> p j n", j=HALF)
                    last = dve.tensor_tensor(et[:, js], et[:, js], b6[:, :, HEADS:2 * HEADS], ALU.subtract)
                ch.step(last)
                dve.tensor_scalar(et[:], et[:], 0.0, None, ALU.min).then_inc(s_et, 1)

            def split_weights(dve, ch, k, u):
                dve.wait_ge(s_ex, k + 1)
                split3(dve, ch, ex[:].rearrange("p j h -> p (j h)"),
                       [exb[:, u, i].rearrange("p j h -> p (j h)") for i in range(3)],
                       tmp[:, 0:TILES * HEADS]).then_inc(s_xb, 1)

            def weigh(dve, u, g):
                v = ring[:, (2 * u + g) % SLOTS].rearrange("p (j n) -> p j n", j=HALF)[:, :, 0:2 * D].rearrange(
                    "p j (h c) -> p j h c", h=HEADS)
                w = ex[:, g * HALF:(g + 1) * HALF].unsqueeze(3).to_broadcast([P, HALF, HEADS, HW])
                dve.tensor_tensor(v, v, w, ALU.mult).then_inc(s_ms, 1)

            def read_den(dve, k):
                b = slice(0, BP)
                dve.wait_ge(f.used, k * 2 + 2 + SLOTS)
                dve.tensor_copy(dsum[b], pb[3][b, 0:HEADS]).then_inc(s_dc, 1)
                dve.wait_ge(s_dc, k + 2)

            def node_rows(dve, ch, k, u):
                b = slice(0, BP)
                num = pb[NUMB[u]][b, :]
                al, be = ab5[b, u, 0], ab5[b, u, 1]
                dve.wait_ge(s_ab, k + 1)
                ch.step(dve.tensor_scalar(al, al, cb[b, u, 0:1], None, ALU.mult))
                ch.step(dve.tensor_tensor(den[b], den[b], al, ALU.mult))
                ch.step(dve.tensor_tensor(wide(acc[b]), wide(acc[b]), over(al), ALU.mult))
                ch.step(dve.tensor_tensor(den[b], den[b], dsum[b], ALU.add))
                ch.step(dve.tensor_tensor(acc[b], acc[b], num, ALU.add))
                ch.step(dve.tensor_tensor(wide(xo[b]), wide(self_h[b, u, 0:2 * D]), over(be), ALU.mult))
                dve.sem_inc(s_nf, 1)
                ch.step(dve.scalar_tensor_tensor(rd[b], den[b], 1e-16, be, ALU.add, ALU.add))
                ch.step(dve.reciprocal(rd[b], rd[b]))
                ch.step(dve.tensor_tensor(xo[b], xo[b], acc[b], ALU.add))
                ch.step(dve.tensor_tensor(wide(xo[b]), wide(xo[b]), over(rd[b]), ALU.mult))
                dve.tensor_tensor(xo[b], xo[b], ab[b], ALU.add).then_inc(s_xr, 1)

            def elu(dve, k):
                b = slice(0, BP)
                dve.wait_ge(s_el, k + 1)
                dve.scalar_tensor_tensor(xo[b], xo[b], 0.0, neg[b], ALU.max, ALU.add).then_inc(s_xc, 1)

            def result(dve, k, u):
                b = slice(0, BP)
                dve.wait_ge(s_u, k + 1)
                dve.wait_ge(f.free, k + 1)
                dve.tensor_tensor(res[b], pb[7][b, 0:D], side_c[b, u, HEADS:SIDE], ALU.add).then_inc(f.fin, 1)

            def at(it, u, d):
                return it + (u + d) // UNROLL, (u + d) % UNROLL

            def gat_vector(dve, ch, it, u, first=False, last=0):
                k = it * UNROLL + u
                split_weights(dve, ch, k, u)
                weigh(dve, u, 0)
                if last < 2:
                    run_maxima(dve, ch, *at(it, u, 1))
                if not first:
                    read_den(dve, k - 1)
                weigh(dve, u, 1)
                if last < 2:
                    carry(dve, ch, k + 1)
                if not first:
                    node_rows(dve, ch, k - 1, (u - 1) % UNROLL)
                if last < 2:
                    whole_runs(dve, ch, k + 1)
                if not first:
                    elu(dve, k - 1)
                if last < 2:
                    node_maxima(dve, ch, k + 1, (u + 1) % UNROLL)
                if last == 0:
                    edge_flags(dve, ch, *at(it, u, 2))
                if last < 2:
                    edge_weights(dve, ch, k + 1)
                if not first:
                    result(dve, k - 1, (u - 1) % UNROLL)

            BCB = [6, 4]

            def turn_hot(pe, it, u, m):
                k = it * UNROLL + u
                for j in range(6 * m, 6 * m + 6):
                    g = j // HALF
                    if j == 0 or j == HALF or j == 6 * m:
                        pe.wait_ge(s_hb, it * 2 * UNROLL + 2 * u + g + 1)
                    if j == 0:
                        pe.wait_ge(s_et, k + 1)
                    if j == 6 * m:
                        pe.wait_ge(s_oc, 3 * k + m + 1)
                    last = pe.transpose(pb4b[0:BP, (j % 6) * P:(j % 6 + 1) * P],
                                        hotb[:, (2 * u + g) % SLOTS, j % HALF], iden_b[:])
                last.then_inc(s_ot, 1)

            def turn_last(pe, k):
                pe.wait_ge(s_cp, k + 1)
                for i in range(3):
                    last = pe.transpose(pb[5][0:HEADS, i * P:(i + 1) * P], cpk[:, i], ident[:])
                last.then_inc(s_tp, 1)

            def turn_back(pe, k):
                pe.wait_ge(s_ci, k + 1)
                pe.sem_inc(s_gate, 1)
                pe.transpose(pb[5][:, 384:384 + HEADS], cin[:], ident[0:HEADS, 0:HEADS]).then_inc(s_tb, 1)

            def to_nodes(pe, k, u):
                pe.wait_ge(s_fl, k + 1)
                for j in range(TILES):
                    for i in range(3):
                        last = pe.matmul(pb[5][0:BP, 400:401 + HEADS], hotb[:, (2 * u + j // HALF) % SLOTS, j % HALF],
                                         flb[:, i, j], start=(i == 0 and j == 0), stop=(i == 2 and j == TILES - 1))
                last.then_inc(s_mx, 1)

            def to_edges(pe, k):
                pe.wait_ge(s_r3, k + 1)
                pe.wait_ge(s_oc, 3 * k + 4)
                for j in range(TILES):
                    bank, c = BCB[j // HALF], (j % HALF) * 2 * HEADS
                    for i in range(3):
                        last = pe.matmul(pb[bank][:, c:c + 2 * HEADS], hotT[:, j], rb[0:BP, i],
                                         start=(i == 0), stop=(i == 2))
                last.then_inc(s_bc, 1)

            def sums(pe, u, g, js):
                q = (2 * u + g) % SLOTS
                for j in js:
                    a, z = (g == 0 and j == 0), (g == 1 and j == HALF - 1)
                    pe.matmul(pb[NUMB[u]][0:BP, :], hot[:, q, j], ring[:, q, j * ROW3:j * ROW3 + 2 * D],
                              start=a, stop=z)

            def denominators(pe, k, u, g):
                if g == 0:
                    pe.wait_ge(s_dc, k + 1)
                for j in range(HALF):
                    for i in range(3):
                        last = pe.matmul(pb[3][0:BP, 0:HEADS],
                                         hotb[:, (2 * u + g) % SLOTS, j], exb[:, u, i, g * HALF + j],
                                         start=(g == 0 and j == 0 and i == 0),
                                         stop=(g == 1 and j == HALF - 1 and i == 2))
                last.then_inc(f.used, 1)

            def out_turn(pe, k):
                pe.wait_ge(s_xc, k + 1)
                for c in range(4):
                    last = pe.transpose(pb[7][:, c * BP:(c + 1) * BP], xo[0:BP, c * P:(c + 1) * P],
                                        ident[0:BP, 0:BP])
                last.then_inc(s_xt, 1)

            def out_project(pe, k):
                pe.wait_ge(s_xs, k + 1)
                for c in range(4):
                    last = pe.matmul(pb[7][0:BP, 0:D], xcT[:, c], wu_s[:, c], start=(c == 0), stop=(c == 3))
                last.then_inc(s_u, 1)

            def gat_tensor(pe, it, u, first=False, last=0):
                k = it * UNROLL + u
                nxt = at(it, u, 1)
                pe.wait_ge(f.hot, it * 2 * UNROLL + 2 * u + 2)
                if not first:
                    pe.wait_ge(s_nf, k)
                pe.wait_ge(s_xb, k + 1)
                pe.wait_ge(s_ms, it * 2 * UNROLL + 2 * u + 1)
                sums(pe, u, 0, range(0, 3))
                if last < 2:
                    turn_hot(pe, *nxt, 0)
                sums(pe, u, 0, range(3, 6))
                if last < 2:
                    turn_hot(pe, *nxt, 1)
                    turn_last(pe, k + 1)
                sums(pe, u, 0, range(6, 9))
                denominators(pe, k, u, 0)
                if last < 2:
                    turn_hot(pe, *nxt, 2)
                    turn_back(pe, k + 1)
                pe.wait_ge(s_ms, it * 2 * UNROLL + 2 * u + 2)
                sums(pe, u, 1, range(0, 5))
                if last < 2:
                    to_nodes(pe, k + 1, nxt[1])
                if not first:
                    out_turn(pe, k - 1)
                sums(pe, u, 1, range(5, 8))
                if last < 2:
                    to_edges(pe, k + 1)
                if not first:
                    out_project(pe, k - 1)
                sums(pe, u, 1, range(8, 9))
                denominators(pe, k, u, 1)

            def hot_out(act, k, m):
                act.wait_ge(s_ot, 3 * k + m + 1)
                act.copy(hotT[:, 6 * m:6 * m + 6], pb4b[0:BP, 0:6 * P].rearrange("p (j n) -> p j n", j=6)
                         ).then_inc(s_oc, 1)

            def hot_f32(act, it, u):
                for g in range(2):
                    q = 2 * u + g
                    act.wait_ge(s_hb, it * 2 * UNROLL + q + 1)
                    act.copy(hot[:, q % SLOTS], hotb[:, q % SLOTS]).then_inc(f.hot, 1)

            def last_out(act, k):
                act.wait_ge(s_tp, k + 1)
                act.copy(cpT[:].rearrange("p i n -> p (i n)"), pb[5][0:HEADS, 0:3 * P]).then_inc(s_tc, 1)

            def state_exp(act, k, u):
                act.wait_ge(s_df, k + 1)
                act.activation(ab5[0:BP, u], dif[0:BP], ACT.Exp).then_inc(s_ab, 1)

            def edge_exp(act, k):
                act.wait_ge(s_et, k + 2)
                act.activation(ex[:], et[:], ACT.Exp).then_inc(s_ex, 1)

            def neg_exp(act, k):
                b = slice(0, BP)
                act.wait_ge(s_xr, k + 1)
                act.activation(neg[b], xo[b], ACT.Relu, scale=-1.0).then_inc(s_ng, 1)
                act.wait_ge(s_ng, k + 1)
                act.activation(neg[b], neg[b], ACT.Exp, scale=-1.0).then_inc(s_el, 1)

            def out_rows(act, k):
                act.wait_ge(s_xt, k + 1)
                act.activation(xcT[:].rearrange("p c n -> p (c n)"), pb[7][:, 0:4 * BP], ACT.Identity,
                               bias=minus1[:]).then_inc(s_xs, 1)

            def gat_scalar(act, it, u, first=False, last=0):
                k = it * UNROLL + u
                nxt = at(it, u, 1)
                if last < 2:
                    hot_out(act, k + 1, 0)
                    hot_f32(act, *nxt)
                    hot_out(act, k + 1, 1)
                    last_out(act, k + 1)
                    hot_out(act, k + 1, 2)
                if not first:
                    neg_exp(act, k - 1)
                if last < 2:
                    state_exp(act, k + 1, nxt[1])
                if not first:
                    out_rows(act, k - 1)
                if last < 2:
                    edge_exp(act, k + 1)

            def steps(eng, n, body):
                for u in range(UNROLL):
                    body(0, u, first=(u == 0))
                with eng.Fori(1, n) as it:
                    for u in range(UNROLL):
                        body(it, u)
                for u in range(UNROLL):
                    body(n, u, last=max(0, u - (UNROLL - 3)))

            def own3(sp, f, node, u):
                sp.dma_start(self_h[0:BP, u], table[2][bass.ds(node, BP), :]).then_inc(f.rec[u], 16)
                sp.dma_start(side_c[0:BP, u], side_d[bass.ds(node, BP), :]).then_inc(f.rec[u], 16)

            def store3(sp, f, node):
                sp.dma_start(out[bass.ds(node, BP), :], res[0:BP]).then_inc(f.st, 16)

            FIRST, LOOP = 243, 215

            with nc.Block() as block:
                @block.sync
                def _(sp):
                    sp_phase(sp, f, own3, store3, 1)

                @block.gpsimd
                def _(pool):
                    pool.memset(endc[:], 0.0)
                    pool.memset(notp0[:], 1.0)
                    pool.memset(minus1[:], -1.0)
                    pool.memset(pen[:, :, 0:1], -BIG)
                    pool.memset(cin[:, 0:1], -BIG)
                    pool.tensor_copy(iden_b[:], ident[:]).then_inc(s_c3, 1)
                    pool.wait_ge(s_c3, 1)
                    pool.affine_select(endc[:], endc[:], pattern=[[1, TILES]], compare_op=ALU.not_equal,
                                       fill=1.0, base=1 - CAP, channel_multiplier=TILES)
                    pool.affine_select(notp0[:], notp0[:], pattern=[[0, 1]], compare_op=ALU.not_equal,
                                       fill=0.0, base=0, channel_multiplier=1).then_inc(s_c3, 1)
                    pool_phase(pool, f)

                @block.vector
                def _(dve):
                    n = dve.value_load(niter_i[0:1, 1:2], min_val=UNROLL - 1, max_val=MAXCH // UNROLL - 1)
                    ch = Chain(dve, f.dve)
                    dve.memset(acc[:], 0.0)
                    dve.memset(den[:], 0.0)
                    ch.step(dve.memset(mx[:], 0.0))
                    dve.sem_inc(s_et, 1)
                    dve.sem_inc(s_nf, 1)
                    dve.sem_inc(s_dc, 1)
                    dve.wait_ge(s_c3, 2)
                    edge_flags(dve, ch, 0, 0)
                    run_maxima(dve, ch, 0, 0)
                    carry(dve, ch, 0)
                    whole_runs(dve, ch, 0)
                    node_maxima(dve, ch, 0, 0)
                    edge_flags(dve, ch, 0, 1)
                    edge_weights(dve, ch, 0)

                    def body(it, u, first=False, last=0):
                        if u == 0 and not first:
                            ch.base, ch.n = FIRST + (it - 1) * LOOP, 0
                        gat_vector(dve, ch, it, u, first, last)
                        if u == UNROLL - 1 and not last:
                            want = FIRST if isinstance(it, int) else LOOP
                            assert ch.n == want, (ch.n, want)

                    steps(dve, n, body)
                    k = n * UNROLL + UNROLL - 1
                    read_den(dve, k)
                    node_rows(dve, ch, k, UNROLL - 1)
                    elu(dve, k)
                    result(dve, k, UNROLL - 1)

                @block.tensor
                def _(pe):
                    n = pe.value_load(niter_i[0:1, 1:2], min_val=UNROLL - 1, max_val=MAXCH // UNROLL - 1)
                    pe.wait_ge(s_c3, 2)
                    pe.sem_inc(f.used, SLOTS)
                    for m in range(3):
                        turn_hot(pe, 0, 0, m)
                    turn_last(pe, 0)
                    turn_back(pe, 0)
                    to_nodes(pe, 0, 0)
                    to_edges(pe, 0)
                    steps(pe, n, lambda it, u, first=False, last=0: gat_tensor(pe, it, u, first, last))
                    out_turn(pe, n * UNROLL + UNROLL - 1)
                    out_project(pe, n * UNROLL + UNROLL - 1)

                @block.scalar
                def _(act):
                    n = act.value_load(niter_i[0:1, 1:2], min_val=UNROLL - 1, max_val=MAXCH // UNROLL - 1)
                    act.sem_inc(s_oc, 1)
                    hot_out(act, 0, 0)
                    hot_f32(act, 0, 0)
                    hot_out(act, 0, 1)
                    hot_out(act, 0, 2)
                    last_out(act, 0)
                    state_exp(act, 0, 0)
                    edge_exp(act, 0)
                    steps(act, n, lambda it, u, first=False, last=0: gat_scalar(act, it, u, first, last))
                    neg_exp(act, n * UNROLL + UNROLL - 1)
                    out_rows(act, n * UNROLL + UNROLL - 1)


_INS = ['x', 'src', 'dst', 'L0_gnn_W1', 'L0_gnn_b1', 'L0_gnn_W2', 'L0_gnn_b2', 'L1_gnn_gamma', 'L1_gnn_beta',
        'L1_gnn_W1', 'L1_gnn_a_src1', 'L1_gnn_a_dst1', 'L1_gnn_b1', 'L1_gnn_W2', 'L1_gnn_a_src2',
        'L1_gnn_a_dst2', 'L1_gnn_b2', 'L1_gnn_Wu', 'L1_gnn_bu']


def kernel(**inputs):
    import numpy as _np
    import concourse.bacc as _bacc
    from concourse import mybir as _mybir
    from concourse.bass_utils import run_bass_kernel_spmd as _run

    nc = _bacc.Bacc("TRN2", target_bir_lowering=False, num_devices=1)
    arrays, args = {}, []
    for name in _INS:
        a = _np.ascontiguousarray(inputs[name])
        arrays[f"in_{name}_dram"] = a
        args.append(nc.dram_tensor(f"in_{name}_dram", a.shape, _mybir.dt.from_np(a.dtype), kind="ExternalInput").ap())
    args.append(nc.dram_tensor("out_0_dram", (3125, 256), _mybir.dt.float32, kind="ExternalOutput").ap())
    gnn(nc, *args)
    r = _run(nc, [arrays], core_ids=[0])
    return r.results[0]["out_0_dram"]
```

```python
import concourse.bass as bass
from concourse import mybir
from contextlib import ExitStack

F32 = mybir.dt.float32
BF16 = mybir.dt.bfloat16
I32 = mybir.dt.int32
ALU = mybir.AluOpType
ACT = mybir.ActivationFunctionType
AX = mybir.AxisListType

N = 3125
E = 53125
D = 256
BP = 125
BLOCKS = N // BP
P = 128
TILES = 18
HALF = TILES // 2
CAP = P * TILES
UNROLL = 5
SLOTS = 5
AHEAD = 4
MAXCH = -(-(BLOCKS + E // CAP) // UNROLL) * UNROLL
NCH = MAXCH + AHEAD
EC = E // BP
H1, C1, H2, C2 = 4, 64, 8, 32
HW = 32
HEADS = 2 * D // HW
ROW3 = 2 * D + HEADS
SIDE = HEADS + D
WC = 2 * D + 2 * HEADS
EPS = 1e-5
BIG = 1e30
ROUND = 1.5 * 2 ** 23


class Chain:

    def __init__(self, eng, sem, base=0):
        self.eng, self.sem, self.base, self.n = eng, sem, base, 0

    def step(self, ins):
        self.n += 1
        ins.then_inc(self.sem, 1)
        self.eng.wait_ge(self.sem, self.base + self.n)


def gnn(nc, x, src, dst, gw1, gb1, gw2, gb2, gamma, beta, aw1, as1, ad1, ab1, aw2, as2, ad2, ab2,
        wu, bu, out):
    ctx = ExitStack()
    with ctx:
        def sb(name, shape, dt=F32):
            return ctx.enter_context(nc.sbuf_tensor(name, shape, dt))

        def sem(name):
            return ctx.enter_context(nc.semaphore(name))

        def dram(name, shape, dt=F32):
            return nc.dram_tensor(name, shape, dt, kind="Internal").ap()

        src_lin = dram("src_lin", [E + CAP], I32)
        dst_lin = dram("dst_lin", [E + CAP + 2], I32)
        plan_d = dram("plan_d", [NCH, 2])
        sout_d = dram("sout_d", [BLOCKS, BP])
        table = [dram("table1", [N, D]), dram("table2", [N, D]), dram("table3", [N, ROW3])]
        side_d = dram("side", [N, SIDE])

        ident = sb("ident", [P, P])
        ones = sb("ones", [P, P])
        iota_v = sb("iota_v", [P, BP])
        ring = sb("ring", [P, SLOTS, HALF * ROW3])
        hot = sb("hot", [P, SLOTS, HALF, BP])
        idx = sb("idx", [P, UNROLL, TILES], I32)
        dwin = sb("dwin", [P, UNROLL, TILES + 2], I32)
        cb = sb("cb", [P, UNROLL, 2])
        sout_c = sb("sout_c", [P, UNROLL])
        wg = sb("wg", [P, 2, 2, D])
        bg = sb("bg", [P, 2, D])
        wcat = sb("wcat", [P, 2, WC])
        wu_s = sb("wu_s", [P, 4, D])
        gam = sb("gam", [P, D])
        bet = sb("bet", [P, D])
        bu_s = sb("bu_s", [P, D])
        abT = sb("abT", [P, 4])
        arow = sb("arow", [P, 2, 2 * D])
        dwf = sb("dwf", [P, TILES + 2])
        pb = [ctx.enter_context(nc.psum_tensor(f"bank{i}", [P, 512], F32)) for i in range(8)]

        s_const = sem("s_const")
        s_ld = sem("s_ld")
        s_x = sem("s_x")
        s_w = sem("s_w")
        s_pad = sem("s_pad")
        s_dve = sem("s_dve")
        s_h1 = sem("s_h1")
        s_hm = sem("s_hm")
        s_cnt = sem("s_cnt")
        s_df1 = sem("s_df1")
        s_ac = sem("s_ac")
        s_sc = sem("s_sc")
        s_sq = sem("s_sq")
        s_rt = sem("s_rt")
        s_t1 = sem("s_t1")
        s_plan = sem("s_plan")
        s_pd = sem("s_pd")
        s_go = [sem(f"s_go{i}") for i in range(3)]
        s_st1 = sem("s_st1")
        s_gate = sem("s_gate")

        NOWHERE = 1 << 20
        plan_i = sb("plan_i", [1, 2, NCH], I32)
        niter_i = sb("niter_i", [1, 2], I32)

        class Phase:
            def __init__(self, i):
                self.i = i
                self.rec = [sem(f"rec{i}_{u}") for u in range(UNROLL)]
                self.rows = [sem(f"rows{i}_{s}") for s in range(SLOTS)]
                self.hot = sem(f"hot{i}")
                self.used = sem(f"used{i}")
                self.acc = sem(f"acc{i}")
                self.z = sem(f"z{i}")
                self.t = sem(f"t{i}")
                self.fin = sem(f"fin{i}")
                self.st = sem(f"st{i}")
                self.free = sem(f"free{i}")
                self.dve = sem(f"dve{i}")
                self.hc = sem(f"hc{i}")
                self.dg = sem(f"dg{i}")
                self.sq = sem(f"sq{i}")
                self.rt = sem(f"rt{i}")

        ph = [Phase(i) for i in range(3)]
        NREC = [4, 4, 5]

        phase_a = ExitStack()
        def sa(name, shape, dt=F32):
            return phase_a.enter_context(nc.sbuf_tensor(name, shape, dt))
        with phase_a:
            src_i = sa("src_i", [BP, EC], I32)
            dst_i = sa("dst_i", [BP, EC], I32)
            src_f = sa("src_f", [BP, EC])
            low_f = sa("low_f", [BP, EC])
            low_b = sa("low_b", [BP, EC], BF16)
            high_b = sa("high_b", [BP, EC], BF16)
            dst_f = sa("dst_f", [BP, EC])
            junk = sa("junk", [BP, EC])
            x_all = ring[0:BP, :, :].rearrange("p s n -> p (s n)")[:, 0:BLOCKS * D].rearrange(
                "p (b d) -> p b d", d=D)
            PC = EC // 25
            XB = 8
            iota_r = sa("iota_r", [BP, BP, PC], BF16)
            oh_lo = sa("oh_lo", [BP, 2, BP, PC], BF16)
            oh_hi = sa("oh_hi", [BP, 2, BLOCKS, PC], BF16)
            stats = sa("stats", [BP, BLOCKS, 6])
            mv = sa("mv", [BP, BLOCKS, 2])
            rstd = sa("rstd", [BP, BLOCKS])
            sout = sa("sout", [BP, BLOCKS])
            sc1 = sa("sc1", [BP, BLOCKS])
            nb1 = sa("nb1", [BP, BLOCKS])
            cnt = sa("cnt", [BP, BLOCKS])
            lim = sa("lim", [BP, BLOCKS - 1])
            pad_i = sa("pad_i", [1, 2, CAP + 2], I32)
            row = sa("row", [1, 8, BLOCKS + 1])
            grid = sa("grid", [1, NCH * BLOCKS])
            iotas = sa("iotas", [1, NCH * BLOCKS])
            pl = sa("pl", [1, 4, NCH])
            plan_f = sa("plan_f", [1, NCH, 2])

            with nc.Block() as block:
                @block.sync
                def _(sp):
                    sp.dma_start(src_i[:], src.rearrange("(p c) -> p c", p=BP)).then_inc(s_ld, 16)
                    sp.dma_start(dst_i[:], dst.rearrange("(p c) -> p c", p=BP)).then_inc(s_ld, 16)
                    sp.dma_start(x_all, x.rearrange("(b p) d -> p b d", p=BP)).then_inc(s_x, 16)
                    sp.dma_start(src_lin[0:E].rearrange("(p c) -> p c", p=BP),
                                 src.rearrange("(p c) -> p c", p=BP)).then_inc(s_pad, 16)
                    sp.dma_start(dst_lin[1:1 + E].rearrange("(p c) -> p c", p=BP),
                                 dst.rearrange("(p c) -> p c", p=BP)).then_inc(s_pad, 16)
                    sp.wait_ge(s_const, 1)
                    sp.dma_start(src_lin[E:E + CAP].unsqueeze(0), pad_i[:, 0, 0:CAP]).then_inc(s_pad, 16)
                    sp.dma_start(dst_lin[1 + E:E + CAP + 2].unsqueeze(0),
                                 pad_i[:, 1, 0:CAP + 1]).then_inc(s_pad, 16)
                    sp.dma_start(dst_lin[0:1].unsqueeze(0), pad_i[:, 1, 0:1]).then_inc(s_pad, 16)
                    for w, l in ((gw1, 0), (gw2, 1)):
                        sp.dma_start(wg[:, l], w.rearrange("(c p) n -> p c n", p=P)).then_inc(s_w, 16)
                    sp.dma_start(wcat[:, :, 0:D], aw1.rearrange("(c p) n -> p c n", p=P)).then_inc(s_w, 16)
                    sp.dma_start(wcat[:, :, D:2 * D], aw2.rearrange("(c p) n -> p c n", p=P)).then_inc(s_w, 16)
                    sp.dma_start(wu_s[:], wu.rearrange("(c p) n -> p c n", p=P)).then_inc(s_w, 16)
                    for to, of in ((bg[:, 0], gb1), (bg[:, 1], gb2), (gam[:], gamma), (bet[:], beta),
                                   (bu_s[:], bu),
                                   (arow[:, 0, 0:D], as1.rearrange("h c -> (h c)")),
                                   (arow[:, 0, D:2 * D], as2.rearrange("h c -> (h c)")),
                                   (arow[:, 1, 0:D], ad1.rearrange("h c -> (h c)")),
                                   (arow[:, 1, D:2 * D], ad2.rearrange("h c -> (h c)"))):
                        sp.dma_start(to, of.partition_broadcast(P)).then_inc(s_w, 16)
                    with nc.allow_non_contiguous_dma(reason="biases with features on partitions, once"):
                        sp.dma_start(abT[:, 0:2], ab1.rearrange("(c p) -> p c", p=P)).then_inc(s_w, 16)
                        sp.dma_start(abT[:, 2:4], ab2.rearrange("(c p) -> p c", p=P)).then_inc(s_w, 16)
                    sp.wait_ge(s_sc, 1)
                    with nc.allow_non_contiguous_dma(reason="a scale per node, once"):
                        sp.dma_start(sout_d.rearrange("b p -> p b"), sout[:]).then_inc(s_pd, 16)
                    for b in range(0, BLOCKS, UNROLL):
                        sp.wait_ge(s_t1, b + UNROLL)
                        sp.dma_start(table[0][b * BP:(b + UNROLL) * BP, :].rearrange("(b p) d -> p b d", p=BP),
                                     x_all[:, b:b + UNROLL, :]).then_inc(s_st1, 16)
                    sp.wait_ge(s_plan, 1)
                    sp.dma_start(plan_d.unsqueeze(0), plan_f[:]).then_inc(s_pd, 16)
                    sp.wait_ge(s_st1, 16 * (BLOCKS // UNROLL))
                    sp.wait_ge(s_pd, 32)
                    sp.wait_ge(s_pad, 16 * 5)
                    sp.sem_inc(s_go[0], 1)

                @block.gpsimd
                def _(pool):
                    pool.memset(pad_i[:, 0, :], 0)
                    pool.memset(pad_i[:, 1, :], NOWHERE).then_inc(s_const, 1)
                    pool.iota(iota_r[:], [[1, BP], [0, PC]], base=0, channel_multiplier=0,
                              allow_small_or_imprecise_dtypes=True).then_inc(s_const, 1)
                    pool.iota(iotas[:], [[1, NCH * BLOCKS]], base=0, channel_multiplier=0,
                              allow_small_or_imprecise_dtypes=True)
                    pool.iota(iota_v[:], [[1, BP]], base=0, channel_multiplier=0,
                              allow_small_or_imprecise_dtypes=True)
                    pool.iota(lim[:], [[2 * BP, BLOCKS - 1]], base=2 * BP - 1, channel_multiplier=0,
                              allow_small_or_imprecise_dtypes=True)
                    pool.memset(ones[:], 1.0)
                    pool.memset(ident[:], 0.0).then_inc(s_const, 1)
                    pool.wait_ge(s_const, 3)
                    pool.affine_select(ident[:], ident[:], pattern=[[-1, P]], compare_op=ALU.not_equal,
                                       fill=1.0, base=0, channel_multiplier=1).then_inc(s_const, 1)

                @block.vector
                def _(dve):
                    ch = Chain(dve, s_dve)
                    dve.wait_ge(s_ld, 32)
                    dve.tensor_copy(dst_f[:], dst_i[:]).then_inc(s_df1, 1)
                    ch.step(dve.tensor_copy(src_f[:], src_i[:]))
                    ch.step(dve.tensor_scalar(low_f[:], src_f[:], -float(BP // 2), 1.0 / BP, ALU.add, ALU.mult))
                    ch.step(dve.tensor_scalar(low_f[:], low_f[:], ROUND, None, ALU.add))
                    ch.step(dve.tensor_scalar(low_f[:], low_f[:], -ROUND, None, ALU.add))
                    ch.step(dve.tensor_copy(high_b[:], low_f[:]))
                    ch.step(dve.scalar_tensor_tensor(low_b[:], low_f[:], -float(BP), src_f[:], ALU.mult, ALU.add))
                    dve.wait_ge(s_const, 4)
                    for c in range(25):
                        cs = slice(c * PC, (c + 1) * PC)
                        if c >= 2:
                            dve.wait_ge(s_hm, c - 1)
                        dve.tensor_tensor(oh_lo[:, c % 2], iota_r[:],
                                          low_b[:, cs].unsqueeze(1).to_broadcast([BP, BP, PC]),
                                          ALU.is_equal)
                        dve.tensor_tensor(oh_hi[:, c % 2], iota_r[:, 0:BLOCKS],
                                          high_b[:, cs].unsqueeze(1).to_broadcast([BP, BLOCKS, PC]),
                                          ALU.is_equal).then_inc(s_h1, 1)
                        if c == XB:
                            dve.wait_ge(s_x, 16)
                        for b in ((c - XB) * 2, (c - XB) * 2 + 1):
                            if 0 <= b < BLOCKS:
                                last = dve.bn_stats(stats[:, b], x_all[:, b])
                    ch.step(last)
                    for b in range(BLOCKS):
                        last = dve.bn_aggr(mv[:, b], stats[:, b])
                    ch.step(last)
                    dve.tensor_scalar(rstd[:], mv[:, :, 1], EPS, None, ALU.add).then_inc(s_sq, 1)
                    dve.wait_ge(s_hm, 25)
                    dve.tensor_scalar(sout[:], pb[0][0:BP, 0:BLOCKS], 1.0, None, ALU.max).then_inc(s_sq, 1)
                    dve.wait_ge(s_rt, 2)
                    ch.step(dve.reciprocal(rstd[:], rstd[:]))
                    ch.step(dve.reciprocal(sout[:], sout[:]))
                    ch.step(dve.tensor_tensor(sc1[:], rstd[:], sout[:], ALU.mult))
                    dve.scalar_tensor_tensor(nb1[:], mv[:, :, 0], -1.0, sc1[:], ALU.mult,
                                             ALU.mult).then_inc(s_sc, 1)
                    dve.wait_ge(s_cnt, 2)
                    st, ln, nch, cum, off = (row[:, i, :] for i in range(5))
                    onerow = row[:, 5, 0:BLOCKS]
                    dve.wait_ge(s_const, 4)
                    dve.memset(onerow, 1.0)
                    dve.memset(st[:, 0:1], 0.0)
                    dve.memset(st[:, BLOCKS:BLOCKS + 1], float(E))
                    ch.step(dve.tensor_scalar(st[:, 1:BLOCKS], pb[1][0:1, 0:BLOCKS - 1], float(E), 0.5,
                                              ALU.add, ALU.mult))
                    ch.step(dve.tensor_tensor(ln[:, 0:BLOCKS], st[:, 1:BLOCKS + 1], st[:, 0:BLOCKS],
                                              ALU.subtract))
                    M = E // CAP
                    caps = grid[:, 0:M]
                    ch.step(dve.tensor_scalar(caps, iotas[:, 1:1 + M], float(CAP), None, ALU.mult))
                    g2 = grid[:, M:M + BLOCKS * M].rearrange("p (b m) -> p b m", m=M)
                    ch.step(dve.tensor_tensor(g2, ln[:, 0:BLOCKS].unsqueeze(2).to_broadcast([1, BLOCKS, M]),
                                              caps.unsqueeze(1).to_broadcast([1, BLOCKS, M]), ALU.is_gt))
                    ch.step(dve.tensor_reduce(nch[:, 0:BLOCKS], g2, AX.X, ALU.add))
                    ch.step(dve.tensor_scalar(nch[:, 0:BLOCKS], nch[:, 0:BLOCKS], 1.0, None, ALU.add))
                    ch.step(dve.tensor_tensor_scan(cum[:, 0:BLOCKS], onerow, nch[:, 0:BLOCKS], 0.0,
                                                   ALU.mult, ALU.add))
                    gk = grid[:, 0:NCH * (BLOCKS - 1)].rearrange("p (k b) -> p k b", k=NCH)
                    kk = iotas[:, 0:NCH]
                    ch.step(dve.tensor_tensor(gk, kk.unsqueeze(2).to_broadcast([1, NCH, BLOCKS - 1]),
                                              cum[:, 0:BLOCKS - 1].unsqueeze(1).to_broadcast([1, NCH, BLOCKS - 1]),
                                              ALU.is_ge))
                    blk = pl[:, 0, :]
                    ch.step(dve.tensor_reduce(blk, gk, AX.X, ALU.add))
                    ch.step(dve.tensor_tensor(off[:, 0:BLOCKS], nch[:, 0:BLOCKS], cum[:, 0:BLOCKS], ALU.subtract))
                    ch.step(dve.scalar_tensor_tensor(off[:, 0:BLOCKS], off[:, 0:BLOCKS], float(CAP),
                                                     st[:, 0:BLOCKS], ALU.mult, ALU.add))
                    gb = grid[:, 0:NCH * BLOCKS].rearrange("p (k b) -> p k b", k=NCH)
                    ch.step(dve.tensor_tensor(gb, blk.unsqueeze(2).to_broadcast([1, NCH, BLOCKS]),
                                              iotas[:, 0:BLOCKS].unsqueeze(1).to_broadcast([1, NCH, BLOCKS]),
                                              ALU.is_equal))
                    ch.step(dve.tensor_tensor(gb, gb, off[:, 0:BLOCKS].unsqueeze(1).to_broadcast([1, NCH, BLOCKS]),
                                              ALU.mult))
                    base = pl[:, 1, :]
                    ch.step(dve.tensor_reduce(base, gb, AX.X, ALU.add))
                    ch.step(dve.scalar_tensor_tensor(base, kk, float(CAP), base, ALU.mult, ALU.add))
                    ch.step(dve.tensor_scalar(base, base, float(E), None, ALU.min))
                    goes, first = plan_f[:, :, 0], plan_f[:, :, 1]
                    ch.step(dve.memset(goes, 0.0))
                    ch.step(dve.tensor_tensor(goes[:, 1:NCH], blk[:, 1:NCH], blk[:, 0:NCH - 1], ALU.is_equal))
                    ch.step(dve.tensor_scalar(first, blk, float(BP), None, ALU.mult))
                    ch.step(dve.tensor_copy(plan_i[:, 0, :], base))
                    ch.step(dve.tensor_copy(plan_i[:, 1, :], first))
                    T = MAXCH // UNROLL
                    g5 = pl[:, 2, 0:T]
                    ch.step(dve.tensor_scalar(g5, iotas[:, 0:T], float(UNROLL), cum[:, BLOCKS - 1:BLOCKS],
                                              ALU.mult, ALU.is_lt))
                    ch.step(dve.tensor_reduce(pl[:, 3, 0:1], g5, AX.X, ALU.add))
                    ch.step(dve.tensor_scalar(pl[:, 3, 1:2], pl[:, 3, 0:1], -1.0, None, ALU.add))
                    dve.tensor_copy(niter_i[:], pl[:, 3, 0:2]).then_inc(s_plan, 1)

                @block.scalar
                def _(act):
                    act.wait_ge(s_const, 4)
                    act.wait_ge(s_df1, 1)
                    for b in range(BLOCKS - 1):
                        act.activation(junk[:], dst_f[:], ACT.Sign, bias=lim[:, b:b + 1], scale=-2.0,
                                       accum_out=cnt[:, b:b + 1]).then_inc(s_ac, 1)
                        act.wait_ge(s_ac, b + 1)
                    act.sem_inc(s_cnt, 1)
                    for n, v in enumerate((rstd, sout)):
                        act.wait_ge(s_sq, n + 1)
                        act.activation(v[:], v[:], ACT.Sqrt).then_inc(s_rt, 1)
                    act.wait_ge(s_sc, 1)
                    for b in range(BLOCKS):
                        act.activation(x_all[:, b], x_all[:, b], ACT.Relu, bias=nb1[:, b:b + 1],
                                       scale=sc1[:, b:b + 1]).then_inc(s_t1, 1)

                @block.tensor
                def _(pe):
                    for c in range(25):
                        pe.wait_ge(s_h1, c + 1)
                        for j in range(PC):
                            last = pe.matmul(pb[0][0:BP, 0:BLOCKS], oh_lo[:, c % 2, :, j], oh_hi[:, c % 2, :, j],
                                             start=(c == 0 and j == 0), stop=(c == 24 and j == PC - 1))
                        last.then_inc(s_hm, 1)
                    pe.wait_ge(s_const, 4)
                    pe.wait_ge(s_cnt, 1)
                    pe.matmul(pb[1][0:1, 0:BLOCKS - 1], ones[0:BP, 0:1], cnt[:, 0:BLOCKS - 1],
                              start=True, stop=True).then_inc(s_cnt, 1)

        def load_record(sp, f, k, u, own):
            base = sp.value_load(plan_i[0:1, 0, bass.ds(k, 1)], min_val=0, max_val=E)
            node = sp.value_load(plan_i[0:1, 1, bass.ds(k, 1)], min_val=0, max_val=N - BP)
            sp.dma_start(idx[:, u], bass.AP(src_lin.tensor, base, [[TILES, P], [1, TILES]])).then_inc(f.rec[u], 16)
            sp.dma_start(dwin[:, u], bass.AP(dst_lin.tensor, base, [[TILES, P], [1, TILES + 2]])).then_inc(f.rec[u], 16)
            sp.dma_start(cb[:, u], bass.AP(plan_d.tensor, k * 2, [[0, P], [1, 2]])).then_inc(f.rec[u], 16)
            own(sp, f, node, u)

        def sp_phase(sp, f, own, store, nst):
            n = sp.value_load(niter_i[0:1, 0:1], min_val=UNROLL, max_val=MAXCH // UNROLL)
            for k in range(AHEAD):
                load_record(sp, f, k, k, own)
            sp.sem_inc(f.free, 1)
            with sp.Fori(0, n) as it:
                for u in range(UNROLL):
                    k = it * UNROLL + u
                    load_record(sp, f, k + AHEAD, (u + AHEAD) % UNROLL, own)
                    node = sp.value_load(plan_i[0:1, 1, bass.ds(k, 1)], min_val=0, max_val=N - BP)
                    sp.wait_ge(f.fin, k + 1)
                    store(sp, f, node)
                    sp.wait_ge(f.st, (k + 1) * 16 * nst)
                    sp.sem_inc(f.free, 1)
            for u in range(AHEAD):
                sp.wait_ge(f.rec[u], (n + 1) * 16 * NREC[f.i])
            if f.i < 2:
                sp.sem_inc(s_go[f.i + 1], 1)
            else:
                sp.sem_inc(s_gate, 1)

        def pool_phase(pool, f):
            width = D if f.i < 2 else ROW3
            n = pool.value_load(niter_i[0:1, 0:1], min_val=UNROLL, max_val=MAXCH // UNROLL)
            pool.wait_ge(s_go[f.i], 1)
            with pool.Fori(0, n) as it:
                for u in range(UNROLL):
                    pool.wait_ge(f.rec[u], (it + 1) * 16 * NREC[f.i])
                    for g in range(2):
                        q = 2 * u + g
                        pool.wait_ge(f.used, it * (2 * UNROLL) + q + 1)
                        pool.sem_inc(s_gate, 1)
                        for j in range(HALF):
                            t = g * HALF + j
                            pool.indirect_dma_start(
                                ring[:, q % SLOTS, j * width:(j + 1) * width], None, table[f.i],
                                bass.IndirectOffsetOnAxis(idx[:, u, t:t + 1], 0)).then_inc(f.rows[q % SLOTS], 16)

        def rows_wait(eng, f, it, q):
            eng.wait_ge(f.rows[q % SLOTS], (it * 2 + (q // SLOTS + 1)) * 16 * HALF)

        def make_hot(dve, f, it, u):
            for g in range(2):
                q = 2 * u + g
                dve.wait_ge(f.used, it * (2 * UNROLL) + q + 1)
                dve.tensor_tensor(hot[:, q % SLOTS], iota_v[:].unsqueeze(1).to_broadcast([P, HALF, BP]),
                                  dwf[:, 1 + g * HALF:1 + (g + 1) * HALF].unsqueeze(2).to_broadcast([P, HALF, BP]),
                                  ALU.is_equal).then_inc(f.hot, 1)

        phase_b = ExitStack()
        def sbb(name, shape, dt=F32):
            return phase_b.enter_context(nc.sbuf_tensor(name, shape, dt))
        with phase_b:
            xrow = sbb("xrow", [P, UNROLL, D])
            aggT = sbb("aggT", [P, 2, BP])
            deg = sbb("deg", [P, 1])
            s_in = sbb("s_in", [P, 1])
            part = sbb("part", [P, 2, BP])
            zt = sbb("zt", [P, D])
            row12 = sbb("row12", [P, D])
            x2 = sbb("x2", [P, D])
            h2 = sbb("h2", [P, D])
            xn = sbb("xn", [P, D])
            xnT = sbb("xnT", [P, 2, BP])
            row3 = sbb("row3", [P, ROW3])
            rowS = sbb("rowS", [P, SIDE])
            prod = sbb("prod", [P, 2, 2 * D])
            bst = sbb("bst", [P, 6])
            bmv = sbb("bmv", [P, 2])
            brs = sbb("brs", [P, 2])
            s_wa = sem("s_wa")
            s_xn = sem("s_xn")
            s_xt = sem("s_xt")
            s_xc = sem("s_xc")
            s_H = sem("s_H")
            s_rs = sem("s_rs")

            LINKS = [5, 19]
            ROOTS = [1, 3]

            def inv_root(dve, ch, f, count, v, ins):
                ins.then_inc(f.sq, 1)
                dve.wait_ge(f.rt, count)
                ch.step(dve.reciprocal(v, v))

            def root(act, f, count, v):
                act.wait_ge(f.sq, count)
                act.activation(v, v, ACT.Sqrt).then_inc(f.rt, 1)

            def gcn_hot(dve, ch, f, it, u):
                dve.wait_ge(f.rec[u], (it + 1) * 16 * NREC[f.i])
                ch.step(dve.tensor_scalar(dwf[:], dwin[:, u], cb[:, u, 1:2], None, ALU.subtract))
                make_hot(dve, f, it, u)

            def gcn_counts(dve, f, it, u):
                dve.wait_ge(f.hot, it * (2 * UNROLL) + 2 * u + 2)
                for g in range(2):
                    last = dve.tensor_reduce(part[:, g], hot[:, (2 * u + g) % SLOTS].rearrange("p j v -> p v j"),
                                             AX.X, ALU.add)
                last.then_inc(f.hc, 1)

            def gcn_vector(dve, f, it, u):
                k = it * UNROLL + u
                ch = Chain(dve, f.dve, 1 + k * LINKS[f.i])
                ahead = (it + (u + 1) // UNROLL, (u + 1) % UNROLL)
                gcn_hot(dve, ch, f, *ahead)
                goes = cb[:, u, 0:1]
                dve.wait_ge(f.used, k * 2 + 2 + SLOTS)
                for h in range(2):
                    last = dve.scalar_tensor_tensor(aggT[:, h], aggT[:, h], goes, pb[h][:, 0:BP],
                                                    ALU.mult, ALU.add)
                last.then_inc(f.acc, 1)
                dve.wait_ge(f.dg, k + 1)
                ch.step(dve.scalar_tensor_tensor(deg[0:BP], deg[0:BP], goes[0:BP], pb[2][0:BP, 0:1],
                                                 ALU.mult, ALU.add))
                inv_root(dve, ch, f, k * ROOTS[f.i] + 1, s_in[0:BP],
                         dve.tensor_scalar(s_in[0:BP], deg[0:BP], 1.0, None, ALU.max))
                gcn_counts(dve, f, *ahead)
                dve.wait_ge(f.z, k + 1)
                dve.wait_ge(f.free, k + 1)
                if f.i == 0:
                    ch.step(dve.scalar_tensor_tensor(zt[0:BP], pb[3][0:BP, 0:D], s_in[0:BP], bg[0:BP, 0],
                                                     ALU.mult, ALU.add))
                    ch.step(dve.tensor_scalar(row12[0:BP], zt[0:BP], 0.0, sout_c[0:BP, u:u + 1],
                                              ALU.max, ALU.mult))
                    dve.sem_inc(f.fin, 1)
                    assert ch.n == LINKS[0], ch.n
                    return
                ch.step(dve.scalar_tensor_tensor(zt[0:BP], pb[3][0:BP, 0:D], s_in[0:BP], bg[0:BP, 1],
                                                 ALU.mult, ALU.add))
                ch.step(dve.scalar_tensor_tensor(x2[0:BP], zt[0:BP], 0.0, xrow[0:BP, u], ALU.max, ALU.add))
                ch.step(dve.bn_stats(bst[0:BP], x2[0:BP]))
                dve.sem_inc(s_gate, 1)
                ch.step(dve.bn_aggr(bmv[0:BP], bst[0:BP]))
                inv_root(dve, ch, f, k * ROOTS[f.i] + 2, brs[0:BP, 0:1],
                         dve.tensor_scalar(brs[0:BP, 0:1], bmv[0:BP, 1:2], EPS, None, ALU.add))
                ch.step(dve.scalar_tensor_tensor(brs[0:BP, 1:2], bmv[0:BP, 0:1], -1.0, brs[0:BP, 0:1],
                                                 ALU.mult, ALU.mult))
                ch.step(dve.tensor_scalar(zt[0:BP], x2[0:BP], brs[0:BP, 0:1], brs[0:BP, 1:2], ALU.mult, ALU.add))
                ch.step(dve.tensor_scalar(h2[0:BP], zt[0:BP], 0.0, None, ALU.max))
                ch.step(dve.tensor_tensor(x2[0:BP], x2[0:BP], h2[0:BP], ALU.add))
                ch.step(dve.bn_stats(bst[0:BP], h2[0:BP]))
                dve.sem_inc(s_gate, 1)
                ch.step(dve.bn_aggr(bmv[0:BP], bst[0:BP]))
                inv_root(dve, ch, f, k * ROOTS[f.i] + 3, brs[0:BP, 0:1],
                         dve.tensor_scalar(brs[0:BP, 0:1], bmv[0:BP, 1:2], EPS, None, ALU.add))
                ch.step(dve.tensor_scalar(xn[0:BP], h2[0:BP], bmv[0:BP, 0:1], brs[0:BP, 0:1],
                                          ALU.subtract, ALU.mult))
                ch.step(dve.tensor_tensor(xn[0:BP], xn[0:BP], gam[0:BP], ALU.mult))
                ch.step(dve.tensor_tensor(xn[0:BP], xn[0:BP], bet[0:BP], ALU.add))
                dve.sem_inc(s_xn, 1)
                ch.step(dve.tensor_tensor(rowS[0:BP, HEADS:SIDE], x2[0:BP], bu_s[0:BP], ALU.add))
                dve.sem_inc(s_rs, 1)
                assert ch.n == LINKS[1], ch.n

            def gcn_project(pe, k):
                pe.wait_ge(s_xn, k + 1)
                for h in range(2):
                    last = pe.transpose(pb[4][:, h * P:h * P + BP], xn[0:BP, h * P:(h + 1) * P],
                                        ident[0:BP, 0:BP])
                last.then_inc(s_xt, 1)
                pe.wait_ge(s_xc, k + 1)
                for h in range(2):
                    pe.matmul(pb[5][0:BP, :], xnT[:, h], wcat[:, h, 0:2 * D], start=(h == 0), stop=(h == 1))
                for h in range(2):
                    last = pe.matmul(pb[6][0:BP, 0:2 * HEADS], xnT[:, h], wcat[:, h, 2 * D:WC],
                                     start=(h == 0), stop=(h == 1))
                last.then_inc(s_H, 1)

            def gcn_tensor(pe, f, it, u, first=False):
                k = it * UNROLL + u
                for g in range(2):
                    q = 2 * u + g
                    pe.wait_ge(f.hot, it * (2 * UNROLL) + q + 1)
                    rows_wait(pe, f, it, q)
                    for j in range(HALF):
                        a, z = (g == 0 and j == 0), (g == 1 and j == HALF - 1)
                        for h in range(2):
                            lo = j * D + h * P
                            last = pe.matmul(pb[h][:, 0:BP], ring[:, q % SLOTS, lo:lo + P],
                                             hot[:, q % SLOTS, j, :], start=a, stop=z)
                    last.then_inc(f.used, 1)
                    if f.i == 1 and g == 0 and not first:
                        gcn_project(pe, k - 1)
                pe.wait_ge(f.hc, k + 1)
                for g in range(2):
                    last = pe.matmul(pb[2][0:BP, 0:1], part[:, g], ones[:, 0:1], start=(g == 0), stop=(g == 1))
                last.then_inc(f.dg, 1)
                pe.wait_ge(f.acc, k + 1)
                for h in range(2):
                    last = pe.matmul(pb[3][0:BP, 0:D], aggT[:, h], wg[:, f.i, h], start=(h == 0), stop=(h == 1))
                last.then_inc(f.z, 1)

            def gcn2_scalar(act, f, it, u):
                k = it * UNROLL + u
                root(act, f, k * ROOTS[1] + 1, s_in[0:BP])
                root(act, f, k * ROOTS[1] + 2, brs[0:BP, 0:1])
                root(act, f, k * ROOTS[1] + 3, brs[0:BP, 0:1])
                act.wait_ge(s_xt, k + 1)
                act.copy(xnT[:], pb[4][:, 0:2 * P].rearrange("p (h n) -> p h n", h=2)[:, :, 0:BP]).then_inc(s_xc, 1)
                act.wait_ge(s_H, k + 1)
                act.wait_ge(f.free, k + 1)
                act.copy(row3[0:BP, 0:2 * D], pb[5][0:BP, :])
                act.copy(row3[0:BP, 2 * D:ROW3], pb[6][0:BP, 0:HEADS])
                act.copy(rowS[0:BP, 0:HEADS], pb[6][0:BP, HEADS:2 * HEADS]).then_inc(f.t, 1)
                act.wait_ge(f.t, k + 1)
                act.wait_ge(s_rs, k + 1)
                act.sem_inc(f.fin, 1)

            def own1(sp, f, node, u):
                sp.dma_start(sout_c[0:BP, u:u + 1],
                             bass.AP(sout_d.tensor, node, [[1, BP], [1, 1]])).then_inc(f.rec[u], 16)

            def own2(sp, f, node, u):
                sp.dma_start(xrow[0:BP, u], x[bass.ds(node, BP), :]).then_inc(f.rec[u], 16)

            def store1(sp, f, node):
                sp.dma_start(table[1][bass.ds(node, BP), :], row12[0:BP]).then_inc(f.st, 16)

            def store2(sp, f, node):
                sp.dma_start(table[2][bass.ds(node, BP), :], row3[0:BP]).then_inc(f.st, 16)
                sp.dma_start(side_d[bass.ds(node, BP), :], rowS[0:BP]).then_inc(f.st, 16)

            with nc.Block() as block:
                @block.sync
                def _(sp):
                    sp_phase(sp, ph[0], own1, store1, 1)
                    sp_phase(sp, ph[1], own2, store2, 2)

                @block.gpsimd
                def _(pool):
                    pool_phase(pool, ph[0])
                    pool_phase(pool, ph[1])

                @block.vector
                def _(dve):
                    n = dve.value_load(niter_i[0:1, 0:1], min_val=UNROLL, max_val=MAXCH // UNROLL)
                    dve.memset(aggT[:], 0.0)
                    dve.memset(deg[:], 0.0)
                    dve.wait_ge(s_w, 16 * 16)
                    cw = Chain(dve, s_wa)
                    for c in range(2):
                        for s in range(2):
                            cw.step(dve.tensor_tensor(prod[:, s], wcat[:, c, 0:2 * D], arow[:, s], ALU.mult))
                            lo = 2 * D + s * HEADS
                            for twin in range(2):
                                dve.tensor_reduce(wcat[:, c, lo + twin:lo + 2 * H1:2],
                                                  prod[:, s, 0:D].rearrange("p (h k) -> p h k", k=C1),
                                                  AX.X, ALU.add)
                            cw.step(dve.tensor_reduce(wcat[:, c, lo + 2 * H1:lo + HEADS],
                                                      prod[:, s, D:2 * D].rearrange("p (h k) -> p h k", k=C2),
                                                      AX.X, ALU.add))
                    dve.wait_ge(s_go[0], 1)
                    for f in ph[0:2]:
                        if f.i == 1:
                            dve.wait_ge(ph[0].hot, n * (2 * UNROLL) + 2)
                            dve.wait_ge(ph[0].hc, n * UNROLL + 1)
                        gcn_hot(dve, Chain(dve, f.dve), f, 0, 0)
                        gcn_counts(dve, f, 0, 0)
                        with dve.Fori(0, n) as it:
                            for u in range(UNROLL):
                                gcn_vector(dve, f, it, u)

                @block.tensor
                def _(pe):
                    n = pe.value_load(niter_i[0:1, 0:1], min_val=UNROLL, max_val=MAXCH // UNROLL)
                    for f in ph[0:2]:
                        pe.sem_inc(f.used, SLOTS)
                        for u in range(UNROLL):
                            gcn_tensor(pe, f, 0, u, first=(u == 0))
                        with pe.Fori(1, n) as it:
                            for u in range(UNROLL):
                                gcn_tensor(pe, f, it, u)
                    gcn_project(pe, n * UNROLL - 1)

                @block.scalar
                def _(act):
                    n = act.value_load(niter_i[0:1, 0:1], min_val=UNROLL, max_val=MAXCH // UNROLL)
                    with act.Fori(0, n) as it:
                        for u in range(UNROLL):
                            root(act, ph[0], it * UNROLL + u + 1, s_in[0:BP])
                    with act.Fori(0, n) as it:
                        for u in range(UNROLL):
                            gcn2_scalar(act, ph[1], it, u)

        phase_c = ExitStack()
        def sc(name, shape, dt=F32):
            return phase_c.enter_context(nc.sbuf_tensor(name, shape, dt))
        with phase_c:
            f = ph[2]
            hotb = sc("hotb", [P, SLOTS, BP, HALF], BF16)
            iota_b = sc("iota_b", [P, BP, HALF], BF16)
            dwb = sc("dwb", [P, TILES], BF16)
            hotT = sc("hotT", [BP, TILES, P], BF16)
            iden_b = sc("iden_b", [P, P], BF16)
            dwa = sc("dwa", [P, TILES + 2])
            same = sc("same", [P, TILES + 1])
            fr = sc("fr", [P, TILES])
            frp = sc("frp", [P, TILES])
            lastf = sc("lastf", [P, TILES])
            endc = sc("endc", [P, TILES])
            notp0 = sc("notp0", [P, 1])
            cc = sc("cc", [P, 2])
            pen = sc("pen", [P, HEADS, TILES])
            ash = sc("ash", [P, HEADS, TILES])
            pre = sc("pre", [P, HEADS, TILES])
            cpk = sc("cpk", [P, 3, HEADS])
            cpT = sc("cpT", [HEADS, 3, P])
            car = sc("car", [HEADS, P])
            cin = sc("cin", [HEADS, P])
            fl = sc("fl", [P, TILES, HEADS + 1])
            tmp = sc("tmp", [P, TILES * (HEADS + 1)])
            mx = sc("mx", [P, HEADS])
            hp = sc("hp", [P, 2])
            lk = sc("lk", [P, 3, HEADS])
            dif = sc("dif", [P, 2, HEADS])
            rr = sc("rr", [P, 2 * HEADS])
            rb = sc("rb", [P, 3, 2 * HEADS], BF16)
            et = sc("et", [P, TILES, HEADS])
            ex = sc("ex", [P, UNROLL, TILES, HEADS])
            ab5 = sc("ab5", [P, UNROLL, 2, HEADS])
            den = sc("den", [P, HEADS])
            dsum = sc("dsum", [P, HEADS])
            rd = sc("rd", [P, HEADS])
            acc = sc("acc", [P, 2 * D])
            xo = sc("xo", [P, 2 * D])
            nabT = sc("nabT", [P, 4])
            pos = sc("pos", [P, 4, BP])
            neg = sc("neg", [P, 4, BP])
            xcT = sc("xcT", [P, 4, BP])
            res = sc("res", [P, D])
            self_h = sc("self_h", [P, UNROLL, ROW3])
            side_c = sc("side_c", [P, UNROLL, SIDE])
            pb4b = pb[4][:, :].bitcast(BF16)
            s_dc = sem("s_dc")
            s_nf = sem("s_nf")
            NUMB = [0, 1, 0, 1, 2]
            s_c3 = sem("s_c3")
            s_hb = sem("s_hb")
            s_ot = sem("s_ot")
            s_oc = sem("s_oc")
            s_cp = sem("s_cp")
            s_tp = sem("s_tp")
            s_tc = sem("s_tc")
            s_ci = sem("s_ci")
            s_tb = sem("s_tb")
            s_fl = sem("s_fl")
            s_mx = sem("s_mx")
            s_r3 = sem("s_r3")
            s_bc = sem("s_bc")
            s_df = sem("s_df")
            s_ab = sem("s_ab")
            s_et = sem("s_et")
            s_ex = sem("s_ex")
            s_ms = sem("s_ms")
            s_xr = sem("s_xr")
            s_xt = sem("s_xt2")
            s_ng = sem("s_ng")
            s_el = sem("s_el")
            s_xc = sem("s_xc2")
            s_u = sem("s_u")

            def wide(ap):
                return ap.rearrange("p (h c) -> p h c", h=HEADS)

            def over(ap, n=HW):
                return ap.unsqueeze(2).to_broadcast([ap.shape[0], HEADS, n])

            def edge_hot(dve, ch, it, u):
                dve.wait_ge(f.rec[u], (it + 1) * 16 * NREC[2])
                dve.tensor_scalar(dwa[:], dwin[:, u], cb[:, u, 1:2], None, ALU.subtract)
                ch.step(dve.tensor_scalar(dwb[:], dwin[:, u, 1:TILES + 1], cb[:, u, 1:2], None, ALU.subtract))
                for g in range(2):
                    q = 2 * u + g
                    dve.wait_ge(f.used, it * (2 * UNROLL) + q + 1)
                    dve.tensor_tensor(hotb[:, q % SLOTS], iota_b[:],
                                      dwb[:, g * HALF:(g + 1) * HALF].unsqueeze(1).to_broadcast([P, BP, HALF]),
                                      ALU.is_equal).then_inc(s_hb, 1)

            def edge_flags(dve, ch):
                ch.step(dve.tensor_tensor(same[:], dwa[:, 0:TILES + 1], dwa[:, 1:TILES + 2], ALU.is_equal))
                ch.step(dve.tensor_scalar(fr[:], dwa[:, 1:TILES + 1], dwa[:, 1:2], None, ALU.is_equal))
                ch.step(dve.tensor_tensor(cc[:, 1:2], same[:, 0:1], notp0[:], ALU.mult))
                ch.step(dve.tensor_tensor(cc[:, 0:1], cc[:, 1:2], fr[:, TILES - 1:TILES], ALU.mult))
                dve.tensor_scalar(cpk[:, 1:3], cc[:].unsqueeze(2).to_broadcast([P, 2, HEADS]), -1.0, BIG,
                                  ALU.add, ALU.mult)
                dve.tensor_scalar(pen[:, :, 1:TILES],
                                  same[:, 1:TILES].unsqueeze(1).to_broadcast([P, HEADS, TILES - 1]), -1.0, BIG,
                                  ALU.add, ALU.mult)
                dve.tensor_scalar(frp[:], fr[:], -1.0, BIG, ALU.add, ALU.mult)
                ch.step(dve.tensor_scalar(lastf[:], same[:, 1:TILES + 1], -1.0, 1.0, ALU.mult, ALU.add))
                ch.step(dve.tensor_tensor(lastf[:], lastf[:], endc[:], ALU.max))

            def run_maxima(dve, ch, it, u):
                for g in range(2):
                    q = 2 * u + g
                    rows_wait(dve, f, it, q)
                    last = dve.tensor_copy(ash[:, :, g * HALF:(g + 1) * HALF],
                                           ring[:, q % SLOTS].rearrange("p (j n) -> p n j", j=HALF)[:, 2 * D:ROW3])
                ch.step(last)
                ch.step(dve.tensor_tensor_scan(pre[:].rearrange("p h j -> p (h j)"),
                                               pen[:].rearrange("p h j -> p (h j)"),
                                               ash[:].rearrange("p h j -> p (h j)"), -BIG, ALU.add, ALU.max))
                dve.tensor_copy(cpk[:, 0], pre[:, :, TILES - 1]).then_inc(s_cp, 1)

            def carry(dve, ch, k):
                dve.wait_ge(s_tc, k + 1)
                ch.step(dve.tensor_tensor_scan(car[:], cpT[:, 1], cpT[:, 0], -BIG, ALU.add, ALU.max))
                dve.tensor_tensor(cin[:, 1:P], car[:, 0:P - 1], cpT[:, 2, 1:P], ALU.add).then_inc(s_ci, 1)

            def whole_runs(dve, ch, k):
                dve.wait_ge(s_tb, k + 1)
                t = tmp[:, 0:HEADS * TILES].rearrange("p (h j) -> p h j", h=HEADS)
                ch.step(dve.tensor_tensor(t, frp[:].unsqueeze(1).to_broadcast([P, HEADS, TILES]),
                                          over(pb[5][:, 384:384 + HEADS], TILES), ALU.add))
                ch.step(dve.tensor_tensor(pre[:], pre[:], t, ALU.max))
                dve.tensor_copy(fl[:, :, HEADS], lastf[:])
                dve.tensor_tensor(fl[:, :, 0:HEADS].rearrange("p j h -> p h j"), pre[:],
                                  lastf[:].unsqueeze(1).to_broadcast([P, HEADS, TILES]), ALU.mult).then_inc(s_fl, 1)

            def leaky(dve, ch, v):
                ch.step(dve.scalar_tensor_tensor(v, v, 0.2, v, ALU.mult, ALU.max))

            def node_maxima(dve, ch, k, u):
                b = slice(0, BP)
                dve.wait_ge(s_mx, k + 1)
                as_self, ad = self_h[b, u, 2 * D:ROW3], side_c[b, u, 0:HEADS]
                ch.step(dve.tensor_scalar(hp[b, 0:1], pb[5][b, 400 + HEADS:401 + HEADS], -1.0, BIG,
                                          ALU.add, ALU.mult))
                ch.step(dve.tensor_scalar(hp[b, 1:2], cb[b, u, 0:1], -1.0, BIG, ALU.add, ALU.mult))
                dve.tensor_tensor(lk[b, 0], mx[b], ad, ALU.add)
                ch.step(dve.scalar_tensor_tensor(lk[b, 1], pb[5][b, 400:400 + HEADS], hp[b, 0:1], as_self,
                                                 ALU.add, ALU.max))
                ch.step(dve.scalar_tensor_tensor(mx[b], mx[b], hp[b, 1:2], lk[b, 1], ALU.add, ALU.max))
                dve.tensor_tensor(lk[b, 1], mx[b], ad, ALU.add)
                ch.step(dve.tensor_tensor(lk[b, 2], as_self, ad, ALU.add))
                leaky(dve, ch, lk[b])
                dve.tensor_copy(rr[b, 0:HEADS], ad)
                ch.step(dve.tensor_copy(rr[b, HEADS:2 * HEADS], lk[b, 1]))
                dve.tensor_tensor(dif[b, 0], lk[b, 0], lk[b, 1], ALU.subtract)
                ch.step(dve.tensor_tensor(dif[b, 1], lk[b, 2], lk[b, 1], ALU.subtract))
                dve.tensor_scalar(dif[b], dif[b], 0.0, None, ALU.min).then_inc(s_df, 1)
                t = tmp[b, 0:2 * HEADS]
                ch.step(dve.tensor_copy(rb[b, 0], rr[b]))
                ch.step(dve.tensor_tensor(t, rr[b], rb[b, 0], ALU.subtract))
                ch.step(dve.tensor_copy(rb[b, 1], t))
                dve.tensor_tensor(rb[b, 2], t, rb[b, 1], ALU.subtract).then_inc(s_r3, 1)

            def edge_weights(dve, ch, k):
                dve.wait_ge(s_bc, k + 1)
                for g in range(2):
                    js = slice(g * HALF, (g + 1) * HALF)
                    b6 = pb[BCB[g]][:, 0:HALF * 2 * HEADS].rearrange("p (j n) -> p j n", j=HALF)
                    last = dve.tensor_tensor(et[:, js], ash[:, :, js].rearrange("p h j -> p j h"),
                                             b6[:, :, 0:HEADS], ALU.add)
                ch.step(last)
                leaky(dve, ch, et[:].rearrange("p j h -> p (j h)"))
                for g in range(2):
                    js = slice(g * HALF, (g + 1) * HALF)
                    b6 = pb[BCB[g]][:, 0:HALF * 2 * HEADS].rearrange("p (j n) -> p j n", j=HALF)
                    last = dve.tensor_tensor(et[:, js], et[:, js], b6[:, :, HEADS:2 * HEADS], ALU.subtract)
                ch.step(last)
                dve.tensor_scalar(et[:], et[:], 0.0, None, ALU.min).then_inc(s_et, 1)

            def weigh(dve, k, u, g):
                dve.wait_ge(s_ex, k + 1)
                v = ring[:, (2 * u + g) % SLOTS].rearrange("p (j n) -> p j n", j=HALF)[:, :, 0:2 * D].rearrange(
                    "p j (h c) -> p j h c", h=HEADS)
                w = ex[:, u, g * HALF:(g + 1) * HALF].unsqueeze(3).to_broadcast([P, HALF, HEADS, HW])
                dve.tensor_tensor(v, v, w, ALU.mult).then_inc(s_ms, 1)

            def read_den(dve, k):
                b = slice(0, BP)
                dve.wait_ge(f.used, k * 2 + 2 + SLOTS)
                dve.tensor_copy(dsum[b], pb[3][b, 0:HEADS]).then_inc(s_dc, 1)
                dve.wait_ge(s_dc, k + 2)

            def node_rows(dve, ch, k, u):
                b = slice(0, BP)
                num = pb[NUMB[u]][b, :]
                al, be = ab5[b, u, 0], ab5[b, u, 1]
                dve.wait_ge(s_ab, k + 1)
                ch.step(dve.tensor_scalar(al, al, cb[b, u, 0:1], None, ALU.mult))
                ch.step(dve.tensor_tensor(den[b], den[b], al, ALU.mult))
                ch.step(dve.tensor_tensor(wide(acc[b]), wide(acc[b]), over(al), ALU.mult))
                ch.step(dve.tensor_tensor(den[b], den[b], dsum[b], ALU.add))
                ch.step(dve.tensor_tensor(acc[b], acc[b], num, ALU.add))
                ch.step(dve.tensor_tensor(wide(xo[b]), wide(self_h[b, u, 0:2 * D]), over(be), ALU.mult))
                dve.sem_inc(s_nf, 1)
                ch.step(dve.scalar_tensor_tensor(rd[b], den[b], 1e-16, be, ALU.add, ALU.add))
                ch.step(dve.reciprocal(rd[b], rd[b]))
                ch.step(dve.tensor_tensor(xo[b], xo[b], acc[b], ALU.add))
                dve.tensor_tensor(wide(xo[b]), wide(xo[b]), over(rd[b]), ALU.mult).then_inc(s_xr, 1)

            def elu(dve, k):
                dve.wait_ge(s_el, k + 1)
                dve.scalar_tensor_tensor(xcT[:], neg[:], -1.0, pos[:], ALU.add, ALU.add).then_inc(s_xc, 1)

            def result(dve, k, u):
                b = slice(0, BP)
                dve.wait_ge(s_u, k + 1)
                dve.wait_ge(f.free, k + 1)
                dve.tensor_tensor(res[b], pb[7][b, 0:D], side_c[b, u, HEADS:SIDE], ALU.add).then_inc(f.fin, 1)

            def at(it, u, d):
                return it + (u + d) // UNROLL, (u + d) % UNROLL

            def gat_vector(dve, ch, it, u, first=False, last=0):
                k = it * UNROLL + u
                weigh(dve, k, u, 0)
                if last < 2:
                    run_maxima(dve, ch, *at(it, u, 1))
                if not first:
                    read_den(dve, k - 1)
                weigh(dve, k, u, 1)
                if last < 2:
                    carry(dve, ch, k + 1)
                if not first:
                    node_rows(dve, ch, k - 1, (u - 1) % UNROLL)
                if last < 2:
                    whole_runs(dve, ch, k + 1)
                if last == 0:
                    edge_hot(dve, ch, *at(it, u, 2))
                    edge_flags(dve, ch)
                if last < 2:
                    node_maxima(dve, ch, k + 1, (u + 1) % UNROLL)
                if not first:
                    elu(dve, k - 1)
                if last < 2:
                    edge_weights(dve, ch, k + 1)
                if not first:
                    result(dve, k - 1, (u - 1) % UNROLL)

            BCB = [6, 4]

            def turn_hot(pe, it, u, m):
                k = it * UNROLL + u
                for j in range(6 * m, 6 * m + 6):
                    g = j // HALF
                    if j == 0 or j == HALF or j == 6 * m:
                        pe.wait_ge(s_hb, it * 2 * UNROLL + 2 * u + g + 1)
                    if j == 0:
                        pe.wait_ge(s_et, k + 1)
                    if j == 6 * m:
                        pe.wait_ge(s_oc, 3 * k + m + 1)
                    last = pe.transpose(pb4b[0:BP, (j % 6) * P:(j % 6 + 1) * P],
                                        hotb[:, (2 * u + g) % SLOTS, :, j % HALF], iden_b[:])
                last.then_inc(s_ot, 1)

            def turn_last(pe, k):
                pe.wait_ge(s_cp, k + 1)
                for i in range(3):
                    last = pe.transpose(pb[5][0:HEADS, i * P:(i + 1) * P], cpk[:, i], ident[:])
                last.then_inc(s_tp, 1)

            def turn_back(pe, k):
                pe.wait_ge(s_ci, k + 1)
                pe.sem_inc(s_gate, 1)
                pe.transpose(pb[5][:, 384:384 + HEADS], cin[:], ident[0:HEADS, 0:HEADS]).then_inc(s_tb, 1)

            def to_nodes(pe, it, u):
                k = it * UNROLL + u
                pe.wait_ge(f.hot, it * 2 * UNROLL + 2 * u + 2)
                pe.wait_ge(s_fl, k + 1)
                for j in range(TILES):
                    last = pe.matmul(pb[5][0:BP, 400:401 + HEADS], hot[:, (2 * u + j // HALF) % SLOTS, j % HALF],
                                     fl[:, j], start=(j == 0), stop=(j == TILES - 1))
                last.then_inc(s_mx, 1)

            def to_edges(pe, k):
                pe.wait_ge(s_r3, k + 1)
                pe.wait_ge(s_oc, 3 * k + 4)
                for j in range(TILES):
                    bank, c = BCB[j // HALF], (j % HALF) * 2 * HEADS
                    for i in range(3):
                        last = pe.matmul(pb[bank][:, c:c + 2 * HEADS], hotT[:, j], rb[0:BP, i],
                                         start=(i == 0), stop=(i == 2))
                last.then_inc(s_bc, 1)

            def sums(pe, u, g, js):
                q = (2 * u + g) % SLOTS
                for j in js:
                    a, z = (g == 0 and j == 0), (g == 1 and j == HALF - 1)
                    pe.matmul(pb[NUMB[u]][0:BP, :], hot[:, q, j], ring[:, q, j * ROW3:j * ROW3 + 2 * D],
                              start=a, stop=z)

            def denominators(pe, k, u, g):
                if g == 0:
                    pe.wait_ge(s_dc, k + 1)
                for j in range(HALF):
                    last = pe.matmul(pb[3][0:BP, 0:HEADS], hot[:, (2 * u + g) % SLOTS, j], ex[:, u, g * HALF + j],
                                     start=(g == 0 and j == 0), stop=(g == 1 and j == HALF - 1))
                last.then_inc(f.used, 1)

            def out_turn(pe, k):
                pe.wait_ge(s_xr, k + 1)
                for c in range(4):
                    last = pe.transpose(pb[7][:, c * BP:(c + 1) * BP], xo[0:BP, c * P:(c + 1) * P],
                                        ident[0:BP, 0:BP])
                last.then_inc(s_xt, 1)

            def out_project(pe, k):
                pe.wait_ge(s_xc, k + 1)
                for c in range(4):
                    last = pe.matmul(pb[7][0:BP, 0:D], xcT[:, c], wu_s[:, c], start=(c == 0), stop=(c == 3))
                last.then_inc(s_u, 1)

            def gat_tensor(pe, it, u, first=False, last=0):
                k = it * UNROLL + u
                nxt = at(it, u, 1)
                if not first:
                    pe.wait_ge(s_nf, k)
                pe.wait_ge(s_ms, it * 2 * UNROLL + 2 * u + 1)
                sums(pe, u, 0, range(0, 3))
                if last < 2:
                    turn_last(pe, k + 1)
                sums(pe, u, 0, range(3, 9))
                if last < 2:
                    turn_back(pe, k + 1)
                denominators(pe, k, u, 0)
                pe.wait_ge(s_ms, it * 2 * UNROLL + 2 * u + 2)
                sums(pe, u, 1, range(0, 2))
                if last < 2:
                    to_nodes(pe, *nxt)
                if not first:
                    out_turn(pe, k - 1)
                sums(pe, u, 1, range(2, 5))
                if last < 2:
                    to_edges(pe, k + 1)
                if not first:
                    out_project(pe, k - 1)
                sums(pe, u, 1, range(5, 9))
                if last == 0:
                    turn_hot(pe, *at(it, u, 2), 0)
                denominators(pe, k, u, 1)
                if last == 0:
                    turn_hot(pe, *at(it, u, 2), 1)
                    turn_hot(pe, *at(it, u, 2), 2)

            def hot_out(act, k, m):
                act.wait_ge(s_ot, 3 * k + m + 1)
                act.copy(hotT[:, 6 * m:6 * m + 6], pb4b[0:BP, 0:6 * P].rearrange("p (j n) -> p j n", j=6)
                         ).then_inc(s_oc, 1)

            def hot_f32(act, it, u):
                for g in range(2):
                    q = 2 * u + g
                    act.wait_ge(s_hb, it * 2 * UNROLL + q + 1)
                    act.copy(hot[:, q % SLOTS], hotb[:, q % SLOTS].rearrange("p v j -> p j v")).then_inc(f.hot, 1)

            def last_out(act, k):
                act.wait_ge(s_tp, k + 1)
                act.copy(cpT[:].rearrange("p i n -> p (i n)"), pb[5][0:HEADS, 0:3 * P]).then_inc(s_tc, 1)

            def state_exp(act, k, u):
                act.wait_ge(s_df, k + 1)
                act.activation(ab5[0:BP, u], dif[0:BP], ACT.Exp).then_inc(s_ab, 1)

            def edge_exp(act, k, u):
                act.wait_ge(s_et, k + 2)
                act.activation(ex[:, u], et[:], ACT.Exp).then_inc(s_ex, 1)

            def out_parts(act, k):
                act.wait_ge(s_xt, k + 1)
                for c in range(4):
                    x_c = pb[7][:, c * BP:(c + 1) * BP]
                    last = act.activation(neg[:, c], x_c, ACT.Relu, bias=nabT[:, c:c + 1], scale=-1.0)
                last.then_inc(s_ng, 1)
                for c in range(4):
                    act.activation(pos[:, c], pb[7][:, c * BP:(c + 1) * BP], ACT.Relu, bias=abT[:, c:c + 1])
                act.wait_ge(s_ng, k + 1)
                act.activation(neg[:], neg[:], ACT.Exp, scale=-1.0).then_inc(s_el, 1)

            def gat_scalar(act, it, u, first=False, last=0):
                k = it * UNROLL + u
                nxt = at(it, u, 1)
                if last < 2:
                    last_out(act, k + 1)
                if not first:
                    out_parts(act, k - 1)
                if last < 2:
                    state_exp(act, k + 1, nxt[1])
                    edge_exp(act, k + 1, nxt[1])
                if last == 0:
                    for m in range(3):
                        hot_out(act, k + 2, m)
                    hot_f32(act, *at(it, u, 2))

            def steps(eng, n, body):
                for u in range(UNROLL):
                    body(0, u, first=(u == 0))
                with eng.Fori(1, n) as it:
                    for u in range(UNROLL):
                        body(it, u)
                for u in range(UNROLL):
                    body(n, u, last=max(0, u - (UNROLL - 3)))

            def own3(sp, f, node, u):
                sp.dma_start(self_h[0:BP, u], table[2][bass.ds(node, BP), :]).then_inc(f.rec[u], 16)
                sp.dma_start(side_c[0:BP, u], side_d[bass.ds(node, BP), :]).then_inc(f.rec[u], 16)

            def store3(sp, f, node):
                sp.dma_start(out[bass.ds(node, BP), :], res[0:BP]).then_inc(f.st, 16)

            FIRST, LOOP = 200, 175

            with nc.Block() as block:
                @block.sync
                def _(sp):
                    sp_phase(sp, f, own3, store3, 1)

                @block.gpsimd
                def _(pool):
                    pool.memset(endc[:], 0.0)
                    pool.memset(notp0[:], 1.0)
                    pool.iota(iota_b[:], [[1, BP], [0, HALF]], base=0, channel_multiplier=0,
                              allow_small_or_imprecise_dtypes=True)
                    pool.tensor_scalar(nabT[:], abT[:], -1.0, None, ALU.mult)
                    pool.memset(pen[:, :, 0:1], -BIG)
                    pool.memset(cin[:, 0:1], -BIG)
                    pool.tensor_copy(iden_b[:], ident[:]).then_inc(s_c3, 1)
                    pool.wait_ge(s_c3, 1)
                    pool.affine_select(endc[:], endc[:], pattern=[[1, TILES]], compare_op=ALU.not_equal,
                                       fill=1.0, base=1 - CAP, channel_multiplier=TILES)
                    pool.affine_select(notp0[:], notp0[:], pattern=[[0, 1]], compare_op=ALU.not_equal,
                                       fill=0.0, base=0, channel_multiplier=1).then_inc(s_c3, 1)
                    pool_phase(pool, f)

                @block.vector
                def _(dve):
                    n = dve.value_load(niter_i[0:1, 1:2], min_val=UNROLL - 1, max_val=MAXCH // UNROLL - 1)
                    ch = Chain(dve, f.dve)
                    dve.memset(acc[:], 0.0)
                    dve.memset(den[:], 0.0)
                    ch.step(dve.memset(mx[:], 0.0))
                    dve.sem_inc(s_et, 1)
                    dve.sem_inc(s_nf, 1)
                    dve.sem_inc(s_dc, 1)
                    dve.wait_ge(s_c3, 2)
                    edge_hot(dve, ch, 0, 0)
                    edge_flags(dve, ch)
                    run_maxima(dve, ch, 0, 0)
                    carry(dve, ch, 0)
                    whole_runs(dve, ch, 0)
                    node_maxima(dve, ch, 0, 0)
                    edge_hot(dve, ch, 0, 1)
                    edge_flags(dve, ch)
                    edge_weights(dve, ch, 0)

                    def body(it, u, first=False, last=0):
                        if u == 0 and not first:
                            ch.base, ch.n = FIRST + (it - 1) * LOOP, 0
                        gat_vector(dve, ch, it, u, first, last)
                        if u == UNROLL - 1 and not last:
                            want = FIRST if isinstance(it, int) else LOOP
                            assert ch.n == want, (ch.n, want)

                    steps(dve, n, body)
                    k = n * UNROLL + UNROLL - 1
                    read_den(dve, k)
                    node_rows(dve, ch, k, UNROLL - 1)
                    elu(dve, k)
                    result(dve, k, UNROLL - 1)

                @block.tensor
                def _(pe):
                    n = pe.value_load(niter_i[0:1, 1:2], min_val=UNROLL - 1, max_val=MAXCH // UNROLL - 1)
                    pe.wait_ge(s_c3, 2)
                    pe.sem_inc(f.used, SLOTS)
                    for m in range(3):
                        turn_hot(pe, 0, 0, m)
                    turn_last(pe, 0)
                    turn_back(pe, 0)
                    to_nodes(pe, 0, 0)
                    to_edges(pe, 0)
                    for m in range(3):
                        turn_hot(pe, 0, 1, m)
                    steps(pe, n, lambda it, u, first=False, last=0: gat_tensor(pe, it, u, first, last))
                    out_turn(pe, n * UNROLL + UNROLL - 1)
                    out_project(pe, n * UNROLL + UNROLL - 1)

                @block.scalar
                def _(act):
                    n = act.value_load(niter_i[0:1, 1:2], min_val=UNROLL - 1, max_val=MAXCH // UNROLL - 1)
                    act.sem_inc(s_oc, 1)
                    for m in range(3):
                        hot_out(act, 0, m)
                    hot_f32(act, 0, 0)
                    last_out(act, 0)
                    state_exp(act, 0, 0)
                    edge_exp(act, 0, 0)
                    for m in range(3):
                        hot_out(act, 1, m)
                    hot_f32(act, 0, 1)
                    steps(act, n, lambda it, u, first=False, last=0: gat_scalar(act, it, u, first, last))
                    out_parts(act, n * UNROLL + UNROLL - 1)


_INS = ['x', 'src', 'dst', 'L0_gnn_W1', 'L0_gnn_b1', 'L0_gnn_W2', 'L0_gnn_b2', 'L1_gnn_gamma', 'L1_gnn_beta',
        'L1_gnn_W1', 'L1_gnn_a_src1', 'L1_gnn_a_dst1', 'L1_gnn_b1', 'L1_gnn_W2', 'L1_gnn_a_src2',
        'L1_gnn_a_dst2', 'L1_gnn_b2', 'L1_gnn_Wu', 'L1_gnn_bu']


def kernel(**inputs):
    import numpy as _np
    import concourse.bacc as _bacc
    from concourse import mybir as _mybir
    from concourse.bass_utils import run_bass_kernel_spmd as _run

    nc = _bacc.Bacc("TRN2", target_bir_lowering=False, num_devices=1)
    arrays, args = {}, []
    for name in _INS:
        a = _np.ascontiguousarray(inputs[name])
        arrays[f"in_{name}_dram"] = a
        args.append(nc.dram_tensor(f"in_{name}_dram", a.shape, _mybir.dt.from_np(a.dtype), kind="ExternalInput").ap())
    args.append(nc.dram_tensor("out_0_dram", (3125, 256), _mybir.dt.float32, kind="ExternalOutput").ap())
    gnn(nc, *args)
    r = _run(nc, [arrays], core_ids=[0])
    return r.results[0]["out_0_dram"]
```

```python
import concourse.bass as bass
from concourse import mybir
from contextlib import ExitStack

F32 = mybir.dt.float32
BF16 = mybir.dt.bfloat16
I32 = mybir.dt.int32
ALU = mybir.AluOpType
ACT = mybir.ActivationFunctionType
AX = mybir.AxisListType

N = 3125
E = 53125
D = 256
BP = 125
BLOCKS = N // BP
P = 128
TILES = 18
HALF = TILES // 2
CAP = P * TILES
UNROLL = 5
SLOTS = 5
AHEAD = 4
MAXCH = -(-(BLOCKS + E // CAP) // UNROLL) * UNROLL
NCH = MAXCH + AHEAD
EC = E // BP
H1, C1, H2, C2 = 4, 64, 8, 32
HW = 32
HEADS = 2 * D // HW
ROW3 = 2 * D + HEADS
SIDE = HEADS + D
WC = 2 * D + 2 * HEADS
EPS = 1e-5
BIG = 1e30
ROUND = 1.5 * 2 ** 23


class Chain:

    def __init__(self, eng, sem, base=0):
        self.eng, self.sem, self.base, self.n = eng, sem, base, 0

    def step(self, ins):
        self.n += 1
        ins.then_inc(self.sem, 1)
        self.eng.wait_ge(self.sem, self.base + self.n)


def gnn(nc, x, src, dst, gw1, gb1, gw2, gb2, gamma, beta, aw1, as1, ad1, ab1, aw2, as2, ad2, ab2,
        wu, bu, out):
    ctx = ExitStack()
    with ctx:
        def sb(name, shape, dt=F32):
            return ctx.enter_context(nc.sbuf_tensor(name, shape, dt))

        def sem(name):
            return ctx.enter_context(nc.semaphore(name))

        def dram(name, shape, dt=F32):
            return nc.dram_tensor(name, shape, dt, kind="Internal").ap()

        src_lin = dram("src_lin", [E + CAP], I32)
        dst_lin = dram("dst_lin", [E + CAP + 2], I32)
        plan_d = dram("plan_d", [NCH, 2])
        sout_d = dram("sout_d", [BLOCKS, BP])
        table = [dram("table1", [N, D]), dram("table2", [N, D]), dram("table3", [N, ROW3])]
        side_d = dram("side", [N, SIDE])

        ident = sb("ident", [P, P])
        ones = sb("ones", [P, P])
        iota_v = sb("iota_v", [P, BP])
        ring = sb("ring", [P, SLOTS, HALF * ROW3])
        hot = sb("hot", [P, SLOTS, HALF, BP])
        idx = sb("idx", [P, UNROLL, TILES], I32)
        dwin = sb("dwin", [P, UNROLL, TILES + 2], I32)
        cb = sb("cb", [P, UNROLL, 2])
        sout_c = sb("sout_c", [P, UNROLL])
        wg = sb("wg", [P, 2, 2, D])
        bg = sb("bg", [P, 2, D])
        wcat = sb("wcat", [P, 2, WC])
        wu_s = sb("wu_s", [P, 4, D])
        gam = sb("gam", [P, D])
        bet = sb("bet", [P, D])
        bu_s = sb("bu_s", [P, D])
        abT = sb("abT", [P, 4])
        arow = sb("arow", [P, 2, 2 * D])
        dwf = sb("dwf", [P, TILES + 2])
        pb = [ctx.enter_context(nc.psum_tensor(f"bank{i}", [P, 512], F32)) for i in range(8)]

        s_const = sem("s_const")
        s_ld = sem("s_ld")
        s_x = sem("s_x")
        s_w = sem("s_w")
        s_pad = sem("s_pad")
        s_dve = sem("s_dve")
        s_h1 = sem("s_h1")
        s_hm = sem("s_hm")
        s_cnt = sem("s_cnt")
        s_df1 = sem("s_df1")
        s_ac = sem("s_ac")
        s_sc = sem("s_sc")
        s_sq = sem("s_sq")
        s_rt = sem("s_rt")
        s_t1 = sem("s_t1")
        s_plan = sem("s_plan")
        s_pd = sem("s_pd")
        s_go = [sem(f"s_go{i}") for i in range(3)]
        s_st1 = sem("s_st1")
        s_gate = sem("s_gate")

        NOWHERE = 1 << 20
        plan_i = sb("plan_i", [1, 2, NCH], I32)
        niter_i = sb("niter_i", [1, 2], I32)

        class Phase:
            def __init__(self, i):
                self.i = i
                self.rec = [sem(f"rec{i}_{u}") for u in range(UNROLL)]
                self.rows = [sem(f"rows{i}_{s}") for s in range(SLOTS)]
                self.hot = sem(f"hot{i}")
                self.used = sem(f"used{i}")
                self.acc = sem(f"acc{i}")
                self.z = sem(f"z{i}")
                self.t = sem(f"t{i}")
                self.fin = sem(f"fin{i}")
                self.st = sem(f"st{i}")
                self.free = sem(f"free{i}")
                self.dve = sem(f"dve{i}")
                self.hc = sem(f"hc{i}")
                self.dg = sem(f"dg{i}")
                self.sq = sem(f"sq{i}")
                self.rt = sem(f"rt{i}")

        ph = [Phase(i) for i in range(3)]
        NREC = [4, 4, 5]

        phase_a = ExitStack()
        def sa(name, shape, dt=F32):
            return phase_a.enter_context(nc.sbuf_tensor(name, shape, dt))
        with phase_a:
            src_i = sa("src_i", [BP, EC], I32)
            dst_i = sa("dst_i", [BP, EC], I32)
            src_f = sa("src_f", [BP, EC])
            low_f = sa("low_f", [BP, EC])
            low_b = sa("low_b", [BP, EC], BF16)
            high_b = sa("high_b", [BP, EC], BF16)
            dst_f = sa("dst_f", [BP, EC])
            junk = sa("junk", [BP, EC])
            x_all = ring[0:BP, :, :].rearrange("p s n -> p (s n)")[:, 0:BLOCKS * D].rearrange(
                "p (b d) -> p b d", d=D)
            PARTS = 25
            PC = EC // PARTS
            XB = 8
            iota_r = sa("iota_r", [BP, BP, PC], BF16)
            oh_lo = sa("oh_lo", [BP, 2, BP, PC], BF16)
            oh_hi = sa("oh_hi", [BP, 2, BLOCKS, PC], BF16)
            stats = sa("stats", [BP, BLOCKS, 6])
            mv = sa("mv", [BP, BLOCKS, 2])
            rstd = sa("rstd", [BP, BLOCKS])
            sout = sa("sout", [BP, BLOCKS])
            sc1 = sa("sc1", [BP, BLOCKS])
            nb1 = sa("nb1", [BP, BLOCKS])
            cnt = sa("cnt", [BP, BLOCKS])
            lim = sa("lim", [BP, BLOCKS - 1])
            pad_i = sa("pad_i", [1, 2, CAP + 2], I32)
            row = sa("row", [1, 8, BLOCKS + 1])
            grid = sa("grid", [1, NCH * BLOCKS])
            iotas = sa("iotas", [1, NCH * BLOCKS])
            pl = sa("pl", [1, 4, NCH])
            plan_f = sa("plan_f", [1, NCH, 2])

            PIECE = E // 25
            spare = ring[0:BP, :, :].rearrange("p s n -> p (s n)")[:, BLOCKS * D:BLOCKS * D + 5 * PIECE].rearrange(
                "p (i n) -> p i n", i=5)
            piece_i = spare[:, 0].bitcast(I32)
            piece_f, count_up, before, larger = (spare[:, i] for i in range(1, 5))
            rank = sa("rank", [BP, EC])
            rank_i = sa("rank_i", [BP, 2, EC], I32)
            own_e = sa("own_e", [BP, EC])
            part_r = sa("part_r", [BP, 1])
            next_i = sa("next_i", [BP, 1], I32)
            next_f = sa("next_f", [BP, 1])
            down = sa("down", [BP, EC])
            unsorted_i = sa("unsorted_i", [1, 1], I32)
            s_desc = sem("s_desc")
            s_uns = sem("s_uns")
            s_uc = sem("s_uc")
            s_piece = sem("s_piece")
            s_pfree = sem("s_pfree")
            s_rk = sem("s_rk")
            s_rkd = sem("s_rkd")
            put = sa("put", [BP, 4, PC], I32)
            s_put = sem("s_put")
            s_scat = sem("s_scat")

            def order_sync(sp):
                sp.wait_ge(s_uns, 1)
                n = sp.value_load(unsorted_i[0:1, 0:1], min_val=0, max_val=1)
                with sp.If(n > 0):
                    with sp.Fori(0, E // PIECE) as r:
                        sp.wait_ge(s_pfree, r + 1)
                        sp.dma_start(piece_i, bass.AP(dst.tensor, r * PIECE, [[0, BP], [1, PIECE]])
                                     ).then_inc(s_piece, 16)
                    sp.wait_ge(s_scat, 16 * 2 * EC)

            def order_vector(dve):
                n = dve.value_load(unsorted_i[0:1, 0:1], min_val=0, max_val=1)
                with dve.If(n > 0):
                    dve.memset(rank[:], 0.0)
                    dve.sem_inc(s_pfree, 1)
                    dve.wait_ge(s_uc, 1)
                    with dve.Fori(0, E // PIECE) as r:
                        dve.wait_ge(s_piece, (r + 1) * 16)
                        rk = Chain(dve, s_rk, r * (2 + 3 * EC))
                        rk.step(dve.tensor_copy(piece_f, piece_i))
                        dve.sem_inc(s_gate, 1)
                        with dve.Fori(0, EC) as c:
                            rc = Chain(dve, s_rk, r * (2 + 3 * EC) + 1 + c * 3)
                            rc.step(dve.tensor_scalar(before, count_up, own_e[:, bass.ds(c, 1)], 0.5,
                                                      ALU.is_lt, ALU.mult))
                            rc.step(dve.scalar_tensor_tensor(larger, before, dst_f[:, bass.ds(c, 1)], piece_f,
                                                             ALU.add, ALU.is_gt, accum_out=part_r[:]))
                            rc.step(dve.tensor_tensor(rank[:, bass.ds(c, 1)], rank[:, bass.ds(c, 1)],
                                                      part_r[:], ALU.add))
                        re = Chain(dve, s_rk, r * (2 + 3 * EC) + 1 + 3 * EC)
                        re.step(dve.tensor_scalar(own_e[:], own_e[:], -float(PIECE), None, ALU.add))
                        dve.sem_inc(s_pfree, 1)
                    dve.tensor_copy(rank_i[:, 0], rank[:])
                    dve.tensor_scalar(rank_i[:, 1], rank[:], 1.0, None, ALU.add).then_inc(s_rkd, 1)

            def order_gpsimd(pool):
                pool.wait_ge(s_uns, 1)
                n = pool.value_load(unsorted_i[0:1, 0:1], min_val=0, max_val=1)
                with pool.If(n > 0):
                    pool.iota(own_e[:], [[1, EC]], base=0, channel_multiplier=EC,
                              allow_small_or_imprecise_dtypes=True)
                    pool.iota(count_up, [[1, PIECE]], base=0, channel_multiplier=0,
                              allow_small_or_imprecise_dtypes=True).then_inc(s_uc, 1)
                    pool.wait_ge(s_rkd, 1)
                    pool.wait_ge(s_pad, 16 * 5)
                    with pool.Fori(0, EC // PC) as c:
                        cols = bass.ds(c * PC, PC)
                        pool.tensor_copy(put[:, 0:2], rank_i[:, :, cols])
                        pool.tensor_copy(put[:, 2], src_i[:, cols])
                        pool.tensor_copy(put[:, 3], dst_i[:, cols]).then_inc(s_put, 1)
                        pool.wait_ge(s_put, c + 1)
                        pool.sem_inc(s_gate, 1)
                        for j in range(PC):
                            for i, to in enumerate((src_lin, dst_lin)):
                                pool.indirect_dma_start(
                                    to.unsqueeze(1), bass.IndirectOffsetOnAxis(put[:, i, j:j + 1], 0),
                                    put[:, 2 + i, j:j + 1], None).then_inc(s_scat, 16)
                        pool.wait_ge(s_scat, (c + 1) * (16 * 2 * PC))
                        pool.sem_inc(s_gate, 1)

            with nc.Block() as block:
                @block.sync
                def _(sp):
                    sp.dma_start(src_i[:], src.rearrange("(p c) -> p c", p=BP)).then_inc(s_ld, 16)
                    sp.dma_start(dst_i[:], dst.rearrange("(p c) -> p c", p=BP)).then_inc(s_ld, 16)
                    with nc.allow_non_contiguous_dma(reason="one destination per partition, once"):
                        sp.dma_start(next_i[0:BP - 1], bass.AP(dst.tensor, EC, [[EC, BP - 1], [1, 1]])
                                     ).then_inc(s_ld, 16)
                    sp.dma_start(x_all, x.rearrange("(b p) d -> p b d", p=BP)).then_inc(s_x, 16)
                    sp.dma_start(src_lin[0:E].rearrange("(p c) -> p c", p=BP),
                                 src.rearrange("(p c) -> p c", p=BP)).then_inc(s_pad, 16)
                    sp.dma_start(dst_lin[1:1 + E].rearrange("(p c) -> p c", p=BP),
                                 dst.rearrange("(p c) -> p c", p=BP)).then_inc(s_pad, 16)
                    sp.wait_ge(s_const, 2)
                    sp.dma_start(src_lin[E:E + CAP].unsqueeze(0), pad_i[:, 0, 0:CAP]).then_inc(s_pad, 16)
                    sp.dma_start(dst_lin[1 + E:E + CAP + 2].unsqueeze(0),
                                 pad_i[:, 1, 0:CAP + 1]).then_inc(s_pad, 16)
                    sp.dma_start(dst_lin[0:1].unsqueeze(0), pad_i[:, 1, 0:1]).then_inc(s_pad, 16)
                    for w, l in ((gw1, 0), (gw2, 1)):
                        sp.dma_start(wg[:, l], w.rearrange("(c p) n -> p c n", p=P)).then_inc(s_w, 16)
                    sp.dma_start(wcat[:, :, 0:D], aw1.rearrange("(c p) n -> p c n", p=P)).then_inc(s_w, 16)
                    sp.dma_start(wcat[:, :, D:2 * D], aw2.rearrange("(c p) n -> p c n", p=P)).then_inc(s_w, 16)
                    sp.dma_start(wu_s[:], wu.rearrange("(c p) n -> p c n", p=P)).then_inc(s_w, 16)
                    for to, of in ((bg[:, 0], gb1), (bg[:, 1], gb2), (gam[:], gamma), (bet[:], beta),
                                   (bu_s[:], bu),
                                   (arow[:, 0, 0:D], as1.rearrange("h c -> (h c)")),
                                   (arow[:, 0, D:2 * D], as2.rearrange("h c -> (h c)")),
                                   (arow[:, 1, 0:D], ad1.rearrange("h c -> (h c)")),
                                   (arow[:, 1, D:2 * D], ad2.rearrange("h c -> (h c)"))):
                        sp.dma_start(to, of.partition_broadcast(P)).then_inc(s_w, 16)
                    with nc.allow_non_contiguous_dma(reason="biases with features on partitions, once"):
                        sp.dma_start(abT[:, 0:2], ab1.rearrange("(c p) -> p c", p=P)).then_inc(s_w, 16)
                        sp.dma_start(abT[:, 2:4], ab2.rearrange("(c p) -> p c", p=P)).then_inc(s_w, 16)
                    sp.wait_ge(s_sc, 1)
                    with nc.allow_non_contiguous_dma(reason="a scale per node, once"):
                        sp.dma_start(sout_d.rearrange("b p -> p b"), sout[:]).then_inc(s_pd, 16)
                    for b in range(0, BLOCKS, UNROLL):
                        sp.wait_ge(s_t1, b + UNROLL)
                        sp.dma_start(table[0][b * BP:(b + UNROLL) * BP, :].rearrange("(b p) d -> p b d", p=BP),
                                     x_all[:, b:b + UNROLL, :]).then_inc(s_st1, 16)
                    sp.wait_ge(s_plan, 1)
                    sp.dma_start(plan_d.unsqueeze(0), plan_f[:]).then_inc(s_pd, 16)
                    sp.wait_ge(s_st1, 16 * (BLOCKS // UNROLL))
                    sp.wait_ge(s_pd, 32)
                    sp.wait_ge(s_pad, 16 * 5)
                    order_sync(sp)
                    sp.sem_inc(s_go[0], 1)

                @block.gpsimd
                def _(pool):
                    pool.iota(iota_r[:], [[1, BP], [0, PC]], base=0, channel_multiplier=0,
                              allow_small_or_imprecise_dtypes=True).then_inc(s_const, 1)
                    pool.memset(pad_i[:, 0, :], 0)
                    pool.memset(pad_i[:, 1, :], NOWHERE).then_inc(s_const, 1)
                    pool.iota(iotas[:], [[1, NCH * BLOCKS]], base=0, channel_multiplier=0,
                              allow_small_or_imprecise_dtypes=True)
                    pool.iota(iota_v[:], [[1, BP]], base=0, channel_multiplier=0,
                              allow_small_or_imprecise_dtypes=True)
                    pool.iota(lim[:], [[2 * BP, BLOCKS - 1]], base=2 * BP - 1, channel_multiplier=0,
                              allow_small_or_imprecise_dtypes=True)
                    pool.memset(ones[:], 1.0)
                    pool.memset(ident[:], 0.0).then_inc(s_const, 1)
                    pool.wait_ge(s_const, 3)
                    pool.affine_select(ident[:], ident[:], pattern=[[-1, P]], compare_op=ALU.not_equal,
                                       fill=1.0, base=0, channel_multiplier=1).then_inc(s_const, 1)
                    order_gpsimd(pool)

                @block.vector
                def _(dve):
                    ch = Chain(dve, s_dve)
                    ch.step(dve.memset(next_f[:], float(NOWHERE)))
                    dve.wait_ge(s_ld, 48)
                    ch.step(dve.tensor_copy(next_f[0:BP - 1], next_i[0:BP - 1]))
                    dve.tensor_copy(dst_f[:], dst_i[:]).then_inc(s_df1, 1)
                    dve.wait_ge(s_df1, 1)
                    dve.tensor_tensor(down[:, EC - 1:EC], dst_f[:, EC - 1:EC], next_f[:], ALU.is_gt)
                    ch.step(dve.tensor_tensor(down[:, 0:EC - 1], dst_f[:, 0:EC - 1], dst_f[:, 1:EC], ALU.is_gt))
                    dve.tensor_reduce(cnt[:, BLOCKS - 1:BLOCKS], down[:], AX.X, ALU.add).then_inc(s_desc, 1)
                    ch.step(dve.tensor_copy(src_f[:], src_i[:]))
                    ch.step(dve.tensor_scalar(low_f[:], src_f[:], -float(BP // 2), 1.0 / BP, ALU.add, ALU.mult))
                    ch.step(dve.tensor_scalar(low_f[:], low_f[:], ROUND, None, ALU.add))
                    ch.step(dve.tensor_scalar(low_f[:], low_f[:], -ROUND, None, ALU.add))
                    ch.step(dve.tensor_copy(high_b[:], low_f[:]))
                    ch.step(dve.scalar_tensor_tensor(low_b[:], low_f[:], -float(BP), src_f[:], ALU.mult, ALU.add))
                    dve.wait_ge(s_const, 1)
                    for c in range(PARTS):
                        cs = slice(c * PC, (c + 1) * PC)
                        if c >= 2:
                            dve.wait_ge(s_hm, c - 1)
                        dve.tensor_tensor(oh_lo[:, c % 2], iota_r[:],
                                          low_b[:, cs].unsqueeze(1).to_broadcast([BP, BP, PC]),
                                          ALU.is_equal)
                        dve.tensor_tensor(oh_hi[:, c % 2], iota_r[:, 0:BLOCKS],
                                          high_b[:, cs].unsqueeze(1).to_broadcast([BP, BLOCKS, PC]),
                                          ALU.is_equal).then_inc(s_h1, 1)
                        if c == XB:
                            dve.wait_ge(s_x, 16)
                        for b in ((c - XB) * 2, (c - XB) * 2 + 1):
                            if 0 <= b < BLOCKS:
                                last = dve.bn_stats(stats[:, b], x_all[:, b])
                    ch.step(last)
                    for b in range(BLOCKS):
                        last = dve.bn_aggr(mv[:, b], stats[:, b])
                    ch.step(last)
                    dve.tensor_scalar(rstd[:], mv[:, :, 1], EPS, None, ALU.add).then_inc(s_sq, 1)
                    dve.wait_ge(s_hm, PARTS)
                    dve.tensor_scalar(sout[:], pb[0][0:BP, 0:BLOCKS], 1.0, None, ALU.max).then_inc(s_sq, 1)
                    dve.wait_ge(s_rt, 2)
                    ch.step(dve.reciprocal(rstd[:], rstd[:]))
                    ch.step(dve.reciprocal(sout[:], sout[:]))
                    ch.step(dve.tensor_tensor(sc1[:], rstd[:], sout[:], ALU.mult))
                    dve.scalar_tensor_tensor(nb1[:], mv[:, :, 0], -1.0, sc1[:], ALU.mult,
                                             ALU.mult).then_inc(s_sc, 1)
                    dve.wait_ge(s_cnt, 2)
                    dve.tensor_scalar(unsorted_i[:], pb[1][0:1, BLOCKS - 1:BLOCKS], 1.0, None,
                                      ALU.min).then_inc(s_uns, 1)
                    st, ln, nch, cum, off = (row[:, i, :] for i in range(5))
                    onerow = row[:, 5, 0:BLOCKS]
                    dve.wait_ge(s_const, 4)
                    dve.memset(onerow, 1.0)
                    dve.memset(st[:, 0:1], 0.0)
                    dve.memset(st[:, BLOCKS:BLOCKS + 1], float(E))
                    ch.step(dve.tensor_scalar(st[:, 1:BLOCKS], pb[1][0:1, 0:BLOCKS - 1], float(E), 0.5,
                                              ALU.add, ALU.mult))
                    ch.step(dve.tensor_tensor(ln[:, 0:BLOCKS], st[:, 1:BLOCKS + 1], st[:, 0:BLOCKS],
                                              ALU.subtract))
                    M = E // CAP
                    caps = grid[:, 0:M]
                    ch.step(dve.tensor_scalar(caps, iotas[:, 1:1 + M], float(CAP), None, ALU.mult))
                    g2 = grid[:, M:M + BLOCKS * M].rearrange("p (b m) -> p b m", m=M)
                    ch.step(dve.tensor_tensor(g2, ln[:, 0:BLOCKS].unsqueeze(2).to_broadcast([1, BLOCKS, M]),
                                              caps.unsqueeze(1).to_broadcast([1, BLOCKS, M]), ALU.is_gt))
                    ch.step(dve.tensor_reduce(nch[:, 0:BLOCKS], g2, AX.X, ALU.add))
                    ch.step(dve.tensor_scalar(nch[:, 0:BLOCKS], nch[:, 0:BLOCKS], 1.0, None, ALU.add))
                    ch.step(dve.tensor_tensor_scan(cum[:, 0:BLOCKS], onerow, nch[:, 0:BLOCKS], 0.0,
                                                   ALU.mult, ALU.add))
                    gk = grid[:, 0:NCH * (BLOCKS - 1)].rearrange("p (k b) -> p k b", k=NCH)
                    kk = iotas[:, 0:NCH]
                    ch.step(dve.tensor_tensor(gk, kk.unsqueeze(2).to_broadcast([1, NCH, BLOCKS - 1]),
                                              cum[:, 0:BLOCKS - 1].unsqueeze(1).to_broadcast([1, NCH, BLOCKS - 1]),
                                              ALU.is_ge))
                    blk = pl[:, 0, :]
                    ch.step(dve.tensor_reduce(blk, gk, AX.X, ALU.add))
                    ch.step(dve.tensor_tensor(off[:, 0:BLOCKS], nch[:, 0:BLOCKS], cum[:, 0:BLOCKS], ALU.subtract))
                    ch.step(dve.scalar_tensor_tensor(off[:, 0:BLOCKS], off[:, 0:BLOCKS], float(CAP),
                                                     st[:, 0:BLOCKS], ALU.mult, ALU.add))
                    gb = grid[:, 0:NCH * BLOCKS].rearrange("p (k b) -> p k b", k=NCH)
                    ch.step(dve.tensor_tensor(gb, blk.unsqueeze(2).to_broadcast([1, NCH, BLOCKS]),
                                              iotas[:, 0:BLOCKS].unsqueeze(1).to_broadcast([1, NCH, BLOCKS]),
                                              ALU.is_equal))
                    ch.step(dve.tensor_tensor(gb, gb, off[:, 0:BLOCKS].unsqueeze(1).to_broadcast([1, NCH, BLOCKS]),
                                              ALU.mult))
                    base = pl[:, 1, :]
                    ch.step(dve.tensor_reduce(base, gb, AX.X, ALU.add))
                    ch.step(dve.scalar_tensor_tensor(base, kk, float(CAP), base, ALU.mult, ALU.add))
                    ch.step(dve.tensor_scalar(base, base, float(E), None, ALU.min))
                    goes, first = plan_f[:, :, 0], plan_f[:, :, 1]
                    ch.step(dve.memset(goes, 0.0))
                    ch.step(dve.tensor_tensor(goes[:, 1:NCH], blk[:, 1:NCH], blk[:, 0:NCH - 1], ALU.is_equal))
                    ch.step(dve.tensor_scalar(first, blk, float(BP), None, ALU.mult))
                    ch.step(dve.tensor_copy(plan_i[:, 0, :], base))
                    ch.step(dve.tensor_copy(plan_i[:, 1, :], first))
                    T = MAXCH // UNROLL
                    g5 = pl[:, 2, 0:T]
                    ch.step(dve.tensor_scalar(g5, iotas[:, 0:T], float(UNROLL), cum[:, BLOCKS - 1:BLOCKS],
                                              ALU.mult, ALU.is_lt))
                    ch.step(dve.tensor_reduce(pl[:, 3, 0:1], g5, AX.X, ALU.add))
                    ch.step(dve.tensor_scalar(pl[:, 3, 1:2], pl[:, 3, 0:1], -1.0, None, ALU.add))
                    dve.tensor_copy(niter_i[:], pl[:, 3, 0:2]).then_inc(s_plan, 1)
                    dve.wait_ge(s_uns, 1)
                    order_vector(dve)

                @block.scalar
                def _(act):
                    act.wait_ge(s_const, 4)
                    act.wait_ge(s_df1, 1)
                    for b in range(BLOCKS - 1):
                        act.activation(junk[:], dst_f[:], ACT.Sign, bias=lim[:, b:b + 1], scale=-2.0,
                                       accum_out=cnt[:, b:b + 1]).then_inc(s_ac, 1)
                        act.wait_ge(s_ac, b + 1)
                    act.sem_inc(s_cnt, 1)
                    for n, v in enumerate((rstd, sout)):
                        act.wait_ge(s_sq, n + 1)
                        act.activation(v[:], v[:], ACT.Sqrt).then_inc(s_rt, 1)
                    act.wait_ge(s_sc, 1)
                    for b in range(BLOCKS):
                        act.activation(x_all[:, b], x_all[:, b], ACT.Relu, bias=nb1[:, b:b + 1],
                                       scale=sc1[:, b:b + 1]).then_inc(s_t1, 1)

                @block.tensor
                def _(pe):
                    for c in range(PARTS):
                        pe.wait_ge(s_h1, c + 1)
                        for j in range(PC):
                            last = pe.matmul(pb[0][0:BP, 0:BLOCKS], oh_lo[:, c % 2, :, j], oh_hi[:, c % 2, :, j],
                                             start=(c == 0 and j == 0), stop=(c == PARTS - 1 and j == PC - 1))
                        last.then_inc(s_hm, 1)
                    pe.wait_ge(s_const, 4)
                    pe.wait_ge(s_cnt, 1)
                    pe.wait_ge(s_desc, 1)
                    pe.matmul(pb[1][0:1, 0:BLOCKS], ones[0:BP, 0:1], cnt[:, 0:BLOCKS],
                              start=True, stop=True).then_inc(s_cnt, 1)

        def load_record(sp, f, k, u, own):
            base = sp.value_load(plan_i[0:1, 0, bass.ds(k, 1)], min_val=0, max_val=E)
            node = sp.value_load(plan_i[0:1, 1, bass.ds(k, 1)], min_val=0, max_val=N - BP)
            sp.dma_start(idx[:, u], bass.AP(src_lin.tensor, base, [[TILES, P], [1, TILES]])).then_inc(f.rec[u], 16)
            sp.dma_start(dwin[:, u], bass.AP(dst_lin.tensor, base, [[TILES, P], [1, TILES + 2]])).then_inc(f.rec[u], 16)
            sp.dma_start(cb[:, u], bass.AP(plan_d.tensor, k * 2, [[0, P], [1, 2]])).then_inc(f.rec[u], 16)
            own(sp, f, node, u)

        def sp_phase(sp, f, own, store, nst):
            n = sp.value_load(niter_i[0:1, 0:1], min_val=UNROLL, max_val=MAXCH // UNROLL)
            for k in range(AHEAD):
                load_record(sp, f, k, k, own)
            sp.sem_inc(f.free, 1 if f.i < 2 else 3)
            with sp.Fori(0, n) as it:
                for u in range(UNROLL):
                    k = it * UNROLL + u
                    load_record(sp, f, k + AHEAD, (u + AHEAD) % UNROLL, own)
                    node = sp.value_load(plan_i[0:1, 1, bass.ds(k, 1)], min_val=0, max_val=N - BP)
                    sp.wait_ge(f.fin, k + 1)
                    store(sp, f, node)
                    sp.wait_ge(f.st, (k + 1) * 16 * nst)
                    sp.sem_inc(f.free, 1)
            for u in range(AHEAD):
                sp.wait_ge(f.rec[u], (n + 1) * 16 * NREC[f.i])
            if f.i < 2:
                sp.sem_inc(s_go[f.i + 1], 1)
            else:
                sp.sem_inc(s_gate, 1)

        def pool_phase(pool, f):
            width = D if f.i < 2 else ROW3
            n = pool.value_load(niter_i[0:1, 0:1], min_val=UNROLL, max_val=MAXCH // UNROLL)
            pool.wait_ge(s_go[f.i], 1)
            with pool.Fori(0, n) as it:
                for u in range(UNROLL):
                    pool.wait_ge(f.rec[u], (it + 1) * 16 * NREC[f.i])
                    for g in range(2):
                        q = 2 * u + g
                        pool.wait_ge(f.used, it * (2 * UNROLL) + q + 1)
                        pool.sem_inc(s_gate, 1)
                        for j in range(HALF):
                            t = g * HALF + j
                            pool.indirect_dma_start(
                                ring[:, q % SLOTS, j * width:(j + 1) * width], None, table[f.i],
                                bass.IndirectOffsetOnAxis(idx[:, u, t:t + 1], 0)).then_inc(f.rows[q % SLOTS], 16)

        def rows_wait(eng, f, it, q):
            eng.wait_ge(f.rows[q % SLOTS], (it * 2 + (q // SLOTS + 1)) * 16 * HALF)

        def make_hot(dve, f, it, u):
            for g in range(2):
                q = 2 * u + g
                dve.wait_ge(f.used, it * (2 * UNROLL) + q + 1)
                dve.tensor_tensor(hot[:, q % SLOTS], iota_v[:].unsqueeze(1).to_broadcast([P, HALF, BP]),
                                  dwf[:, 1 + g * HALF:1 + (g + 1) * HALF].unsqueeze(2).to_broadcast([P, HALF, BP]),
                                  ALU.is_equal).then_inc(f.hot, 1)

        phase_b = ExitStack()
        def sbb(name, shape, dt=F32):
            return phase_b.enter_context(nc.sbuf_tensor(name, shape, dt))
        with phase_b:
            xrow = sbb("xrow", [P, UNROLL, D])
            aggT = sbb("aggT", [P, 2, BP])
            deg = sbb("deg", [P, 1])
            s_in = sbb("s_in", [P, 1])
            part = sbb("part", [P, 2, BP])
            zt = sbb("zt", [P, D])
            row12 = sbb("row12", [P, D])
            x2 = sbb("x2", [P, D])
            h2 = sbb("h2", [P, D])
            xn = sbb("xn", [P, D])
            xnT = sbb("xnT", [P, 2, BP])
            row3 = sbb("row3", [P, ROW3])
            rowS = sbb("rowS", [P, SIDE])
            prod = sbb("prod", [P, 2, 2 * D])
            bst = sbb("bst", [P, 6])
            bmv = sbb("bmv", [P, 2])
            brs = sbb("brs", [P, 2])
            s_wa = sem("s_wa")
            s_xn = sem("s_xn")
            s_xt = sem("s_xt")
            s_xc = sem("s_xc")
            s_H = sem("s_H")
            s_rs = sem("s_rs")

            LINKS = [5, 19]
            ROOTS = [1, 3]

            def inv_root(dve, ch, f, count, v, ins):
                ins.then_inc(f.sq, 1)
                dve.wait_ge(f.rt, count)
                ch.step(dve.reciprocal(v, v))

            def root(act, f, count, v):
                act.wait_ge(f.sq, count)
                act.activation(v, v, ACT.Sqrt).then_inc(f.rt, 1)

            def gcn_hot(dve, ch, f, it, u):
                dve.wait_ge(f.rec[u], (it + 1) * 16 * NREC[f.i])
                ch.step(dve.tensor_scalar(dwf[:], dwin[:, u], cb[:, u, 1:2], None, ALU.subtract))
                make_hot(dve, f, it, u)

            def gcn_counts(dve, f, it, u):
                dve.wait_ge(f.hot, it * (2 * UNROLL) + 2 * u + 2)
                for g in range(2):
                    last = dve.tensor_reduce(part[:, g], hot[:, (2 * u + g) % SLOTS].rearrange("p j v -> p v j"),
                                             AX.X, ALU.add)
                last.then_inc(f.hc, 1)

            def gcn_vector(dve, f, it, u):
                k = it * UNROLL + u
                ch = Chain(dve, f.dve, 1 + k * LINKS[f.i])
                ahead = (it + (u + 1) // UNROLL, (u + 1) % UNROLL)
                gcn_hot(dve, ch, f, *ahead)
                goes = cb[:, u, 0:1]
                dve.wait_ge(f.used, k * 2 + 2 + SLOTS)
                for h in range(2):
                    last = dve.scalar_tensor_tensor(aggT[:, h], aggT[:, h], goes, pb[h][:, 0:BP],
                                                    ALU.mult, ALU.add)
                last.then_inc(f.acc, 1)
                dve.wait_ge(f.dg, k + 1)
                ch.step(dve.scalar_tensor_tensor(deg[0:BP], deg[0:BP], goes[0:BP], pb[2][0:BP, 0:1],
                                                 ALU.mult, ALU.add))
                inv_root(dve, ch, f, k * ROOTS[f.i] + 1, s_in[0:BP],
                         dve.tensor_scalar(s_in[0:BP], deg[0:BP], 1.0, None, ALU.max))
                gcn_counts(dve, f, *ahead)
                dve.wait_ge(f.z, k + 1)
                dve.wait_ge(f.free, k + 1)
                if f.i == 0:
                    ch.step(dve.scalar_tensor_tensor(zt[0:BP], pb[3][0:BP, 0:D], s_in[0:BP], bg[0:BP, 0],
                                                     ALU.mult, ALU.add))
                    ch.step(dve.tensor_scalar(row12[0:BP], zt[0:BP], 0.0, sout_c[0:BP, u:u + 1],
                                              ALU.max, ALU.mult))
                    dve.sem_inc(f.fin, 1)
                    assert ch.n == LINKS[0], ch.n
                    return
                ch.step(dve.scalar_tensor_tensor(zt[0:BP], pb[3][0:BP, 0:D], s_in[0:BP], bg[0:BP, 1],
                                                 ALU.mult, ALU.add))
                ch.step(dve.scalar_tensor_tensor(x2[0:BP], zt[0:BP], 0.0, xrow[0:BP, u], ALU.max, ALU.add))
                ch.step(dve.bn_stats(bst[0:BP], x2[0:BP]))
                dve.sem_inc(s_gate, 1)
                ch.step(dve.bn_aggr(bmv[0:BP], bst[0:BP]))
                inv_root(dve, ch, f, k * ROOTS[f.i] + 2, brs[0:BP, 0:1],
                         dve.tensor_scalar(brs[0:BP, 0:1], bmv[0:BP, 1:2], EPS, None, ALU.add))
                ch.step(dve.scalar_tensor_tensor(brs[0:BP, 1:2], bmv[0:BP, 0:1], -1.0, brs[0:BP, 0:1],
                                                 ALU.mult, ALU.mult))
                ch.step(dve.tensor_scalar(zt[0:BP], x2[0:BP], brs[0:BP, 0:1], brs[0:BP, 1:2], ALU.mult, ALU.add))
                ch.step(dve.tensor_scalar(h2[0:BP], zt[0:BP], 0.0, None, ALU.max))
                ch.step(dve.tensor_tensor(x2[0:BP], x2[0:BP], h2[0:BP], ALU.add))
                ch.step(dve.bn_stats(bst[0:BP], h2[0:BP]))
                dve.sem_inc(s_gate, 1)
                ch.step(dve.bn_aggr(bmv[0:BP], bst[0:BP]))
                inv_root(dve, ch, f, k * ROOTS[f.i] + 3, brs[0:BP, 0:1],
                         dve.tensor_scalar(brs[0:BP, 0:1], bmv[0:BP, 1:2], EPS, None, ALU.add))
                ch.step(dve.tensor_scalar(xn[0:BP], h2[0:BP], bmv[0:BP, 0:1], brs[0:BP, 0:1],
                                          ALU.subtract, ALU.mult))
                ch.step(dve.tensor_tensor(xn[0:BP], xn[0:BP], gam[0:BP], ALU.mult))
                ch.step(dve.tensor_tensor(xn[0:BP], xn[0:BP], bet[0:BP], ALU.add))
                dve.sem_inc(s_xn, 1)
                ch.step(dve.tensor_tensor(rowS[0:BP, HEADS:SIDE], x2[0:BP], bu_s[0:BP], ALU.add))
                dve.sem_inc(s_rs, 1)
                assert ch.n == LINKS[1], ch.n

            def gcn_project(pe, k):
                pe.wait_ge(s_xn, k + 1)
                for h in range(2):
                    last = pe.transpose(pb[4][:, h * P:h * P + BP], xn[0:BP, h * P:(h + 1) * P],
                                        ident[0:BP, 0:BP])
                last.then_inc(s_xt, 1)
                pe.wait_ge(s_xc, k + 1)
                for h in range(2):
                    pe.matmul(pb[5][0:BP, :], xnT[:, h], wcat[:, h, 0:2 * D], start=(h == 0), stop=(h == 1))
                for h in range(2):
                    last = pe.matmul(pb[6][0:BP, 0:2 * HEADS], xnT[:, h], wcat[:, h, 2 * D:WC],
                                     start=(h == 0), stop=(h == 1))
                last.then_inc(s_H, 1)

            def gcn_tensor(pe, f, it, u, first=False):
                k = it * UNROLL + u
                for g in range(2):
                    q = 2 * u + g
                    pe.wait_ge(f.hot, it * (2 * UNROLL) + q + 1)
                    rows_wait(pe, f, it, q)
                    for j in range(HALF):
                        a, z = (g == 0 and j == 0), (g == 1 and j == HALF - 1)
                        for h in range(2):
                            lo = j * D + h * P
                            last = pe.matmul(pb[h][:, 0:BP], ring[:, q % SLOTS, lo:lo + P],
                                             hot[:, q % SLOTS, j, :], start=a, stop=z)
                    last.then_inc(f.used, 1)
                    if f.i == 1 and g == 0 and not first:
                        gcn_project(pe, k - 1)
                pe.wait_ge(f.hc, k + 1)
                for g in range(2):
                    last = pe.matmul(pb[2][0:BP, 0:1], part[:, g], ones[:, 0:1], start=(g == 0), stop=(g == 1))
                last.then_inc(f.dg, 1)
                pe.wait_ge(f.acc, k + 1)
                for h in range(2):
                    last = pe.matmul(pb[3][0:BP, 0:D], aggT[:, h], wg[:, f.i, h], start=(h == 0), stop=(h == 1))
                last.then_inc(f.z, 1)

            def gcn2_scalar(act, f, it, u):
                k = it * UNROLL + u
                root(act, f, k * ROOTS[1] + 1, s_in[0:BP])
                root(act, f, k * ROOTS[1] + 2, brs[0:BP, 0:1])
                root(act, f, k * ROOTS[1] + 3, brs[0:BP, 0:1])
                act.wait_ge(s_xt, k + 1)
                act.copy(xnT[:], pb[4][:, 0:2 * P].rearrange("p (h n) -> p h n", h=2)[:, :, 0:BP]).then_inc(s_xc, 1)
                act.wait_ge(s_H, k + 1)
                act.wait_ge(f.free, k + 1)
                act.copy(row3[0:BP, 0:2 * D], pb[5][0:BP, :])
                act.copy(row3[0:BP, 2 * D:ROW3], pb[6][0:BP, 0:HEADS])
                act.copy(rowS[0:BP, 0:HEADS], pb[6][0:BP, HEADS:2 * HEADS]).then_inc(f.t, 1)
                act.wait_ge(f.t, k + 1)
                act.wait_ge(s_rs, k + 1)
                act.sem_inc(f.fin, 1)

            def own1(sp, f, node, u):
                sp.dma_start(sout_c[0:BP, u:u + 1],
                             bass.AP(sout_d.tensor, node, [[1, BP], [1, 1]])).then_inc(f.rec[u], 16)

            def own2(sp, f, node, u):
                sp.dma_start(xrow[0:BP, u], x[bass.ds(node, BP), :]).then_inc(f.rec[u], 16)

            def store1(sp, f, node):
                sp.dma_start(table[1][bass.ds(node, BP), :], row12[0:BP]).then_inc(f.st, 16)

            def store2(sp, f, node):
                sp.dma_start(table[2][bass.ds(node, BP), :], row3[0:BP]).then_inc(f.st, 16)
                sp.dma_start(side_d[bass.ds(node, BP), :], rowS[0:BP]).then_inc(f.st, 16)

            with nc.Block() as block:
                @block.sync
                def _(sp):
                    sp_phase(sp, ph[0], own1, store1, 1)
                    sp_phase(sp, ph[1], own2, store2, 2)

                @block.gpsimd
                def _(pool):
                    pool_phase(pool, ph[0])
                    pool_phase(pool, ph[1])

                @block.vector
                def _(dve):
                    n = dve.value_load(niter_i[0:1, 0:1], min_val=UNROLL, max_val=MAXCH // UNROLL)
                    dve.memset(aggT[:], 0.0)
                    dve.memset(deg[:], 0.0)
                    dve.wait_ge(s_w, 16 * 16)
                    cw = Chain(dve, s_wa)
                    for c in range(2):
                        for s in range(2):
                            cw.step(dve.tensor_tensor(prod[:, s], wcat[:, c, 0:2 * D], arow[:, s], ALU.mult))
                            lo = 2 * D + s * HEADS
                            for twin in range(2):
                                dve.tensor_reduce(wcat[:, c, lo + twin:lo + 2 * H1:2],
                                                  prod[:, s, 0:D].rearrange("p (h k) -> p h k", k=C1),
                                                  AX.X, ALU.add)
                            cw.step(dve.tensor_reduce(wcat[:, c, lo + 2 * H1:lo + HEADS],
                                                      prod[:, s, D:2 * D].rearrange("p (h k) -> p h k", k=C2),
                                                      AX.X, ALU.add))
                    dve.wait_ge(s_go[0], 1)
                    for f in ph[0:2]:
                        if f.i == 1:
                            dve.wait_ge(ph[0].hot, n * (2 * UNROLL) + 2)
                            dve.wait_ge(ph[0].hc, n * UNROLL + 1)
                        gcn_hot(dve, Chain(dve, f.dve), f, 0, 0)
                        gcn_counts(dve, f, 0, 0)
                        with dve.Fori(0, n) as it:
                            for u in range(UNROLL):
                                gcn_vector(dve, f, it, u)

                @block.tensor
                def _(pe):
                    n = pe.value_load(niter_i[0:1, 0:1], min_val=UNROLL, max_val=MAXCH // UNROLL)
                    for f in ph[0:2]:
                        pe.sem_inc(f.used, SLOTS)
                        for u in range(UNROLL):
                            gcn_tensor(pe, f, 0, u, first=(u == 0))
                        with pe.Fori(1, n) as it:
                            for u in range(UNROLL):
                                gcn_tensor(pe, f, it, u)
                    gcn_project(pe, n * UNROLL - 1)

                @block.scalar
                def _(act):
                    n = act.value_load(niter_i[0:1, 0:1], min_val=UNROLL, max_val=MAXCH // UNROLL)
                    with act.Fori(0, n) as it:
                        for u in range(UNROLL):
                            root(act, ph[0], it * UNROLL + u + 1, s_in[0:BP])
                    with act.Fori(0, n) as it:
                        for u in range(UNROLL):
                            gcn2_scalar(act, ph[1], it, u)

        phase_c = ExitStack()
        def sc(name, shape, dt=F32):
            return phase_c.enter_context(nc.sbuf_tensor(name, shape, dt))
        with phase_c:
            f = ph[2]
            hotb = sc("hotb", [P, SLOTS, BP, HALF], BF16)
            iota_b = sc("iota_b", [P, BP, HALF], BF16)
            dwb = sc("dwb", [P, TILES], BF16)
            hotT = sc("hotT", [BP, TILES, P], BF16)
            iden_b = sc("iden_b", [P, P], BF16)
            dwa = sc("dwa", [P, TILES + 2])
            same = sc("same", [P, TILES + 1])
            fr = sc("fr", [P, TILES])
            frp = sc("frp", [P, TILES])
            lastf = sc("lastf", [P, TILES])
            endc = sc("endc", [P, TILES])
            notp0 = sc("notp0", [P, 1])
            cc = sc("cc", [P, 2])
            pen = sc("pen", [P, HEADS, TILES])
            ash = sc("ash", [P, HEADS, TILES])
            pre = sc("pre", [P, HEADS, TILES])
            cpk = sc("cpk", [P, 3, HEADS])
            cpT = sc("cpT", [HEADS, 3, P])
            car = sc("car", [HEADS, P])
            cin = sc("cin", [HEADS, P])
            fl = sc("fl", [P, TILES, HEADS + 1])
            tmp = sc("tmp", [P, TILES * (HEADS + 1)])
            mx = sc("mx", [P, HEADS])
            hp = sc("hp", [P, 2])
            lk = sc("lk", [P, 3, HEADS])
            dif = sc("dif", [P, 2, HEADS])
            rr = sc("rr", [P, 2 * HEADS])
            rb = sc("rb", [P, 3, 2 * HEADS], BF16)
            et = sc("et", [P, TILES, HEADS])
            ex = sc("ex", [P, UNROLL, TILES, HEADS])
            ab5 = sc("ab5", [P, UNROLL, 2, HEADS])
            den = sc("den", [P, HEADS])
            dsum = sc("dsum", [P, HEADS])
            rd = sc("rd", [P, HEADS])
            acc = sc("acc", [P, 2 * D])
            xo = sc("xo", [P, 2 * D])
            nabT = sc("nabT", [P, 4])
            pos = sc("pos", [P, 4, BP])
            neg = sc("neg", [P, 4, BP])
            xcT = sc("xcT", [P, 4, BP])
            res = sc("res", [P, D])
            self_h = sc("self_h", [P, UNROLL, ROW3])
            side_c = sc("side_c", [P, UNROLL, SIDE])
            pb4b = pb[4][:, :].bitcast(BF16)
            s_dc = sem("s_dc")
            s_nf = sem("s_nf")
            NUMB = [0, 1, 0, 1, 2]
            s_c3 = sem("s_c3")
            s_hb = sem("s_hb")
            s_ot = sem("s_ot")
            s_oc = sem("s_oc")
            s_cp = sem("s_cp")
            s_tp = sem("s_tp")
            s_tc = sem("s_tc")
            s_ci = sem("s_ci")
            s_tb = sem("s_tb")
            s_fl = sem("s_fl")
            s_mx = sem("s_mx")
            s_r3 = sem("s_r3")
            s_bc = sem("s_bc")
            s_df = sem("s_df")
            s_ab = sem("s_ab")
            s_et = sem("s_et")
            s_ex = sem("s_ex")
            s_ms = sem("s_ms")
            s_xr = sem("s_xr")
            s_xt = sem("s_xt2")
            s_ng = sem("s_ng")
            s_el = sem("s_el")
            s_xc = sem("s_xc2")
            s_u = sem("s_u")

            def wide(ap):
                return ap.rearrange("p (h c) -> p h c", h=HEADS)

            def over(ap, n=HW):
                return ap.unsqueeze(2).to_broadcast([ap.shape[0], HEADS, n])

            def edge_hot(dve, ch, it, u):
                dve.wait_ge(f.rec[u], (it + 1) * 16 * NREC[2])
                dve.tensor_scalar(dwa[:], dwin[:, u], cb[:, u, 1:2], None, ALU.subtract)
                ch.step(dve.tensor_scalar(dwb[:], dwin[:, u, 1:TILES + 1], cb[:, u, 1:2], None, ALU.subtract))
                for g in range(2):
                    q = 2 * u + g
                    dve.wait_ge(f.used, it * (2 * UNROLL) + q + 1)
                    dve.tensor_tensor(hotb[:, q % SLOTS], iota_b[:],
                                      dwb[:, g * HALF:(g + 1) * HALF].unsqueeze(1).to_broadcast([P, BP, HALF]),
                                      ALU.is_equal).then_inc(s_hb, 1)

            def edge_flags(dve, ch):
                ch.step(dve.tensor_tensor(same[:], dwa[:, 0:TILES + 1], dwa[:, 1:TILES + 2], ALU.is_equal))
                ch.step(dve.tensor_scalar(fr[:], dwa[:, 1:TILES + 1], dwa[:, 1:2], None, ALU.is_equal))
                ch.step(dve.tensor_tensor(cc[:, 1:2], same[:, 0:1], notp0[:], ALU.mult))
                ch.step(dve.tensor_tensor(cc[:, 0:1], cc[:, 1:2], fr[:, TILES - 1:TILES], ALU.mult))
                dve.tensor_scalar(cpk[:, 1:3], cc[:].unsqueeze(2).to_broadcast([P, 2, HEADS]), -1.0, BIG,
                                  ALU.add, ALU.mult)
                dve.tensor_scalar(pen[:, :, 1:TILES],
                                  same[:, 1:TILES].unsqueeze(1).to_broadcast([P, HEADS, TILES - 1]), -1.0, BIG,
                                  ALU.add, ALU.mult)
                dve.tensor_scalar(frp[:], fr[:], -1.0, BIG, ALU.add, ALU.mult)
                ch.step(dve.tensor_scalar(lastf[:], same[:, 1:TILES + 1], -1.0, 1.0, ALU.mult, ALU.add))
                ch.step(dve.tensor_tensor(lastf[:], lastf[:], endc[:], ALU.max))

            def run_maxima(dve, ch, it, u):
                for g in range(2):
                    q = 2 * u + g
                    rows_wait(dve, f, it, q)
                    last = dve.tensor_copy(ash[:, :, g * HALF:(g + 1) * HALF],
                                           ring[:, q % SLOTS].rearrange("p (j n) -> p n j", j=HALF)[:, 2 * D:ROW3])
                ch.step(last)
                ch.step(dve.tensor_tensor_scan(pre[:].rearrange("p h j -> p (h j)"),
                                               pen[:].rearrange("p h j -> p (h j)"),
                                               ash[:].rearrange("p h j -> p (h j)"), -BIG, ALU.add, ALU.max))
                dve.tensor_copy(cpk[:, 0], pre[:, :, TILES - 1]).then_inc(s_cp, 1)

            def carry(dve, ch, k):
                dve.wait_ge(s_tc, k + 1)
                ch.step(dve.tensor_tensor_scan(car[:], cpT[:, 1], cpT[:, 0], -BIG, ALU.add, ALU.max))
                dve.tensor_tensor(cin[:, 1:P], car[:, 0:P - 1], cpT[:, 2, 1:P], ALU.add).then_inc(s_ci, 1)

            def whole_runs(dve, ch, k):
                dve.wait_ge(s_tb, k + 1)
                t = tmp[:, 0:HEADS * TILES].rearrange("p (h j) -> p h j", h=HEADS)
                ch.step(dve.tensor_tensor(t, frp[:].unsqueeze(1).to_broadcast([P, HEADS, TILES]),
                                          over(pb[5][:, 384:384 + HEADS], TILES), ALU.add))
                ch.step(dve.tensor_tensor(pre[:], pre[:], t, ALU.max))
                dve.tensor_copy(fl[:, :, HEADS], lastf[:])
                dve.tensor_tensor(fl[:, :, 0:HEADS].rearrange("p j h -> p h j"), pre[:],
                                  lastf[:].unsqueeze(1).to_broadcast([P, HEADS, TILES]), ALU.mult).then_inc(s_fl, 1)

            def leaky(dve, to, v):
                return dve.scalar_tensor_tensor(to, v, 0.2, v, ALU.mult, ALU.max)

            def node_maxima(dve, ch, k, u):
                b = slice(0, BP)
                as_self, ad = self_h[b, u, 2 * D:ROW3], side_c[b, u, 0:HEADS]
                m, greatest = lk[b, 1], rr[b, HEADS:2 * HEADS]
                dve.tensor_scalar(hp[b, 1:2], cb[b, u, 0:1], -1.0, BIG, ALU.add, ALU.mult)
                dve.tensor_copy(rr[b, 0:HEADS], ad)
                dve.tensor_tensor(lk[b, 0], mx[b], ad, ALU.add)
                ch.step(dve.tensor_tensor(lk[b, 2], as_self, ad, ALU.add))
                ch.step(leaky(dve, lk[b, 0::2], lk[b, 0::2]))
                dve.wait_ge(s_mx, k + 1)
                ch.step(dve.tensor_scalar(hp[b, 0:1], pb[5][b, 400 + HEADS:401 + HEADS], -1.0, BIG,
                                          ALU.add, ALU.mult))
                ch.step(dve.scalar_tensor_tensor(m, pb[5][b, 400:400 + HEADS], hp[b, 0:1], as_self,
                                                 ALU.add, ALU.max))
                ch.step(dve.scalar_tensor_tensor(mx[b], mx[b], hp[b, 1:2], m, ALU.add, ALU.max))
                ch.step(dve.tensor_tensor(m, mx[b], ad, ALU.add))
                ch.step(leaky(dve, greatest, m))
                t = tmp[b, 0:2 * HEADS]
                ch.step(dve.tensor_copy(rb[b, 0], rr[b]))
                ch.step(dve.tensor_tensor(t, rr[b], rb[b, 0], ALU.subtract))
                ch.step(dve.tensor_copy(rb[b, 1], t))
                dve.tensor_tensor(rb[b, 2], t, rb[b, 1], ALU.subtract).then_inc(s_r3, 1)
                ch.step(dve.tensor_tensor(dif[b], lk[b, 0::2], greatest.unsqueeze(1).to_broadcast([BP, 2, HEADS]),
                                          ALU.subtract))
                dve.tensor_scalar(dif[b], dif[b], 0.0, None, ALU.min).then_inc(s_df, 1)

            def edge_weights(dve, ch, k):
                dve.wait_ge(s_bc, k + 1)
                for g in range(2):
                    js = slice(g * HALF, (g + 1) * HALF)
                    b6 = pb[BCB[g]][:, 0:HALF * 2 * HEADS].rearrange("p (j n) -> p j n", j=HALF)
                    last = dve.tensor_tensor(et[:, js], ash[:, :, js].rearrange("p h j -> p j h"),
                                             b6[:, :, 0:HEADS], ALU.add)
                ch.step(last)
                flat = et[:].rearrange("p j h -> p (j h)")
                ch.step(leaky(dve, flat, flat))
                for g in range(2):
                    js = slice(g * HALF, (g + 1) * HALF)
                    b6 = pb[BCB[g]][:, 0:HALF * 2 * HEADS].rearrange("p (j n) -> p j n", j=HALF)
                    last = dve.tensor_tensor(et[:, js], et[:, js], b6[:, :, HEADS:2 * HEADS], ALU.subtract)
                ch.step(last)
                dve.tensor_scalar(et[:], et[:], 0.0, None, ALU.min).then_inc(s_et, 1)

            def weigh(dve, k, u, g):
                dve.wait_ge(s_ex, k + 1)
                rows = ring[:, (2 * u + g) % SLOTS].rearrange("p (j n) -> p j n", j=HALF)
                for a, z in ((0, 3), (3, HALF)) if g == 0 else ((0, HALF),):
                    v = rows[:, a:z, 0:2 * D].rearrange("p j (h c) -> p j h c", h=HEADS)
                    w = ex[:, u, g * HALF + a:g * HALF + z].unsqueeze(3).to_broadcast([P, z - a, HEADS, HW])
                    dve.tensor_tensor(v, v, w, ALU.mult).then_inc(s_ms, 1)

            def read_den(dve, k):
                b = slice(0, BP)
                dve.wait_ge(f.used, k * 2 + 2 + SLOTS)
                dve.tensor_copy(dsum[b], pb[3][b, 0:HEADS]).then_inc(s_dc, 1)
                dve.wait_ge(s_dc, k + 2)

            def node_sums(dve, ch, k, u):
                b = slice(0, BP)
                al, be = ab5[b, u, 0], ab5[b, u, 1]
                dve.wait_ge(s_ab, k + 1)
                ch.step(dve.tensor_scalar(al, al, cb[b, u, 0:1], None, ALU.mult))
                dve.tensor_tensor(wide(xo[b]), wide(self_h[b, u, 0:2 * D]), over(be), ALU.mult)
                dve.tensor_tensor(den[b], den[b], al, ALU.mult)
                ch.step(dve.tensor_tensor(wide(acc[b]), wide(acc[b]), over(al), ALU.mult))
                dve.tensor_tensor(den[b], den[b], dsum[b], ALU.add)
                ch.step(dve.tensor_tensor(acc[b], acc[b], pb[NUMB[u]][b, :], ALU.add))
                dve.sem_inc(s_nf, 1)

            def node_rows(dve, ch, k, u):
                b = slice(0, BP)
                dve.tensor_tensor(xo[b], xo[b], acc[b], ALU.add)
                ch.step(dve.scalar_tensor_tensor(rd[b], den[b], 1e-16, ab5[b, u, 1], ALU.add, ALU.add))
                ch.step(dve.reciprocal(rd[b], rd[b]))
                dve.tensor_tensor(wide(xo[b]), wide(xo[b]), over(rd[b]), ALU.mult).then_inc(s_xr, 1)

            def elu(dve, k):
                dve.wait_ge(s_el, k + 1)
                dve.scalar_tensor_tensor(xcT[:], neg[:], -1.0, pos[:], ALU.add, ALU.add).then_inc(s_xc, 1)

            def result(dve, k, u):
                b = slice(0, BP)
                dve.wait_ge(s_u, k + 3)
                dve.wait_ge(f.free, k + 3)
                dve.tensor_tensor(res[b], pb[7][b, 0:D], side_c[b, u, HEADS:SIDE], ALU.add).then_inc(f.fin, 1)

            def at(it, u, d):
                return it + (u + d) // UNROLL, (u + d) % UNROLL

            def gat_vector(dve, ch, it, u, first=0, last=0):
                k = it * UNROLL + u
                weigh(dve, k, u, 0)
                if first < 1:
                    result(dve, k - 2, (u - 2) % UNROLL)
                if last < 2:
                    run_maxima(dve, ch, *at(it, u, 1))
                if first < 2:
                    read_den(dve, k - 1)
                weigh(dve, k, u, 1)
                if last < 2:
                    carry(dve, ch, k + 1)
                if first < 2:
                    node_sums(dve, ch, k - 1, (u - 1) % UNROLL)
                if last < 2:
                    whole_runs(dve, ch, k + 1)
                if first < 2:
                    node_rows(dve, ch, k - 1, (u - 1) % UNROLL)
                if last == 0:
                    edge_hot(dve, ch, *at(it, u, 2))
                    edge_flags(dve, ch)
                if last < 2:
                    node_maxima(dve, ch, k + 1, (u + 1) % UNROLL)
                if first < 2:
                    elu(dve, k - 1)
                if last < 2:
                    edge_weights(dve, ch, k + 1)

            BCB = [6, 4]

            def turn_hot(pe, it, u, m):
                k = it * UNROLL + u
                for j in range(6 * m, 6 * m + 6):
                    g = j // HALF
                    if j == 0 or j == HALF or j == 6 * m:
                        pe.wait_ge(s_hb, it * 2 * UNROLL + 2 * u + g + 1)
                    if j == 0:
                        pe.wait_ge(s_et, k + 1)
                    if j == 6 * m:
                        pe.wait_ge(s_oc, 3 * k + m + 1)
                    last = pe.transpose(pb4b[0:BP, (j % 6) * P:(j % 6 + 1) * P],
                                        hotb[:, (2 * u + g) % SLOTS, :, j % HALF], iden_b[:])
                last.then_inc(s_ot, 1)

            def turn_last(pe, k):
                pe.wait_ge(s_cp, k + 1)
                for i in range(3):
                    last = pe.transpose(pb[5][0:HEADS, i * P:(i + 1) * P], cpk[:, i], ident[:])
                last.then_inc(s_tp, 1)

            def turn_back(pe, k):
                pe.wait_ge(s_ci, k + 1)
                pe.sem_inc(s_gate, 1)
                pe.transpose(pb[5][:, 384:384 + HEADS], cin[:], ident[0:HEADS, 0:HEADS]).then_inc(s_tb, 1)

            def to_nodes(pe, it, u, js=range(TILES)):
                k = it * UNROLL + u
                if js[0] == 0:
                    pe.wait_ge(f.hot, it * 2 * UNROLL + 2 * u + 2)
                    pe.wait_ge(s_fl, k + 1)
                for j in js:
                    last = pe.matmul(pb[5][0:BP, 400:401 + HEADS], hot[:, (2 * u + j // HALF) % SLOTS, j % HALF],
                                     fl[:, j], start=(j == 0), stop=(j == TILES - 1))
                if js[-1] == TILES - 1:
                    last.then_inc(s_mx, 1)

            def to_edges(pe, k):
                pe.wait_ge(s_r3, k + 1)
                pe.wait_ge(s_oc, 3 * k + 4)
                for j in range(TILES):
                    bank, c = BCB[j // HALF], (j % HALF) * 2 * HEADS
                    for i in range(3):
                        last = pe.matmul(pb[bank][:, c:c + 2 * HEADS], hotT[:, j], rb[0:BP, i],
                                         start=(i == 0), stop=(i == 2))
                last.then_inc(s_bc, 1)

            def sums(pe, u, g, js):
                q = (2 * u + g) % SLOTS
                for j in js:
                    a, z = (g == 0 and j == 0), (g == 1 and j == HALF - 1)
                    pe.matmul(pb[NUMB[u]][0:BP, :], hot[:, q, j], ring[:, q, j * ROW3:j * ROW3 + 2 * D],
                              start=a, stop=z)

            def denominators(pe, k, u, g):
                if g == 0:
                    pe.wait_ge(s_dc, k + 1)
                for j in range(HALF):
                    last = pe.matmul(pb[3][0:BP, 0:HEADS], hot[:, (2 * u + g) % SLOTS, j], ex[:, u, g * HALF + j],
                                     start=(g == 0 and j == 0), stop=(g == 1 and j == HALF - 1))
                last.then_inc(f.used, 1)

            def out_turn(pe, k):
                pe.wait_ge(s_xr, k + 1)
                for c in range(4):
                    last = pe.transpose(pb[7][:, c * BP:(c + 1) * BP], xo[0:BP, c * P:(c + 1) * P],
                                        ident[0:BP, 0:BP])
                last.then_inc(s_xt, 1)

            def out_project(pe, k):
                pe.wait_ge(s_xc, k + 1)
                for c in range(4):
                    last = pe.matmul(pb[7][0:BP, 0:D], xcT[:, c], wu_s[:, c], start=(c == 0), stop=(c == 3))
                last.then_inc(s_u, 1)

            def gat_tensor(pe, it, u, first=0, last=0):
                k = it * UNROLL + u
                nxt = at(it, u, 1)
                if first < 2:
                    pe.wait_ge(s_nf, k)
                pe.wait_ge(s_ms, 3 * k + 1)
                sums(pe, u, 0, range(0, 3))
                pe.wait_ge(s_ms, 3 * k + 2)
                if last < 2:
                    turn_last(pe, k + 1)
                sums(pe, u, 0, range(3, 8))
                if last < 2:
                    turn_back(pe, k + 1)
                sums(pe, u, 0, range(8, 9))
                denominators(pe, k, u, 0)
                pe.wait_ge(s_ms, 3 * k + 3)
                sums(pe, u, 1, range(0, 1))
                for i in range(3):
                    sums(pe, u, 1, range(i + 1, i + 2))
                    if last < 2:
                        to_nodes(pe, *nxt, range(i * (TILES // 3), (i + 1) * (TILES // 3)))
                if first < 2:
                    out_turn(pe, k - 1)
                sums(pe, u, 1, range(4, 6))
                if last < 2:
                    to_edges(pe, k + 1)
                sums(pe, u, 1, range(6, 7))
                if first < 2:
                    out_project(pe, k - 1)
                sums(pe, u, 1, range(7, 8))
                if last == 0:
                    turn_hot(pe, *at(it, u, 2), 0)
                sums(pe, u, 1, range(8, 9))
                if last == 0:
                    turn_hot(pe, *at(it, u, 2), 1)
                denominators(pe, k, u, 1)
                if last == 0:
                    turn_hot(pe, *at(it, u, 2), 2)

            def hot_out(act, k, m):
                act.wait_ge(s_ot, 3 * k + m + 1)
                act.copy(hotT[:, 6 * m:6 * m + 6], pb4b[0:BP, 0:6 * P].rearrange("p (j n) -> p j n", j=6)
                         ).then_inc(s_oc, 1)

            def hot_f32(act, it, u):
                for g in range(2):
                    q = 2 * u + g
                    act.wait_ge(s_hb, it * 2 * UNROLL + q + 1)
                    act.copy(hot[:, q % SLOTS], hotb[:, q % SLOTS].rearrange("p v j -> p j v")).then_inc(f.hot, 1)

            def last_out(act, k):
                act.wait_ge(s_tp, k + 1)
                act.copy(cpT[:].rearrange("p i n -> p (i n)"), pb[5][0:HEADS, 0:3 * P]).then_inc(s_tc, 1)

            def state_exp(act, k, u):
                act.wait_ge(s_df, k + 1)
                act.activation(ab5[0:BP, u], dif[0:BP], ACT.Exp).then_inc(s_ab, 1)

            def edge_exp(act, k, u):
                act.wait_ge(s_et, k + 2)
                act.activation(ex[:, u], et[:], ACT.Exp).then_inc(s_ex, 1)

            def out_parts(act, k):
                act.wait_ge(s_xt, k + 1)
                for c in range(4):
                    x_c = pb[7][:, c * BP:(c + 1) * BP]
                    last = act.activation(neg[:, c], x_c, ACT.Relu, bias=nabT[:, c:c + 1], scale=-1.0)
                last.then_inc(s_ng, 1)
                for c in range(4):
                    act.activation(pos[:, c], pb[7][:, c * BP:(c + 1) * BP], ACT.Relu, bias=abT[:, c:c + 1])
                act.wait_ge(s_ng, k + 1)
                act.activation(neg[:], neg[:], ACT.Exp, scale=-1.0).then_inc(s_el, 1)

            def gat_scalar(act, it, u, first=0, last=0):
                k = it * UNROLL + u
                nxt = at(it, u, 1)
                if last < 2:
                    last_out(act, k + 1)
                if first < 2:
                    out_parts(act, k - 1)
                if last < 2:
                    state_exp(act, k + 1, nxt[1])
                    edge_exp(act, k + 1, nxt[1])
                if last == 0:
                    for m in range(3):
                        hot_out(act, k + 2, m)
                    hot_f32(act, *at(it, u, 2))

            def steps(eng, n, body):
                for u in range(UNROLL):
                    body(0, u, first=max(0, 2 - u))
                with eng.Fori(1, n) as it:
                    for u in range(UNROLL):
                        body(it, u)
                for u in range(UNROLL):
                    body(n, u, last=max(0, u - (UNROLL - 3)))

            def own3(sp, f, node, u):
                sp.dma_start(self_h[0:BP, u], table[2][bass.ds(node, BP), :]).then_inc(f.rec[u], 16)
                sp.dma_start(side_c[0:BP, u], side_d[bass.ds(node, BP), :]).then_inc(f.rec[u], 16)

            def store3(sp, f, node):
                sp.dma_start(out[bass.ds(node, BP), :], res[0:BP]).then_inc(f.st, 16)

            FIRST, LOOP = 184, 155

            with nc.Block() as block:
                @block.sync
                def _(sp):
                    sp_phase(sp, f, own3, store3, 1)

                @block.gpsimd
                def _(pool):
                    pool.memset(endc[:], 0.0)
                    pool.memset(notp0[:], 1.0)
                    pool.iota(iota_b[:], [[1, BP], [0, HALF]], base=0, channel_multiplier=0,
                              allow_small_or_imprecise_dtypes=True)
                    pool.tensor_scalar(nabT[:], abT[:], -1.0, None, ALU.mult)
                    pool.memset(pen[:, :, 0:1], -BIG)
                    pool.memset(cin[:, 0:1], -BIG)
                    pool.tensor_copy(iden_b[:], ident[:]).then_inc(s_c3, 1)
                    pool.wait_ge(s_c3, 1)
                    pool.affine_select(endc[:], endc[:], pattern=[[1, TILES]], compare_op=ALU.not_equal,
                                       fill=1.0, base=1 - CAP, channel_multiplier=TILES)
                    pool.affine_select(notp0[:], notp0[:], pattern=[[0, 1]], compare_op=ALU.not_equal,
                                       fill=0.0, base=0, channel_multiplier=1).then_inc(s_c3, 1)
                    pool_phase(pool, f)

                @block.vector
                def _(dve):
                    n = dve.value_load(niter_i[0:1, 1:2], min_val=UNROLL - 1, max_val=MAXCH // UNROLL - 1)
                    ch = Chain(dve, f.dve)
                    dve.memset(acc[:], 0.0)
                    dve.memset(den[:], 0.0)
                    ch.step(dve.memset(mx[:], 0.0))
                    dve.sem_inc(s_et, 1)
                    dve.sem_inc(s_nf, 1)
                    dve.sem_inc(s_dc, 1)
                    dve.wait_ge(s_c3, 2)
                    edge_hot(dve, ch, 0, 0)
                    edge_flags(dve, ch)
                    run_maxima(dve, ch, 0, 0)
                    carry(dve, ch, 0)
                    whole_runs(dve, ch, 0)
                    node_maxima(dve, ch, 0, 0)
                    edge_hot(dve, ch, 0, 1)
                    edge_flags(dve, ch)
                    edge_weights(dve, ch, 0)

                    def body(it, u, first=0, last=0):
                        if u == 0 and not first:
                            ch.base, ch.n = FIRST + (it - 1) * LOOP, 0
                        gat_vector(dve, ch, it, u, first, last)
                        if u == UNROLL - 1 and not last:
                            want = FIRST if isinstance(it, int) else LOOP
                            assert ch.n == want, (ch.n, want)

                    steps(dve, n, body)
                    k = n * UNROLL + UNROLL - 1
                    result(dve, k - 1, UNROLL - 2)
                    read_den(dve, k)
                    node_sums(dve, ch, k, UNROLL - 1)
                    node_rows(dve, ch, k, UNROLL - 1)
                    elu(dve, k)
                    result(dve, k, UNROLL - 1)

                @block.tensor
                def _(pe):
                    n = pe.value_load(niter_i[0:1, 1:2], min_val=UNROLL - 1, max_val=MAXCH // UNROLL - 1)
                    pe.wait_ge(s_c3, 2)
                    pe.sem_inc(f.used, SLOTS)
                    pe.sem_inc(s_u, 2)
                    for m in range(3):
                        turn_hot(pe, 0, 0, m)
                    turn_last(pe, 0)
                    turn_back(pe, 0)
                    to_nodes(pe, 0, 0)
                    to_edges(pe, 0)
                    for m in range(3):
                        turn_hot(pe, 0, 1, m)
                    steps(pe, n, lambda it, u, first=0, last=0: gat_tensor(pe, it, u, first, last))
                    out_turn(pe, n * UNROLL + UNROLL - 1)
                    out_project(pe, n * UNROLL + UNROLL - 1)

                @block.scalar
                def _(act):
                    n = act.value_load(niter_i[0:1, 1:2], min_val=UNROLL - 1, max_val=MAXCH // UNROLL - 1)
                    act.sem_inc(s_oc, 1)
                    for m in range(3):
                        hot_out(act, 0, m)
                    hot_f32(act, 0, 0)
                    last_out(act, 0)
                    state_exp(act, 0, 0)
                    edge_exp(act, 0, 0)
                    for m in range(3):
                        hot_out(act, 1, m)
                    hot_f32(act, 0, 1)
                    steps(act, n, lambda it, u, first=0, last=0: gat_scalar(act, it, u, first, last))
                    out_parts(act, n * UNROLL + UNROLL - 1)


_INS = ['x', 'src', 'dst', 'L0_gnn_W1', 'L0_gnn_b1', 'L0_gnn_W2', 'L0_gnn_b2', 'L1_gnn_gamma', 'L1_gnn_beta',
        'L1_gnn_W1', 'L1_gnn_a_src1', 'L1_gnn_a_dst1', 'L1_gnn_b1', 'L1_gnn_W2', 'L1_gnn_a_src2',
        'L1_gnn_a_dst2', 'L1_gnn_b2', 'L1_gnn_Wu', 'L1_gnn_bu']


def kernel(**inputs):
    import numpy as _np
    import concourse.bacc as _bacc
    from concourse import mybir as _mybir
    from concourse.bass_utils import run_bass_kernel_spmd as _run

    nc = _bacc.Bacc("TRN2", target_bir_lowering=False, num_devices=1)
    arrays, args = {}, []
    for name in _INS:
        a = _np.ascontiguousarray(inputs[name])
        arrays[f"in_{name}_dram"] = a
        args.append(nc.dram_tensor(f"in_{name}_dram", a.shape, _mybir.dt.from_np(a.dtype), kind="ExternalInput").ap())
    args.append(nc.dram_tensor("out_0_dram", (3125, 256), _mybir.dt.float32, kind="ExternalOutput").ap())
    gnn(nc, *args)
    r = _run(nc, [arrays], core_ids=[0])
    return r.results[0]["out_0_dram"]
```
